# Optimizing a Trainium2 kernel written in Bass

```python
import numpy as np
import jax
import jax.numpy as jnp

def _softmax(x, axis=-1):
    return jax.nn.softmax(x, axis=axis)

def _gelu(x):
    return jax.nn.gelu(x, approximate=True)

def _silu(x):
    return jax.nn.silu(x)

def _sigmoid(x):
    return jax.nn.sigmoid(x)

def _layernorm(x, axis=-1, eps=1e-05):
    m = jnp.mean(x, axis=axis, keepdims=True)
    v = jnp.var(x, axis=axis, keepdims=True)
    return (x - m) / jnp.sqrt(v + eps)

def _scatter_add(tgt, idx, src, axis=0):
    return tgt.at[idx].add(src)

def _segment_sum(src, seg, n):
    return jax.ops.segment_sum(src, seg, n)
kernel_name = 'mk_metaformer_d2_conv_nhwc768_r4_6e9143'

def setup_inputs(seed: int=0):
    np.random.seed(seed)
    _w = jnp.asarray

    def _rec_inputs():
        import jax
        import jax.numpy as jnp
        _gk = jax.random.key(seed)
        x = -0.0002221 + 1 * jax.random.normal(jax.random.fold_in(_gk, 1), (8, 16, 16, 192), jnp.float32)
        return x
    x = _rec_inputs()

    def _L0_conv_setup():
        import jax, jax.numpy as jnp
        import numpy as np
        EMBED_DIM = 192
        NUM_HEADS = 12
        HEAD_DIM = EMBED_DIM // NUM_HEADS
        KERNEL = 7

        def _neighbor_index(size, kernel):
            start = np.clip(np.arange(size) - kernel // 2, 0, size - kernel)
            return jnp.asarray(start[:, None] + np.arange(kernel)[None, :])
        key = jax.random.key(seed)
        k1, k2, k3, k4, k5 = jax.random.split(key, 5)
        B, H, W, C = (8, 16, 16, EMBED_DIM)
        x = jax.random.normal(k1, (B, H, W, C), dtype=jnp.float32)
        w_qkv = jax.random.normal(k2, (3 * C, C), dtype=jnp.float32) * C ** (-0.5)
        b_qkv = jax.random.normal(k3, (3 * C,), dtype=jnp.float32) * 0.02
        w_proj = jax.random.normal(k4, (C, C), dtype=jnp.float32) * C ** (-0.5)
        b_proj = jax.random.normal(k5, (C,), dtype=jnp.float32) * 0.02
        return {'x': x, 'w_qkv': w_qkv, 'b_qkv': b_qkv, 'w_proj': w_proj, 'b_proj': b_proj}
    _L0_conv_all = _L0_conv_setup()
    _L0_conv_in = {k: v for k, v in _L0_conv_all.items() if k in ('w_qkv', 'b_qkv', 'w_proj', 'b_proj')}
    del _L0_conv_all

    def _L0_ffn_setup():
        import jax, jax.numpy as jnp
        import numpy as np
        E = 32
        I = 464
        IS = 928
        K = 6
        G = 1
        TG = 1
        SCALE = 2.5
        CAP = 48

        def moe_forward(hidden_states, Wg, e_bias, W_gate_up, W_down, Wsg, Wsu, Wsd):
            B, S, H = hidden_states.shape
            x = hidden_states.reshape(-1, H)
            T = x.shape[0]
            logits = x.astype(jnp.float32) @ Wg.T
            sig = jax.nn.sigmoid(logits)
            choice = sig + e_bias[None, :]
            grp = choice.reshape(T, G, E // G)
            group_scores = jax.lax.top_k(grp, 2)[0].sum(-1)
            gidx = jax.lax.top_k(group_scores, TG)[1]
            gmask = jnp.zeros((T, G), jnp.float32).at[jnp.arange(T)[:, None], gidx].set(1.0)
            smask = jnp.repeat(gmask, E // G, axis=1)
            scores_for_choice = jnp.where(smask > 0, choice, 0.0)
            topk_idx = jax.lax.top_k(scores_for_choice, K)[1]
            topk_w = jnp.take_along_axis(sig, topk_idx, axis=1)
            topk_w = topk_w / (topk_w.sum(-1, keepdims=True) + 1e-20)
            topk_w = topk_w * SCALE
            P = T * K
            flat_e = topk_idx.reshape(-1)
            order = jnp.argsort(flat_e)
            se = flat_e[order]
            counts = jax.ops.segment_sum(jnp.ones(P, jnp.int32), flat_e, num_segments=E)
            starts = jnp.cumsum(counts) - counts
            pos = jnp.arange(P) - starts[se]
            buf_idx = jnp.where(pos < CAP, se * CAP + pos, E * CAP)
            tok_of_pair = (order // K).astype(jnp.int32)
            w_of_pair = topk_w.reshape(-1)[order]
            token_buf = jnp.zeros((E * CAP,), jnp.int32).at[buf_idx].set(tok_of_pair, mode='drop')
            w_buf = jnp.zeros((E * CAP,), x.dtype).at[buf_idx].set(w_of_pair.astype(x.dtype), mode='drop')
            xb = x[token_buf].reshape(E, CAP, H)
            gu = jnp.einsum('ech,ehf->ecf', xb, W_gate_up)
            g, u = jnp.split(gu, 2, axis=-1)
            inter = jax.nn.silu(g) * u
            yb = jnp.einsum('eci,eih->ech', inter, W_down)
            yb = yb * w_buf.reshape(E, CAP, 1)
            routed = jnp.zeros((T, H), x.dtype).at[token_buf].add(yb.reshape(E * CAP, H))
            shared = jax.nn.silu(x @ Wsg) * (x @ Wsu) @ Wsd
            return (routed + shared).reshape(B, S, H)
        key = jax.random.key(seed)
        ks = jax.random.split(key, 8)
        B, S, H = (1, 512, 192)
        sc = 0.02
        return {'hidden_states': jax.random.normal(ks[0], (B, S, H), jnp.float32), 'Wg': jax.random.normal(ks[1], (E, H), jnp.float32) * sc, 'e_bias': jnp.zeros((E,), jnp.float32), 'W_gate_up': jax.random.normal(ks[2], (E, H, 2 * I), jnp.float32) * sc, 'W_down': jax.random.normal(ks[3], (E, I, H), jnp.float32) * sc, 'Wsg': jax.random.normal(ks[4], (H, IS), jnp.float32) * sc, 'Wsu': jax.random.normal(ks[5], (H, IS), jnp.float32) * sc, 'Wsd': jax.random.normal(ks[6], (IS, H), jnp.float32) * sc}
    _L0_ffn_all = _L0_ffn_setup()
    _L0_ffn_in = {k: v for k, v in _L0_ffn_all.items() if k in ('Wg', 'e_bias', 'W_gate_up', 'W_down', 'Wsg', 'Wsu', 'Wsd')}
    del _L0_ffn_all

    def _L1_conv_setup():
        import jax, jax.numpy as jnp
        import numpy as np
        DIM = 192
        NUM_HEADS = 12
        HEAD_DIM = DIM // NUM_HEADS

        def _split_heads(t, b, h, w):
            return t.reshape(b, h, w, NUM_HEADS, HEAD_DIM).transpose(0, 3, 1, 2, 4)
        key = jax.random.key(seed)
        ks = jax.random.split(key, 9)
        s = 1.0 / np.sqrt(DIM)
        x = jax.random.normal(ks[0], (16, 16, 16, DIM), dtype=jnp.float32)
        Wq = jax.random.uniform(ks[1], (DIM, DIM), jnp.float32, -s, s)
        bq = jax.random.uniform(ks[2], (DIM,), jnp.float32, -s, s)
        Wk = jax.random.uniform(ks[3], (DIM, DIM), jnp.float32, -s, s)
        bk = jax.random.uniform(ks[4], (DIM,), jnp.float32, -s, s)
        Wv = jax.random.uniform(ks[5], (DIM, DIM), jnp.float32, -s, s)
        bv = jax.random.uniform(ks[6], (DIM,), jnp.float32, -s, s)
        Wo = jax.random.uniform(ks[7], (DIM, DIM), jnp.float32, -s, s)
        bo = jax.random.uniform(ks[8], (DIM,), jnp.float32, -s, s)
        return {'x': x, 'Wq': Wq, 'bq': bq, 'Wk': Wk, 'bk': bk, 'Wv': Wv, 'bv': bv, 'Wo': Wo, 'bo': bo}
    _L1_conv_all = _L1_conv_setup()
    _L1_conv_in = {k: v for k, v in _L1_conv_all.items() if k in ('Wq', 'bq', 'Wk', 'bk', 'Wv', 'bv', 'Wo', 'bo')}
    del _L1_conv_all

    def _L1_ffn_setup():
        import jax, jax.numpy as jnp
        import numpy as np
        HID = 192
        NQ = 12
        NKV = 3
        HD = 16
        REP = NQ // NKV
        E = 16
        TOPK = 2
        FF = 384
        EPS = 1e-06
        THETA = 10000.0

        def rms_norm(x, w):
            return x / jnp.sqrt(jnp.mean(x * x, axis=-1, keepdims=True) + EPS) * w

        def rope_tables(seq_len):
            inv = 1.0 / THETA ** (jnp.arange(0, HD, 2, dtype=jnp.float32) / HD)
            f = jnp.arange(seq_len, dtype=jnp.float32)[:, None] * inv[None, :]
            return (jnp.cos(f), jnp.sin(f))

        def apply_rope(t, cos, sin):
            B, S, H, _ = t.shape
            tr = t.reshape(B, S, H, HD // 2, 2)
            c = cos[None, :, None, :]
            s = sin[None, :, None, :]
            r0 = tr[..., 0] * c - tr[..., 1] * s
            r1 = tr[..., 0] * s + tr[..., 1] * c
            return jnp.stack([r0, r1], axis=-1).reshape(B, S, H, HD)

        def attention(x, w_qkv, w_out):
            B, S, _ = x.shape
            qkv = x @ w_qkv
            q, k, v = jnp.split(qkv, [NQ * HD, (NQ + NKV) * HD], axis=-1)
            q = q.reshape(B, S, NQ, HD)
            k = k.reshape(B, S, NKV, HD)
            v = v.reshape(B, S, NKV, HD)
            cos, sin = rope_tables(S)
            q = apply_rope(q, cos, sin)
            k = apply_rope(k, cos, sin)
            k = jnp.repeat(k, REP, axis=2)
            v = jnp.repeat(v, REP, axis=2)
            q = q.transpose(0, 2, 1, 3)
            k = k.transpose(0, 2, 1, 3)
            v = v.transpose(0, 2, 1, 3)
            scores = jnp.einsum('bhqd,bhkd->bhqk', q, k) / jnp.sqrt(jnp.float32(HD))
            causal = jnp.tril(jnp.ones((S, S), dtype=bool))
            scores = jnp.where(causal[None, None], scores, jnp.finfo(scores.dtype).min)
            attn = jax.nn.softmax(scores, axis=-1)
            out = jnp.einsum('bhqk,bhkd->bhqd', attn, v)
            out = out.transpose(0, 2, 1, 3).reshape(B, S, NQ * HD)
            return out @ w_out

        def moe_ffn(x2d, w_router, w_gate_up, w_down):
            logits = x2d @ w_router
            probs = jax.nn.softmax(logits, axis=-1)
            vals, idx = jax.lax.top_k(probs, TOPK)
            vals = vals / jnp.sum(vals, axis=-1, keepdims=True)
            combine = jnp.sum(jax.nn.one_hot(idx, E, dtype=x2d.dtype) * vals[..., None], axis=1)
            out = jnp.zeros_like(x2d)
            for e in range(E):
                gu = x2d @ w_gate_up[e]
                gate, up = jnp.split(gu, 2, axis=-1)
                h = jax.nn.silu(gate) * up
                out = out + combine[:, e:e + 1] * (h @ w_down[e])
            return out
        key = jax.random.key(seed)
        ks = jax.random.split(key, 6)
        B, S = (1, 512)
        return {'x': jax.random.normal(ks[0], (B, S, HID), dtype=jnp.float32), 'norm1_w': jnp.ones((HID,), dtype=jnp.float32), 'w_qkv': jax.random.normal(ks[1], (HID, (NQ + 2 * NKV) * HD), dtype=jnp.float32) * 0.02, 'w_out': jax.random.normal(ks[2], (NQ * HD, HID), dtype=jnp.float32) * 0.02, 'norm2_w': jnp.ones((HID,), dtype=jnp.float32), 'w_router': jax.random.normal(ks[3], (HID, E), dtype=jnp.float32) * 0.02, 'w_gate_up': jax.random.normal(ks[4], (E, HID, 2 * FF), dtype=jnp.float32) * 0.02, 'w_down': jax.random.normal(ks[5], (E, FF, HID), dtype=jnp.float32) * 0.02}
    _L1_ffn_all = _L1_ffn_setup()
    _L1_ffn_in = {k: v for k, v in _L1_ffn_all.items() if k in ('norm1_w', 'w_qkv', 'w_out', 'norm2_w', 'w_router', 'w_gate_up', 'w_down')}
    del _L1_ffn_all
    return {'x': x, 'L0_conv_w_qkv': _L0_conv_in['w_qkv'], 'L0_conv_b_qkv': _L0_conv_in['b_qkv'], 'L0_conv_w_proj': _L0_conv_in['w_proj'], 'L0_conv_b_proj': _L0_conv_in['b_proj'], 'L0_ffn_Wg': _L0_ffn_in['Wg'], 'L0_ffn_e_bias': _L0_ffn_in['e_bias'], 'L0_ffn_W_gate_up': _L0_ffn_in['W_gate_up'], 'L0_ffn_W_down': _L0_ffn_in['W_down'], 'L0_ffn_Wsg': _L0_ffn_in['Wsg'], 'L0_ffn_Wsu': _L0_ffn_in['Wsu'], 'L0_ffn_Wsd': _L0_ffn_in['Wsd'], 'L1_conv_Wq': _L1_conv_in['Wq'], 'L1_conv_bq': _L1_conv_in['bq'], 'L1_conv_Wk': _L1_conv_in['Wk'], 'L1_conv_bk': _L1_conv_in['bk'], 'L1_conv_Wv': _L1_conv_in['Wv'], 'L1_conv_bv': _L1_conv_in['bv'], 'L1_conv_Wo': _L1_conv_in['Wo'], 'L1_conv_bo': _L1_conv_in['bo'], 'L1_ffn_norm1_w': _L1_ffn_in['norm1_w'], 'L1_ffn_w_qkv': _L1_ffn_in['w_qkv'], 'L1_ffn_w_out': _L1_ffn_in['w_out'], 'L1_ffn_norm2_w': _L1_ffn_in['norm2_w'], 'L1_ffn_w_router': _L1_ffn_in['w_router'], 'L1_ffn_w_gate_up': _L1_ffn_in['w_gate_up'], 'L1_ffn_w_down': _L1_ffn_in['w_down']}

def reference(x, L0_conv_w_qkv, L0_conv_b_qkv, L0_conv_w_proj, L0_conv_b_proj, L0_ffn_Wg, L0_ffn_e_bias, L0_ffn_W_gate_up, L0_ffn_W_down, L0_ffn_Wsg, L0_ffn_Wsu, L0_ffn_Wsd, L1_conv_Wq, L1_conv_bq, L1_conv_Wk, L1_conv_bk, L1_conv_Wv, L1_conv_bv, L1_conv_Wo, L1_conv_bo, L1_ffn_norm1_w, L1_ffn_w_qkv, L1_ffn_w_out, L1_ffn_norm2_w, L1_ffn_w_router, L1_ffn_w_gate_up, L1_ffn_w_down):
    import jax
    import jax.numpy as jnp

    def _L0_conv_ref(x, w_qkv, b_qkv, w_proj, b_proj):
        import jax, jax.numpy as jnp
        import numpy as np
        EMBED_DIM = 192
        NUM_HEADS = 12
        HEAD_DIM = EMBED_DIM // NUM_HEADS
        KERNEL = 7

        def _neighbor_index(size, kernel):
            start = np.clip(np.arange(size) - kernel // 2, 0, size - kernel)
            return jnp.asarray(start[:, None] + np.arange(kernel)[None, :])
        B, H, W, C = x.shape
        scale = HEAD_DIM ** (-0.5)
        qkv = (x @ w_qkv.T + b_qkv).reshape(B, H, W, 3, NUM_HEADS, HEAD_DIM)
        q = qkv[..., 0, :, :] * scale
        k = qkv[..., 1, :, :]
        v = qkv[..., 2, :, :]
        idx_i = _neighbor_index(H, KERNEL)
        idx_j = _neighbor_index(W, KERNEL)
        logits = []
        for ki in range(KERNEL):
            k_row = jnp.take(k, idx_i[:, ki], axis=1)
            for kj in range(KERNEL):
                k_nb = jnp.take(k_row, idx_j[:, kj], axis=2)
                logits.append(jnp.einsum('bhwnd,bhwnd->bhwn', q, k_nb))
        logits = jnp.stack(logits, axis=-1)
        attn = jax.nn.softmax(logits, axis=-1)
        out = jnp.zeros((B, H, W, NUM_HEADS, HEAD_DIM), dtype=x.dtype)
        off = 0
        for ki in range(KERNEL):
            v_row = jnp.take(v, idx_i[:, ki], axis=1)
            for kj in range(KERNEL):
                v_nb = jnp.take(v_row, idx_j[:, kj], axis=2)
                out = out + attn[..., off][..., None] * v_nb
                off += 1
        out = out.reshape(B, H, W, C)
        return out @ w_proj.T + b_proj

    def _L0_ffn_ref(hidden_states, Wg, e_bias, W_gate_up, W_down, Wsg, Wsu, Wsd):
        import jax, jax.numpy as jnp
        import numpy as np
        E = 32
        I = 464
        IS = 928
        K = 6
        G = 1
        TG = 1
        SCALE = 2.5
        CAP = 48

        def moe_forward(hidden_states, Wg, e_bias, W_gate_up, W_down, Wsg, Wsu, Wsd):
            B, S, H = hidden_states.shape
            x = hidden_states.reshape(-1, H)
            T = x.shape[0]
            logits = x.astype(jnp.float32) @ Wg.T
            sig = jax.nn.sigmoid(logits)
            choice = sig + e_bias[None, :]
            grp = choice.reshape(T, G, E // G)
            group_scores = jax.lax.top_k(grp, 2)[0].sum(-1)
            gidx = jax.lax.top_k(group_scores, TG)[1]
            gmask = jnp.zeros((T, G), jnp.float32).at[jnp.arange(T)[:, None], gidx].set(1.0)
            smask = jnp.repeat(gmask, E // G, axis=1)
            scores_for_choice = jnp.where(smask > 0, choice, 0.0)
            topk_idx = jax.lax.top_k(scores_for_choice, K)[1]
            topk_w = jnp.take_along_axis(sig, topk_idx, axis=1)
            topk_w = topk_w / (topk_w.sum(-1, keepdims=True) + 1e-20)
            topk_w = topk_w * SCALE
            P = T * K
            flat_e = topk_idx.reshape(-1)
            order = jnp.argsort(flat_e)
            se = flat_e[order]
            counts = jax.ops.segment_sum(jnp.ones(P, jnp.int32), flat_e, num_segments=E)
            starts = jnp.cumsum(counts) - counts
            pos = jnp.arange(P) - starts[se]
            buf_idx = jnp.where(pos < CAP, se * CAP + pos, E * CAP)
            tok_of_pair = (order // K).astype(jnp.int32)
            w_of_pair = topk_w.reshape(-1)[order]
            token_buf = jnp.zeros((E * CAP,), jnp.int32).at[buf_idx].set(tok_of_pair, mode='drop')
            w_buf = jnp.zeros((E * CAP,), x.dtype).at[buf_idx].set(w_of_pair.astype(x.dtype), mode='drop')
            xb = x[token_buf].reshape(E, CAP, H)
            gu = jnp.einsum('ech,ehf->ecf', xb, W_gate_up)
            g, u = jnp.split(gu, 2, axis=-1)
            inter = jax.nn.silu(g) * u
            yb = jnp.einsum('eci,eih->ech', inter, W_down)
            yb = yb * w_buf.reshape(E, CAP, 1)
            routed = jnp.zeros((T, H), x.dtype).at[token_buf].add(yb.reshape(E * CAP, H))
            shared = jax.nn.silu(x @ Wsg) * (x @ Wsu) @ Wsd
            return (routed + shared).reshape(B, S, H)
        return moe_forward(hidden_states, Wg, e_bias, W_gate_up, W_down, Wsg, Wsu, Wsd)

    def _L1_conv_ref(x, Wq, bq, Wk, bk, Wv, bv, Wo, bo):
        import jax, jax.numpy as jnp
        import numpy as np
        DIM = 192
        NUM_HEADS = 12
        HEAD_DIM = DIM // NUM_HEADS

        def _split_heads(t, b, h, w):
            return t.reshape(b, h, w, NUM_HEADS, HEAD_DIM).transpose(0, 3, 1, 2, 4)
        b, h, w, _ = x.shape
        q = _split_heads(x @ Wq + bq, b, h, w)
        k = _split_heads(x @ Wk + bk, b, h, w)
        v = _split_heads(x @ Wv + bv, b, h, w)
        scale = 1.0 / np.sqrt(HEAD_DIM).astype(np.float32)
        scores = jnp.einsum('bnhqd,bnhkd->bnhqk', q, k) * scale
        attn = jax.nn.softmax(scores, axis=-1)
        out = jnp.einsum('bnhqk,bnhkd->bnhqd', attn, v)
        out = out.transpose(0, 2, 3, 1, 4).reshape(b, h, w, DIM)
        return out @ Wo + bo

    def _L1_ffn_ref(x, norm1_w, w_qkv, w_out, norm2_w, w_router, w_gate_up, w_down):
        import jax, jax.numpy as jnp
        import numpy as np
        HID = 192
        NQ = 12
        NKV = 3
        HD = 16
        REP = NQ // NKV
        E = 16
        TOPK = 2
        FF = 384
        EPS = 1e-06
        THETA = 10000.0

        def rms_norm(x, w):
            return x / jnp.sqrt(jnp.mean(x * x, axis=-1, keepdims=True) + EPS) * w

        def rope_tables(seq_len):
            inv = 1.0 / THETA ** (jnp.arange(0, HD, 2, dtype=jnp.float32) / HD)
            f = jnp.arange(seq_len, dtype=jnp.float32)[:, None] * inv[None, :]
            return (jnp.cos(f), jnp.sin(f))

        def apply_rope(t, cos, sin):
            B, S, H, _ = t.shape
            tr = t.reshape(B, S, H, HD // 2, 2)
            c = cos[None, :, None, :]
            s = sin[None, :, None, :]
            r0 = tr[..., 0] * c - tr[..., 1] * s
            r1 = tr[..., 0] * s + tr[..., 1] * c
            return jnp.stack([r0, r1], axis=-1).reshape(B, S, H, HD)

        def attention(x, w_qkv, w_out):
            B, S, _ = x.shape
            qkv = x @ w_qkv
            q, k, v = jnp.split(qkv, [NQ * HD, (NQ + NKV) * HD], axis=-1)
            q = q.reshape(B, S, NQ, HD)
            k = k.reshape(B, S, NKV, HD)
            v = v.reshape(B, S, NKV, HD)
            cos, sin = rope_tables(S)
            q = apply_rope(q, cos, sin)
            k = apply_rope(k, cos, sin)
            k = jnp.repeat(k, REP, axis=2)
            v = jnp.repeat(v, REP, axis=2)
            q = q.transpose(0, 2, 1, 3)
            k = k.transpose(0, 2, 1, 3)
            v = v.transpose(0, 2, 1, 3)
            scores = jnp.einsum('bhqd,bhkd->bhqk', q, k) / jnp.sqrt(jnp.float32(HD))
            causal = jnp.tril(jnp.ones((S, S), dtype=bool))
            scores = jnp.where(causal[None, None], scores, jnp.finfo(scores.dtype).min)
            attn = jax.nn.softmax(scores, axis=-1)
            out = jnp.einsum('bhqk,bhkd->bhqd', attn, v)
            out = out.transpose(0, 2, 1, 3).reshape(B, S, NQ * HD)
            return out @ w_out

        def moe_ffn(x2d, w_router, w_gate_up, w_down):
            logits = x2d @ w_router
            probs = jax.nn.softmax(logits, axis=-1)
            vals, idx = jax.lax.top_k(probs, TOPK)
            vals = vals / jnp.sum(vals, axis=-1, keepdims=True)
            combine = jnp.sum(jax.nn.one_hot(idx, E, dtype=x2d.dtype) * vals[..., None], axis=1)
            out = jnp.zeros_like(x2d)
            for e in range(E):
                gu = x2d @ w_gate_up[e]
                gate, up = jnp.split(gu, 2, axis=-1)
                h = jax.nn.silu(gate) * up
                out = out + combine[:, e:e + 1] * (h @ w_down[e])
            return out
        B, S, _ = x.shape
        h = x + attention(rms_norm(x, norm1_w), w_qkv, w_out)
        moe_in = rms_norm(h, norm2_w).reshape(B * S, HID)
        out = h + moe_ffn(moe_in, w_router, w_gate_up, w_down).reshape(B, S, HID)
        return out

    def _gn(v, G=32, eps=1e-05):
        B_, H_, W_, C_ = v.shape
        g = v.reshape(B_, H_, W_, G, C_ // G)
        m = jnp.mean(g, axis=(1, 2, 4), keepdims=True)
        s = jnp.var(g, axis=(1, 2, 4), keepdims=True)
        return ((g - m) / jnp.sqrt(s + eps)).reshape(v.shape)

    def _ln_c(v, eps=1e-06):
        m = jnp.mean(v, axis=-1, keepdims=True)
        s = jnp.var(v, axis=-1, keepdims=True)
        return (v - m) / jnp.sqrt(s + eps)

    def _ln_t(v, eps=1e-05):
        m = jnp.mean(v, axis=-1, keepdims=True)
        s = jnp.var(v, axis=-1, keepdims=True)
        return (v - m) / jnp.sqrt(s + eps)

    def _to_tokens(v):
        B_, H_, W_, C_ = v.shape
        return v.reshape(B_, H_ * W_, C_)

    def _from_tokens(t, like):
        return t.reshape(like.shape)
    x = x + _L0_conv_ref(_ln_c(x), L0_conv_w_qkv, L0_conv_b_qkv, L0_conv_w_proj, L0_conv_b_proj)
    t = _to_tokens(x)
    t = t + _L0_ffn_ref(_ln_t(t), L0_ffn_Wg, L0_ffn_e_bias, L0_ffn_W_gate_up, L0_ffn_W_down, L0_ffn_Wsg, L0_ffn_Wsu, L0_ffn_Wsd)
    x = _from_tokens(t, x)
    x = x + _L1_conv_ref(_ln_c(x), L1_conv_Wq, L1_conv_bq, L1_conv_Wk, L1_conv_bk, L1_conv_Wv, L1_conv_bv, L1_conv_Wo, L1_conv_bo)
    t = _to_tokens(x)
    t = t + _L1_ffn_ref(_ln_t(t), L1_ffn_norm1_w, L1_ffn_w_qkv, L1_ffn_w_out, L1_ffn_norm2_w, L1_ffn_w_router, L1_ffn_w_gate_up, L1_ffn_w_down)
    x = _from_tokens(t, x)
    return x

_drawn_inputs = setup_inputs


def setup_inputs(seed=0):
    import zlib

    import numpy as np

    out = dict(_drawn_inputs(seed))
    spreads = {'L0_ffn_e_bias': (0.0, 0.8), 'L1_ffn_norm1_w': (1.0, 0.6), 'L1_ffn_norm2_w': (1.0, 0.6)}
    factors = {'L0_conv_b_qkv': 2.839,
     'L0_conv_b_proj': 2.782,
     'L0_ffn_Wg': 8.0,
     'L0_ffn_W_gate_up': 8.0,
     'L0_ffn_W_down': 8.0,
     'L1_conv_bq': 8.0,
     'L1_conv_bk': 8.0,
     'L1_ffn_w_qkv': 7.58,
     'L1_ffn_w_out': 7.715,
     'L1_ffn_w_router': 8.0,
     'L1_ffn_w_gate_up': 8.0,
     'L1_ffn_w_down': 8.0}
    for name, (base, spread) in spreads.items():
        noise = np.random.default_rng([zlib.crc32(name.encode()), seed]).standard_normal(out[name].shape)
        drawn = base * np.exp(spread * noise) if base else spread * noise
        out[name] = jnp.asarray(drawn.astype(out[name].dtype))
    for name, factor in factors.items():
        out[name] = (out[name] * factor).astype(out[name].dtype)
    return out
```

```python
from contextlib import ExitStack

import numpy as np

import concourse.bass as bass
from concourse import mybir

P = 128
B, IMG, C = 8, 16, 192
NT = B * IMG * IMG // P
TOK = NT * P
NH, HD = 12, 16
WIN = 7
KC, KP = 2, C // 2
E0, I0, IS0, TOP0, CAP = 32, 464, 928, 6, 48
SLOT = 64
NPAIR = E0 // 2
DC0 = 4
DP0 = I0 // DC0
SC = IS0 // DP0
E1, FF, NKV = 16, 384, 3
REP = NH // NKV
DC1 = FF // P
NSORT = 2 * TOK // P + E1
KW0 = 11 * IMG
BIG = 3.0e38
NEG = -1.0e30
RING = 2

F32 = mybir.dt.float32
BF16 = mybir.dt.bfloat16
I32 = mybir.dt.int32
U32 = mybir.dt.uint32
ALU = mybir.AluOpType
ACT = mybir.ActivationFunctionType
AX = mybir.AxisListType.X

CF = {}
CB = {}


def _lay(table, items):
    at = 0
    for name, n in items:
        table[name] = (at, n)
        at += n
    return at


NCF = _lay(CF, [("ident", P), ("iota_slot", CAP), ("iota_tok", P), ("cos", 2 * HD), ("sin", 2 * HD),
                ("pick", E0), ("tiles", 16), ("sorted", NSORT), ("half", 2), ("neg", 10)])
NCB = _lay(CB, [("identb", P), ("tri", P), ("ones", P), ("mask_n", 4 * KW0), ("mask_w", 512),
                ("mask_c0", 512), ("mask_c1", 512), ("tokinfo", 6)])


def constants():
    f = np.zeros((P, NCF), np.float32)
    b = np.zeros((P, NCB), np.float32)
    p = np.arange(P)

    def put(arr, table, name, val):
        at, n = table[name]
        arr[:, at:at + n] = np.asarray(val, np.float32).reshape(P, n) if np.ndim(val) > 1 else val
    put(f, CF, "ident", np.eye(P))
    put(f, CF, "iota_slot", np.arange(CAP))
    put(f, CF, "iota_tok", np.arange(P))
    s = np.arange(2)[None, :, None] * P + p[:, None, None]
    inv = (1.0 / np.float32(10000.0) ** (np.arange(0, HD, 2, dtype=np.float32) / HD)).astype(np.float32)
    ang = (s.astype(np.float32) * inv[None, None, :]).astype(np.float32)
    put(f, CF, "cos", np.concatenate([np.cos(ang), np.cos(ang)], 2).reshape(P, -1))
    put(f, CF, "sin", np.concatenate([np.sin(ang), np.sin(ang)], 2).reshape(P, -1))
    put(f, CF, "tiles", np.arange(16) * P)
    put(f, CF, "sorted", np.arange(NSORT))
    put(f, CF, "half", np.stack([p < SLOT, p >= SLOT], 1))
    put(f, CF, "neg", np.repeat([-0.5, 1.0, 1.0 / C, 1e-6, 1e-5], 2))
    put(b, CB, "identb", np.eye(P))
    put(b, CB, "tri", (p[:, None] < p[None, :]))
    put(b, CB, "ones", 1.0)
    start = np.clip(np.arange(IMG) - WIN // 2, 0, IMG - WIN)
    m = np.zeros((P, 2, 2, KW0))
    for t, k0 in ((0, 0), (1, 2 * P - KW0)):
        q, k = t * P + p, k0 + np.arange(KW0)
        qr, qc, kr, kc = q // IMG, q % IMG, k // IMG, k % IMG
        seen = ((kr[None] >= start[qr][:, None]) & (kr[None] < start[qr][:, None] + WIN)
                & (kc[None] >= start[qc][:, None]) & (kc[None] < start[qc][:, None] + WIN))
        m[:, t] = np.where(seen, 0.0, NEG)[:, None, :]
    put(b, CB, "mask_n", m.reshape(P, -1))
    w = np.where(p[:, None] // IMG == p[None] // IMG, 0.0, NEG)
    put(b, CB, "mask_w", np.tile(w, (1, 4)))
    c0 = np.where(p[:, None] >= p[None], 0.0, NEG)
    put(b, CB, "mask_c0", np.tile(c0, (1, 4)))
    k2 = np.arange(2 * P)
    put(b, CB, "mask_c1", np.tile(np.where(P + p[:, None] >= k2[None], 0.0, NEG), (1, 2)))
    put(b, CB, "tokinfo", np.stack([np.zeros(P), p, np.ones(P), np.ones(P), p, np.ones(P)], 1))
    return f, b


ONE, PER_C, EPS6, EPS5 = 2, 4, 6, 8


class Attention:

    def __init__(self, name, kinds, dve_links):
        self.name = name
        self.groups = []
        self.last_of_tile = {}
        for t, width, k0, kw, pieces, mask in kinds:
            for h0 in range(0, NH, width):
                self.groups.append((t, list(range(h0, h0 + width)), k0, kw, pieces, mask))
            self.last_of_tile[t] = len(self.groups) - 1
        self.n = len(self.groups)
        self.by_dve = (self.n + 1) // 2
        self.by_act = self.n // 2


NEIGH = Attention("n", [(0, 2, 0, KW0, [(0, P, 0), (P, KW0 - P, 1)], ("mask_n", 0)),
                        (1, 2, 2 * P - KW0, KW0, [(0, KW0 - P, 2), (KW0 - P, P, 1)], ("mask_n", 2 * KW0))], 0)
WINDOW = Attention("w", [(0, 4, 0, P, [(0, P, 0)], ("mask_w", 0)),
                         (1, 4, P, P, [(0, P, 1)], ("mask_w", 0))], 0)
CAUSAL = Attention("c", [(0, 4, 0, P, [(0, P, 0)], ("mask_c0", 0)),
                         (1, 2, 0, 2 * P, [(0, P, 0), (P, P, 1)], ("mask_c1", 0))], 0)

LINKS = {"A": 27, "B": 14, "C": 42}
UPTO = "G"


def build(nc, d, out):
    ctx = ExitStack()
    with ctx:
        def sb(name, shape, dt=F32):
            return ctx.enter_context(nc.sbuf_tensor(name, shape, dt))

        def sem(name):
            return ctx.enter_context(nc.semaphore(name))

        cf = sb("cf", [P, NCF])
        cb = sb("cb", [P, NCB], BF16)

        def cst(name):
            at, n = CF[name]
            return cf[:, at:at + n]

        def cstb(name, off=0, n=None):
            at, m = CB[name]
            return cb[:, at + off:at + off + (n if n is not None else m - off)]

        ident = cst("ident")

        x_all = sb("x_all", [P, NT, C])
        m_all = sb("m_all", [P, NT, C])
        mask12_all = sb("mask12_all", [P, NT, 2, E1], BF16)
        before_all = sb("before_all", [P, NT + 1, E1], BF16)
        w12_all = sb("w12_all", [P, NT, 2])

        wqkv = sb("wqkv", [KP, KC, 3 * C])
        wproj = sb("wproj", [KP, KC, C])
        brow = sb("brow", [P, 4 * C])
        wg0 = sb("wg0", [KP, KC, E0])
        ebias = sb("ebias", [P, E0])
        wqkvf = sb("wqkvf", [KP, KC, (NH + 2 * NKV) * HD])
        wof = sb("wof", [KP, KC, C])
        norm_w = sb("norm_w", [P, 2, C])
        wr1 = sb("wr1", [KP, KC, E1])

        GU0 = KC * 2 * I0
        DN0 = DC0 * C
        GU1 = KC * 2 * FF
        DN1 = DC1 * C
        R = sb("R", [P, E1 * (GU1 + DN1)])
        gu1_all = R[0:KP, 0:E1 * GU1].rearrange("p (e k f) -> p e k f", e=E1, k=KC)
        dn1_all = R[:, E1 * GU1:E1 * (GU1 + DN1)].rearrange("p (e c f) -> p e c f", e=E1, c=DC1)
        low, high = [0], [E1 * (GU1 + DN1)]

        def carve(words, at_end):
            if at_end:
                high[0] -= words
                start = high[0]
            else:
                start = low[0]
                low[0] += words
            assert low[0] <= high[0], (low, high)
            return R[:, start:start + words]

        ring_gu = [carve(2 * GU0, False)[0:KP, :].rearrange("p (h k f) -> p h k f", h=2, k=KC) for _ in range(RING)]
        ring_dn = [carve(2 * DN0, False)[0:DP0, :].rearrange("p (h c f) -> p h c f", h=2, c=DC0) for _ in range(RING)]
        wsg = carve(KC * IS0, False)[0:KP, :].rearrange("p (k f) -> p k f", k=KC)
        wsu = carve(KC * IS0, False)[0:KP, :].rearrange("p (k f) -> p k f", k=KC)
        wsd = carve(SC * C, False)[0:DP0, :].rearrange("p (c f) -> p c f", c=SC)
        onehot = [carve(E0 * SLOT // 2, False).bitcast(BF16).rearrange("p (e s) -> p e s", e=E0) for _ in range(2)]

        xn = carve(2 * C, True).rearrange("p (t c) -> p t c", t=2)
        xnT = carve(KC * 2 * P, True)[0:KP, :].rearrange("p (k t) -> p k t", k=KC)
        qk_pad = carve(2 * 2 * NH * 32, True).rearrange("p (t h e) -> p t h e", t=2, e=32)
        qkT = carve(8 * 2 * P, True).rearrange("p (c t) -> p c t", c=8)
        v_sb = carve(3 * NH * (HD + 1), True).rearrange("p (v h e) -> p v h e", v=3, h=NH)
        probs = carve(2 * 512, True).rearrange("p (b k) -> p b k", b=2)
        probsT = carve(2 * 512, True).rearrange("p (b k) -> p b k", b=2)
        o_sb = carve(2 * C, True).rearrange("p (t c) -> p t c", t=2)
        row0 = carve(2 * (C + E0), True).rearrange("p (t c) -> p t c", t=2)
        tmp = carve(2 * C, True).rearrange("p (t c) -> p t c", t=2)
        u_sb = carve(2 * C, True).rearrange("p (t c) -> p t c", t=2)
        y0_words = carve(NPAIR * 3 * C // 2, True)
        y0_all = y0_words.bitcast(BF16).rearrange("p (j s c) -> p j s c", j=NPAIR, s=3)
        hT_words = carve(SC * 2 * P, True)
        hT = hT_words[0:DP0, :].rearrange("p (c t) -> p c t", c=SC)
        comb_s = hT_words.bitcast(BF16).rearrange("p (t j k) -> p t j k", t=2, j=NPAIR)
        rope_c = hT_words[:, 0:15 * HD].rearrange("p (h e) -> p h e", e=HD)
        rope_s = hT_words[:, 15 * HD:30 * HD].rearrange("p (h e) -> p h e", e=HD)

        neg_max = sb("neg_max", [P, 2, 4])
        rden = sb("rden", [P, 2, NH])
        stats = sb("stats", [P, 2, 6])
        mean_var = sb("mean_var", [P, 2, 2])
        rstd = sb("rstd", [P, 2])
        sumsq = sb("sumsq", [P, 2])
        expl = sb("expl", [P, 2, E0])
        sig = sb("sig", [P, 2, E0])
        choice = sb("choice", [P, 2, 2, E0 + 8])
        top8 = sb("top8", [P, 2, 2, 8])
        left = sb("left", [P, 2, 2, E0 + 8])
        mask = sb("mask", [P, 2, E0])
        mask_b = sb("mask_b", [P, 2, E0], BF16)
        before0 = sb("before0", [P, E0], BF16)
        tokinfo = sb("tokinfo", [P, 2, 3], BF16)
        wsum = sb("wsum", [P, 2, 2])
        pos = sb("pos", [P, 2, E0])
        ids_acc = sb("ids_acc", [P, NPAIR, 3])
        ids_f = sb("ids_f", [P, NPAIR])
        ids_i = sb("ids_i", [P, NPAIR], I32)
        ids_rel = sb("ids_rel", [P, NPAIR])
        scratch = sb("scratch", [P, 16])
        filled = sb("filled", [P, 2])
        h_sb = sb("h_sb", [P, 2, I0])
        hTs = sb("hTs", [P, 2, 4 * P])
        xs = sb("xs", [P, 2, C + E0])
        xsT = sb("xsT", [KP, 2, KC, P])
        wslot = sb("wslot", [P, 2, E0])
        wsl = sb("wsl", [P, 2, 2])
        y_f = sb("y_f", [P, 2, C])
        counts = sb("counts", [P, 6, E1])
        cmp = sb("cmp", [P, E1, 16])
        cmp2 = sb("cmp2", [P, NSORT, E1])
        slot_g = sb("slot_g", [P, NT, E1])
        slots = sb("slots", [P, 2, NT])
        slots_i = sb("slots_i", [P, 2, NT], I32)
        tile_e = sb("tile_e", [P, NSORT])
        tile_ei = sb("tile_ei", [P, NSORT], I32)

        BK = [ctx.enter_context(nc.psum_tensor(f"bank{j}", [P, 512], F32)) for j in range(8)]
        S0, S1, T0, T1, O0, O1, M0, M1 = BK
        SCORE, PT, OB = [S0, S1], [T0, T1], [O0, O1]

        rows0 = nc.dram_tensor("rows0", [TOK, C + E0], F32)
        sorted_x = nc.dram_tensor("sorted_x", [NSORT * P, C], F32)
        sorted_y = nc.dram_tensor("sorted_y", [NSORT * P, C], F32)
        rows0_t = rows0[:, :].rearrange("(i t p) c -> i p t c", t=2, p=P)

        S = {}

        def s(name):
            if name not in S:
                S[name] = sem(name)
            return S[name]

        def per_image(a, name):
            return {"scores": a.n, "max": a.n, "exp": a.n, "pt": a.n, "pv": a.n, "pta": a.by_act, "ptd": a.by_dve,
                    "pad": 2, "norm": 2, "qkv": 2 if a is CAUSAL else 3,
                    "v": 0 if a is CAUSAL else 1}.get(name, 1)

        def psem(name):
            return s(f"att_{name}")

        def count(a, name, i, k):
            if a is NEIGH:
                return i * per_image(a, name) + k
            turn = per_image(WINDOW, name) + per_image(CAUSAL, name)
            before = B * per_image(NEIGH, name) + (per_image(WINDOW, name) if a is CAUSAL else 0)
            return i * turn + (before + k)

        def await_(eng, a, name, i, k):
            eng.wait_ge(psem(name), count(a, name, i, k))

        for n in ("const_loaded", "x_loaded", "wa_loaded", "wc_loaded", "wf_loaded", "ffn1_loaded", "row_stored", "set",
                  "a_var", "a_rstd", "a_xn", "a_tn", "a_xT", "a_xTc", "a_logits", "a_expl", "a_mask", "a_pos",
                  "a_onehot", "a_ids", "a_gu", "a_silu", "a_h", "a_shared", "a_row", "a_link", "a_pool", "a_done",
                  "b_idf", "b_idx", "b_link", "b_done",
                  "c_onehot", "c_comb", "c_link", "c_var", "c_u", "c_ss", "c_rstd", "c_xn", "c_xT", "c_xTc",
                  "c_logits", "c_negmax", "c_expl", "c_pool", "c_m", "c_done", "c_sq",
                  "e_pos", "e_link", "e_slots", "e_tiles", "scattered", "zeroed", "g_link", "g_out", "stored"):
            s(n)
        for r in range(2):
            for n in ("ring", "xs", "b_xT", "b_xTc", "b_wslot", "b_gu", "b_silu", "b_h", "b_hT", "b_hTc", "b_y", "b_yc",
                      "f_loaded", "f_xT", "f_xTc", "f_gu", "f_silu", "f_h", "f_hT", "f_hTc", "f_y", "f_yc", "f_stored",
                      "g_got", "g_used"):
                s(f"{n}{r}")
        for n in ("qkv", "pad", "v", "qkT", "qkTa", "qkTd", "scores", "max", "exp", "pt", "pta", "ptd", "pv",
                  "norm", "oT", "oTc", "proj"):
            psem(n)

        block = ctx.enter_context(nc.Block())

        def settle():
            nc.vector.memset(scratch[:, 0:1], 0.0)

        class Links:

            def __init__(self, eng, sm, i, per):
                self.eng, self.sm, self.base, self.k, self.per = eng, sm, i * per, 0, per

            def inc(self, ins):
                self.k += 1
                ins.then_inc(self.sm, 1)

            def __call__(self, ins):
                self.inc(ins)
                self.eng.wait_ge(self.sm, self.base + self.k)

            def end(self):
                assert self.k == self.per, (self.sm, self.k)

        def q_ap(h, t):
            at = 32 * (h // REP)
            return qkT[at:at + HD, h % REP, t * P:(t + 1) * P]

        def k_ap(a, h, k0, kw):
            at = 32 * (h // REP)
            return qkT[at:at + HD, REP + (0 if a is CAUSAL else h % REP), k0:k0 + kw]

        def v_ap(a, h, n, vt):
            return v_sb[0:n, vt, h // REP if a is CAUSAL else h, :]

        def pad_shape(a):
            return (REP + 1 if a is CAUSAL else 2 * REP), 3 * 32

        def attention_pe(pe, a, i):
            chunks, cw = pad_shape(a)
            for t in range(2):
                await_(pe, a, "pad", i, t + 1)
                for c in range(chunks):
                    ins = nc.tensor.transpose(BK[c // 2][0:cw, (c % 2) * 256 + t * P:(c % 2) * 256 + (t + 1) * P],
                                              qk_pad[:, t, :, :].rearrange("p a b -> p (a b)")[:, c * cw:(c + 1) * cw],
                                              ident)
            ins.then_inc(psem("qkT"), 1)
            await_(pe, a, "qkTa", i, 1)
            await_(pe, a, "qkTd", i, 1)

            def scores(u):
                t, heads, k0, kw, _, (mname, moff) = a.groups[u]
                if u >= 2:
                    await_(pe, a, "exp", i, u - 1)
                bank = SCORE[u % 2]
                nc.tensor.matmul(bank[:, 0:len(heads) * kw], cstb("identb"), cstb(mname, moff, len(heads) * kw),
                                 start=True, stop=False)
                for g, h in enumerate(heads):
                    ins = nc.tensor.matmul(bank[:, g * kw:(g + 1) * kw], q_ap(h, t), k_ap(a, h, k0, kw),
                                           start=False, stop=(g == len(heads) - 1))
                ins.then_inc(psem("scores"), 1)

            def transposes(u):
                t, heads, k0, kw, pieces, _ = a.groups[u]
                await_(pe, a, "exp", i, u + 1)
                if u >= 2:
                    if u % 2 == 0:
                        await_(pe, a, "ptd", i, u // 2)
                    else:
                        await_(pe, a, "pta", i, u // 2)
                for c, (c0, n, _) in sorted(enumerate(pieces), key=lambda e: -e[1][1]):
                    for g in range(len(heads)):
                        col = (c * len(heads) + g) * P
                        ins = nc.tensor.transpose(PT[u % 2][0:n, col:col + P],
                                                  probs[:, u % 2, g * kw + c0:g * kw + c0 + n], ident)
                ins.then_inc(psem("pt"), 1)

            def pv(u):
                t, heads, k0, kw, pieces, _ = a.groups[u]
                if u == 0 and a is not CAUSAL:
                    await_(pe, a, "v", i, 1)
                if u % 2 == 0:
                    await_(pe, a, "ptd", i, u // 2 + 1)
                else:
                    await_(pe, a, "pta", i, u // 2 + 1)
                for g, h in enumerate(heads):
                    for c, (c0, n, vt) in enumerate(pieces):
                        col = (c * len(heads) + g) * P
                        ins = nc.tensor.matmul(OB[t][:, h * (HD + 1):(h + 1) * (HD + 1)],
                                               probsT[0:n, u % 2, col:col + P], v_ap(a, h, n, vt),
                                               start=(c == 0), stop=(c == len(pieces) - 1))
                ins.then_inc(psem("pv"), 1)

            for u in range(a.n + 2):
                if u < a.n:
                    scores(u)
                if 1 <= u <= a.n:
                    transposes(u - 1)
                if u >= 2:
                    pv(u - 2)
            for t in range(2):
                await_(pe, a, "norm", i, t + 1)
                for k in range(KC):
                    ins = nc.tensor.transpose(M0[0:KP, k * 256 + t * P:k * 256 + (t + 1) * P],
                                              o_sb[:, t, :].rearrange("p (f k) -> p k f", k=KC)[:, k, :], ident)
            ins.then_inc(psem("oT"), 1)

        def project(pe, a, w, i):
            await_(pe, a, "oTc", i, 1)
            for t in range(2):
                for k in range(KC):
                    ins = nc.tensor.matmul(M1[:, t * C:(t + 1) * C], xnT[:, k, t * P:(t + 1) * P], w[:, k, :],
                                           start=(k == 0), stop=(k == KC - 1))
            ins.then_inc(psem("proj"), 1)

        def attention_dve(dve, a, i, link):
            def copy_pt(u):
                _, heads, _, _, pieces, _ = a.groups[u]
                await_(dve, a, "pt", i, u + 1)
                if u >= 2:
                    await_(dve, a, "pv", i, u - 1)
                w = len(heads) * P
                for c, (_, n, _) in enumerate(pieces):
                    ins = nc.vector.tensor_copy(probsT[0:n, u % 2, c * w:(c + 1) * w], PT[u % 2][0:n, c * w:(c + 1) * w])
                ins.then_inc(psem("ptd"), 1)

            def normalise(t):
                await_(dve, a, "pv", i, a.last_of_tile[t] + 1)
                ov = OB[t][:, 0:NH * (HD + 1)].rearrange("p (h e) -> p h e", e=HD + 1)
                link(nc.vector.reciprocal(rden[:, t, :], ov[:, :, HD]))
                nc.vector.tensor_tensor(o_sb[:, t, :].rearrange("p (h e) -> p h e", e=HD), ov[:, :, 0:HD],
                                        rden[:, t, :].unsqueeze(2).to_broadcast([P, NH, HD]), ALU.mult)\
                    .then_inc(psem("norm"), 1)

            for u in range(a.n + 3):
                if u < a.n:
                    _, heads, _, kw, _, _ = a.groups[u]
                    await_(dve, a, "scores", i, u + 1)
                    g = len(heads)
                    nc.vector.tensor_reduce(neg_max[:, u % 2, 0:g],
                                            SCORE[u % 2][:, 0:g * kw].rearrange("p (g k) -> p g k", g=g),
                                            AX, ALU.max, negate=True).then_inc(psem("max"), 1)
                if 1 <= u <= a.n and (u - 1) % 2 == 0:
                    copy_pt(u - 1)
                for t in range(2):
                    if u - 3 == a.last_of_tile[t]:
                        normalise(t)

        def attention_act(act, a, i):
            for u in range(a.n + 1):
                if u < a.n:
                    _, heads, _, kw, _, _ = a.groups[u]
                    await_(act, a, "max", i, u + 1)
                    if u >= 2:
                        await_(act, a, "pt", i, u - 1)
                    for g in range(len(heads)):
                        ins = nc.scalar.activation(probs[:, u % 2, g * kw:(g + 1) * kw],
                                                   SCORE[u % 2][:, g * kw:(g + 1) * kw], ACT.Exp,
                                                   bias=neg_max[:, u % 2, g:g + 1])
                    ins.then_inc(psem("exp"), 1)
                if u >= 1 and (u - 1) % 2 == 1:
                    v = u - 1
                    _, heads, _, _, pieces, _ = a.groups[v]
                    await_(act, a, "pt", i, v + 1)
                    if v >= 2:
                        await_(act, a, "pv", i, v - 1)
                    w = len(heads) * P
                    for c, (_, n, _) in enumerate(pieces):
                        ins = nc.scalar.activation(probsT[0:n, v % 2, c * w:(c + 1) * w], PT[v % 2][0:n, c * w:(c + 1) * w],
                                                   ACT.Copy)
                    ins.then_inc(psem("pta"), 1)
            await_(act, a, "oT", i, 1)
            nc.scalar.activation(xnT[:, :, :], M0[0:KP, :].rearrange("p (k t) -> p k t", k=KC), ACT.Copy)\
                .then_inc(psem("oTc"), 1)

        def qk_copies_act(act, a, i):
            cw = pad_shape(a)[1]
            await_(act, a, "qkT", i, 1)
            nc.scalar.activation(qkT[0:cw, 0:2, :], S0[0:cw, :].rearrange("p (c t) -> p c t", c=2), ACT.Copy,
                                 scale=float(HD) ** -0.5)
            ins = nc.scalar.activation(qkT[0:cw, 2:4, :], S1[0:cw, :].rearrange("p (c t) -> p c t", c=2), ACT.Copy,
                                       scale=float(HD) ** -0.5)
            ins.then_inc(psem("qkTa"), 1)

        def qk_copies_dve(dve, a, i):
            chunks, cw = pad_shape(a)
            n = chunks - 4
            await_(dve, a, "qkT", i, 1)
            for c in range(0, n, 2):
                m = min(2, n - c)
                ins = nc.vector.tensor_copy(qkT[0:cw, 4 + c:4 + c + m, :],
                                            PT[c // 2][0:cw, 0:m * 256].rearrange("p (c t) -> p c t", c=m))
            ins.then_inc(psem("qkTd"), 1)

        def transpose_pair(pe, src):
            for t in range(2):
                for k in range(KC):
                    ins = nc.tensor.transpose(M0[0:KP, k * 256 + t * P:k * 256 + (t + 1) * P],
                                              src[:, t, 0:C].rearrange("p (f k) -> p k f", k=KC)[:, k, :], ident)
            return ins

        def copy_pair(dst):
            return nc.scalar.activation(dst[:, :, :], M0[0:KP, :].rearrange("p (k t) -> p k t", k=KC), ACT.Copy)

        def conv_qkv_pe(pe, a, w, i):
            for t, bank in ((0, M1), (1, M0)):
                for k in range(KC):
                    ins = nc.tensor.matmul(bank[:, 0:2 * C], xnT[:, k, t * P:(t + 1) * P], w[:, k, 0:2 * C],
                                           start=(k == 0), stop=(k == KC - 1))
                ins.then_inc(psem("qkv"), 1)
            for t in range(2):
                for k in range(KC):
                    ins = nc.tensor.matmul(OB[t][:, 0:C], xnT[:, k, t * P:(t + 1) * P], w[:, k, 2 * C:3 * C],
                                           start=(k == 0), stop=(k == KC - 1))
            if a is NEIGH:
                n = KW0 - P
                for k in range(KC):
                    ins = nc.tensor.matmul(O0[0:n, C:2 * C], xnT[:, k, P - n:P], w[:, k, 2 * C:3 * C],
                                           start=(k == 0), stop=(k == KC - 1))
            ins.then_inc(psem("qkv"), 1)

        def conv_qkv_dve(dve, a, brow, i):
            for t, bank in ((0, M1), (1, M0)):
                await_(dve, a, "qkv", i, t + 1)
                nc.vector.tensor_tensor(qk_pad[:, t, :, 0:HD], bank[:, 0:2 * C].rearrange("p (h e) -> p h e", e=HD),
                                        brow[:, 0:2 * C].rearrange("p (h e) -> p h e", e=HD), ALU.add)\
                    .then_inc(psem("pad"), 1)
            await_(dve, a, "qkv", i, 3)
            parts = [(P, 0, O0[:, 0:C]), (P, 1, O1[:, 0:C])]
            if a is NEIGH:
                parts.append((KW0 - P, 2, O0[0:KW0 - P, C:2 * C]))
            for n, vt, src in parts:
                ins = nc.vector.tensor_tensor(v_sb[0:n, vt, :, 0:HD], src.rearrange("p (h e) -> p h e", e=HD),
                                              brow[0:n, 2 * C:3 * C].rearrange("p (h e) -> p h e", e=HD), ALU.add)
            ins.then_inc(psem("v"), 1)


        def tile_x(i, t):
            return x_all[:, bass.ds(2 * i + t, 1), :].rearrange("p a c -> p (a c)")

        def image_x(i):
            return x_all[:, bass.ds(2 * i, 2), :]

        def two(psum_cols):
            return psum_cols.rearrange("p (t c) -> p t c", t=2)

        def ln_stats(link, i, ready):
            settle()
            for t in range(2):
                (link if t else link.inc)(nc.vector.bn_stats(stats[:, t, :], tile_x(i, t)))
            settle()
            for t in range(2):
                ins = nc.vector.bn_aggr(mean_var[:, t, :], stats[:, t, :])
            ins.then_inc(ready, 1)

        def ln_apply(dst, i):
            for t in range(2):
                ins = nc.vector.tensor_scalar(dst[:, t, 0:C], tile_x(i, t), mean_var[:, t, 0:1], rstd[:, t:t + 1],
                                              ALU.subtract, ALU.mult)
            return ins

        EARLY = high[0] // GU1
        gu1_d = d["L1_ffn_w_gate_up"].rearrange("e (p k) f -> p e (k f)", k=KC)
        dn1_d = d["L1_ffn_w_down"].rearrange("e (p c) f -> p e (c f)", c=DC1)
        gu0_d = d["L0_ffn_W_gate_up"].rearrange("(j r h) (p k) f -> r j p h (k f)", r=2, h=2, k=KC)
        dn0_d = d["L0_ffn_W_down"].rearrange("(j r h) (p c) f -> r j p h (c f)", r=2, h=2, c=DC0)
        gu1_flat = R[0:KP, 0:E1 * GU1].rearrange("p (e w) -> p e w", e=E1)
        dn1_flat = R[:, E1 * GU1:E1 * (GU1 + DN1)].rearrange("p (e w) -> p e w", e=E1)
        sx = sorted_x[:, :].rearrange("(n r p) c -> r n p c", r=2, p=P)
        sy = sorted_y[:, :].rearrange("(n r p) c -> r n p c", r=2, p=P)

        def chunked(w):
            return w.rearrange("(p k) n -> p k n", k=KC)

        @block.sync
        def _(sp):
            sp.dma_start(cf[:, :], d["cf"]).then_inc(s("const_loaded"), 16)
            sp.dma_start(y0_words[:, 0:NCB], d["cb"]).then_inc(s("const_loaded"), 16)
            sp.dma_start(x_all[:, :, :], d["x"].rearrange("(n p) c -> p n c", p=P)).then_inc(s("x_loaded"), 16)
            for dst, src in ((wqkv, chunked(d["L0_conv_w_qkv"])), (wproj, chunked(d["L0_conv_w_proj"])),
                             (brow, d["brow0"]), (wg0, chunked(d["L0_ffn_Wg"])), (ebias, d["ebias"]),
                             (wsg, chunked(d["L0_ffn_Wsg"])), (wsu, chunked(d["L0_ffn_Wsu"])),
                             (wsd, d["L0_ffn_Wsd"].rearrange("(c p) n -> p c n", p=DP0))):
                sp.dma_start(dst[:, :] if len(dst.shape) == 2 else dst[:, :, :], src).then_inc(s("wa_loaded"), 16)

            def load_pair(jj, r):
                sp.dma_start(ring_gu[r].rearrange("p h k f -> p h (k f)"), gu0_d[r][jj]).then_inc(s(f"ring{r}"), 16)
                sp.dma_start(ring_dn[r].rearrange("p h c f -> p h (c f)"), dn0_d[r][jj]).then_inc(s(f"ring{r}"), 16)

            for r in range(2):
                load_pair(0, r)
            for dst, src in ((wqkvf, chunked(d["L1_ffn_w_qkv"])), (wof, chunked(d["L1_ffn_w_out"])),
                             (norm_w, d["norm_w"]), (wr1, chunked(d["L1_ffn_w_router"]))):
                sp.dma_start(dst[:, :, :], src).then_inc(s("wf_loaded"), 16)
            with sp.Fori(0, B) as i:
                sp.wait_ge(s("a_row"), i + 1)
                sp.dma_start(rows0_t[bass.ds(i, 1), :, :, :].rearrange("a p t c -> (a p) t c"), row0)\
                    .then_inc(s("row_stored"), 16)
            sp.wait_ge(s("a_done"), B)
            for dst, src in ((wqkv, chunked(d["L1_conv_w"])), (wproj, chunked(d["L1_conv_Wo"])), (brow, d["brow1"])):
                sp.dma_start(dst[:, :] if len(dst.shape) == 2 else dst[:, :, :], src).then_inc(s("wc_loaded"), 16)
            with sp.Fori(1, NPAIR // 2) as jj:
                for r in range(2):
                    sp.wait_ge(s(f"b_y{r}"), jj)
                    sp.dma_start(ring_gu[r].rearrange("p h k f -> p h (k f)"),
                                 gu0_d[r][bass.ds(jj, 1)].rearrange("a p h w -> (a p) h w")).then_inc(s(f"ring{r}"), 16)
                    sp.dma_start(ring_dn[r].rearrange("p h c f -> p h (c f)"),
                                 dn0_d[r][bass.ds(jj, 1)].rearrange("a p h w -> (a p) h w")).then_inc(s(f"ring{r}"), 16)
            for r in range(2):
                sp.wait_ge(s(f"b_y{r}"), NPAIR // 2)
            sp.dma_start(gu1_flat[:, 0:EARLY, :], gu1_d[:, 0:EARLY, :]).then_inc(s("ffn1_loaded"), 16)
            sp.wait_ge(s("c_done"), B)
            sp.wait_ge(s("c_m"), B + 1)
            sp.dma_start(gu1_flat[:, EARLY:E1, :], gu1_d[:, EARLY:E1, :]).then_inc(s("ffn1_loaded"), 16)
            sp.dma_start(dn1_flat[:, :, :], dn1_d).then_inc(s("ffn1_loaded"), 16)
            if UPTO == "G":
                with sp.Fori(0, NSORT // 2) as n:
                    for r in range(2):
                        sp.wait_ge(s(f"f_yc{r}"), n + 2)
                        sp.dma_start(sy[r][bass.ds(n, 1)].rearrange("a p c -> (a p) c"), y_f[:, r, :])\
                            .then_inc(s(f"f_stored{r}"), 16)
            o = out.rearrange("(n p) c -> p n c", p=P)
            for n in range(NT):
                sp.wait_ge(s("g_out"), n + 1)
                sp.dma_start(o[:, n, :], x_all[:, n, :]).then_inc(s("stored"), 16)
            sp.wait_ge(s("stored"), 16 * NT)

        @block.gpsimd
        def _(pool):
            def root(link, src, scale, eps):
                link(nc.gpsimd.tensor_tensor(rstd[:, :], src, cst("neg")[:, scale:scale + 2], ALU.mult))
                link(nc.gpsimd.tensor_tensor(rstd[:, :], rstd[:, :], cst("neg")[:, eps:eps + 2], ALU.add))
                return nc.gpsimd.tensor_tensor(rstd[:, :], rstd[:, :], cst("neg")[:, 0:2], ALU.pow)

            pool.wait_ge(s("const_loaded"), 32)
            with pool.Fori(0, B) as i:
                link = Links(pool, s("a_pool"), i, 4)
                for n, eps in enumerate((EPS6, EPS5)):
                    pool.wait_ge(s("a_var"), 2 * i + n + 1)
                    root(link, mean_var[:, :, 1], ONE, eps).then_inc(s("a_rstd"), 1)
                link.end()
            zero = cmp2[:, :, :].rearrange("p a b -> p (a b)")
            pool.wait_ge(s("set"), 1)
            zx = sorted_x[:, :].rearrange("(p a) c -> p (a c)", p=P)
            nz = NSORT * E1
            for z in range(NSORT * C // nz):
                pool.dma_start(zx[:, z * nz:(z + 1) * nz], zero).then_inc(s("zeroed"), 16)

            pool.wait_ge(s("b_idf"), 1)
            pool.wait_ge(s("row_stored"), 16 * B + 16)
            for j in range(NPAIR):
                r = j % 2
                if j >= 2:
                    pool.wait_ge(s(f"b_xT{r}"), j // 2)
                    pool.wait_ge(s(f"b_wslot{r}"), j // 2)
                pool.indirect_dma_start(out=xs[:, r, :], out_offset=None, in_=rows0[:, :],
                                        in_offset=bass.IndirectOffsetOnAxis(ids_i[:, j:j + 1], 0))\
                    .then_inc(s(f"xs{r}"), 16)
            with pool.Fori(0, B) as i:
                link = Links(pool, s("c_pool"), i, 8)
                for n, (sm, k, src, scale, eps) in enumerate((
                        ("c_var", 0, mean_var[:, :, 1], ONE, EPS6), ("c_var", 1, mean_var[:, :, 1], ONE, EPS5),
                        ("c_ss", 0, sumsq[:, :], PER_C, EPS6), ("c_ss", 1, sumsq[:, :], PER_C, EPS6))):
                    pool.wait_ge(s(sm), 2 * i + k + 1)
                    root(link, src, scale, eps).then_inc(s("c_rstd"), 1)
                link.end()
                pool.wait_ge(s("c_xn"), 3 * i + 3)
                nc.gpsimd.tensor_copy(m_all[:, bass.ds(2 * i, 2), :], xn[:, :, :]).then_inc(s("c_m"), 1)
            if UPTO == "G":
                pool.wait_ge(s("e_slots"), 1)
                pool.wait_ge(s("c_m"), B + 1)
                pool.wait_ge(s("zeroed"), 16 * (NSORT * C // nz))
                for n in range(NT):
                    for k in range(2):
                        pool.indirect_dma_start(out=sorted_x[:, :],
                                                out_offset=bass.IndirectOffsetOnAxis(slots_i[:, k, n:n + 1], 0),
                                                in_=m_all[:, n, :], in_offset=None).then_inc(s("scattered"), 16)
                pool.wait_ge(s("scattered"), 16 * 2 * NT)
                with pool.Fori(0, NSORT // 2) as n:
                    for r in range(2):
                        pool.wait_ge(s(f"f_xT{r}"), n + 1)
                        pool.dma_start(xs[:, r, 0:C], sx[r][bass.ds(n, 1)].rearrange("a p c -> (a p) c"))\
                            .then_inc(s(f"f_loaded{r}"), 16)
                for r in range(2):
                    pool.wait_ge(s(f"f_stored{r}"), 16 * (NSORT // 2) + 16)
                for n in range(NT):
                    r = n % 2
                    if n >= 2:
                        pool.wait_ge(s(f"g_used{r}"), n // 2)
                    for k in range(2):
                        pool.indirect_dma_start(out=(xs[:, r, 0:C], y_f[:, r, :])[k], out_offset=None,
                                                in_=sorted_y[:, :],
                                                in_offset=bass.IndirectOffsetOnAxis(slots_i[:, k, n:n + 1], 0))\
                            .then_inc(s(f"g_got{r}"), 16)

        @block.scalar
        def _(act):
            act.wait_ge(s("const_loaded"), 32)
            act.wait_ge(s("wa_loaded"), 16 * 8)
            with act.Fori(0, B) as i:
                act.wait_ge(s("a_xT"), 2 * i + 1)
                copy_pair(xnT).then_inc(s("a_xTc"), 1)
                qk_copies_act(act, NEIGH, i)
                attention_act(act, NEIGH, i)
                act.wait_ge(s("a_xT"), 2 * i + 2)
                copy_pair(xnT).then_inc(s("a_xTc"), 1)
                act.wait_ge(s("a_logits"), i + 1)
                nc.scalar.activation(expl[:, :, :], two(M1[:, 0:2 * E0]), ACT.Exp, scale=-1.0).then_inc(s("a_expl"), 1)
                for c in range(SC):
                    act.wait_ge(s("a_gu"), SC * i + c + 1)
                    if c >= 4:
                        act.wait_ge(s("a_h"), SC * i + c - 3)
                    nc.scalar.activation(probs[0:DP0, (c % 4) // 2, (c % 2) * 256:(c % 2) * 256 + 256],
                                         (S0, S1, O0, O1)[c % 4][0:DP0, 0:256], ACT.Silu).then_inc(s("a_silu"), 1)
            with act.Fori(0, NPAIR // 2) as jj:
                for r in range(2):
                    act.wait_ge(s(f"b_xT{r}"), jj + 1)
                    nc.scalar.activation(xsT[:, r, :, :], (M0, M1)[r][0:KP, 0:256].rearrange("p (k t) -> p k t", k=KC),
                                         ACT.Copy).then_inc(s(f"b_xTc{r}"), 1)
                for r in range(2):
                    act.wait_ge(s(f"b_gu{r}"), jj + 1)
                    nc.scalar.activation(h_sb[:, r, :], (S0, O0)[r][:, 0:I0], ACT.Silu).then_inc(s(f"b_silu{r}"), 1)
                for r in range(2):
                    act.wait_ge(s(f"b_hT{r}"), jj + 1)
                    nc.scalar.activation(hTs[0:DP0, r, :], PT[r][0:DP0, :], ACT.Copy).then_inc(s(f"b_hTc{r}"), 1)
            with act.Fori(0, B) as i:
                act.wait_ge(s("c_xT"), 3 * i + 1)
                copy_pair(xnT).then_inc(s("c_xTc"), 1)
                qk_copies_act(act, WINDOW, i)
                attention_act(act, WINDOW, i)

                def squares(n):
                    act.wait_ge(s("c_u"), 2 * i + n + 1)
                    for t in range(2):
                        ins = nc.scalar.activation(tmp[:, t, :], u_sb[:, t, :], ACT.Square, accum_out=sumsq[:, t:t + 1])
                    ins.then_inc(s("c_ss"), 1)
                squares(0)
                act.wait_ge(s("c_xT"), 3 * i + 2)
                copy_pair(xnT).then_inc(s("c_xTc"), 1)
                qk_copies_act(act, CAUSAL, i)
                attention_act(act, CAUSAL, i)
                squares(1)
                act.wait_ge(s("c_xT"), 3 * i + 3)
                copy_pair(xnT).then_inc(s("c_xTc"), 1)
                act.wait_ge(s("c_negmax"), i + 1)
                for t in range(2):
                    ins = nc.scalar.activation(expl[:, t, 0:E1], M1[:, t * E1:(t + 1) * E1], ACT.Exp,
                                               bias=wsum[:, t, 0:1], accum_out=wsum[:, t, 1:2])
                ins.then_inc(s("c_expl"), 1)
            if UPTO == "G":
                with act.Fori(0, NSORT // 2) as n:
                    for r in range(2):
                        act.wait_ge(s(f"f_xT{r}"), n + 2)
                        nc.scalar.activation(xsT[:, r, :, :],
                                             (M0, M1)[r][0:KP, 0:256].rearrange("p (k t) -> p k t", k=KC),
                                             ACT.Copy).then_inc(s(f"f_xTc{r}"), 1)
                    for r in range(2):
                        act.wait_ge(s(f"f_gu{r}"), n + 1)
                        nc.scalar.activation(h_sb[:, r, 0:FF], (S0, O0)[r][:, 0:FF], ACT.Silu)\
                            .then_inc(s(f"f_silu{r}"), 1)
                    for r in range(2):
                        act.wait_ge(s(f"f_hT{r}"), n + 1)
                        nc.scalar.activation(hTs[:, r, 0:FF], PT[r][:, 0:FF], ACT.Copy).then_inc(s(f"f_hTc{r}"), 1)

        @block.vector
        def _(dve):
            dve.wait_ge(s("const_loaded"), 32)
            nc.vector.memset(v_sb[:, :, :, :], 1.0)
            nc.vector.memset(qk_pad[:, :, :, :], 0.0)
            nc.vector.memset(choice[:, :, :, :], BIG)
            nc.vector.memset(before0[:, :], 0.0)
            nc.vector.memset(before_all[:, 0, :], 0.0)
            nc.vector.memset(ids_acc[:, :, :], 0.0)
            nc.vector.memset(onehot[0][:, :, :], 0.0)
            nc.vector.memset(onehot[1][:, :, :], 0.0)
            nc.vector.tensor_copy(cb[:, :], y0_words[:, 0:NCB])
            nc.vector.tensor_copy(tokinfo[:, :, :], y0_words[:, CB["tokinfo"][0]:NCB].rearrange("p (t n) -> p t n", t=2))
            nc.vector.memset(cmp2[:, :, :], 0.0).then_inc(s("set"), 1)
            ahead = [("c_m", 1), ("row_stored", 16)]
            ahead += [(f"{n}{r}", by) for r in range(2) for n, by in (("b_yc", 1), ("f_xT", 1), ("f_yc", 1),
                                                                      ("f_stored", 16))]
            for n, (name, by) in enumerate(ahead):
                nc.vector.memset(scratch[:, n + 1:n + 2], 0.0).then_inc(s(name), by)
            dve.wait_ge(s("set"), 1)
            dve.wait_ge(s("x_loaded"), 16)
            dve.wait_ge(s("wa_loaded"), 16 * 8)

            with dve.Fori(0, B) as i:
                link = Links(dve, s("a_link"), i, LINKS["A"])
                ln_stats(link, i, s("a_var"))
                dve.wait_ge(s("a_rstd"), 2 * i + 1)
                ln_apply(xn, i).then_inc(s("a_xn"), 1)
                conv_qkv_dve(dve, NEIGH, brow, i)
                qk_copies_dve(dve, NEIGH, i)
                attention_dve(dve, NEIGH, i, link)
                await_(dve, NEIGH, "proj", i, 1)
                link(nc.vector.tensor_tensor(tmp[:, :, :], two(M1[:, 0:2 * C]),
                                             brow[:, 3 * C:4 * C].unsqueeze(1).to_broadcast([P, 2, C]), ALU.add))
                link(nc.vector.tensor_tensor(image_x(i), image_x(i), tmp[:, :, :], ALU.add))
                ln_stats(link, i, s("a_var"))
                dve.wait_ge(s("a_rstd"), 2 * i + 2)
                dve.wait_ge(s("row_stored"), 16 * i + 16)
                ln_apply(row0, i).then_inc(s("a_tn"), 1)
                dve.wait_ge(s("a_expl"), i + 1)
                link(nc.vector.tensor_scalar(sig[:, :, :], expl[:, :, :], 1.0, None, ALU.add))
                link(nc.vector.reciprocal(sig[:, :, :], sig[:, :, :]))
                link(nc.vector.tensor_tensor(choice[:, :, 0, 0:E0], sig[:, :, :],
                                             ebias[:, :].unsqueeze(1).to_broadcast([P, 2, E0]), ALU.add))
                n = E0 + 8 - TOP0
                settle()
                for t in range(2):
                    (link if t else link.inc)(nc.vector.max(top8[:, t, 0, :], choice[:, t, 0, 0:n]))
                settle()
                for t in range(2):
                    (link if t else link.inc)(nc.vector.match_replace(left[:, t, 0, 0:n], top8[:, t, 0, :], choice[:, t, 0, 0:n], NEG))
                link(nc.vector.tensor_scalar(mask[:, :, :], left[:, :, 0, 0:E0], NEG / 2, None, ALU.is_le))
                nc.vector.tensor_copy(mask_b[:, :, :], mask[:, :, :]).then_inc(s("a_mask"), 1)
                link(nc.vector.tensor_tensor(expl[:, :, :], sig[:, :, :], mask[:, :, :], ALU.mult))
                link(nc.vector.tensor_reduce(wsum[:, :, 0], expl[:, :, :], AX, ALU.add))
                link(nc.vector.tensor_scalar(wsum[:, :, 0], wsum[:, :, 0], 1e-20, None, ALU.add))
                link(nc.vector.reciprocal(wsum[:, :, 1], wsum[:, :, 0]))
                for t in range(2):
                    ins = nc.vector.tensor_scalar(row0[:, t, C:C + E0], expl[:, t, :], wsum[:, t, 1:2], 2.5,
                                                  ALU.mult, ALU.mult)
                ins.then_inc(s("a_row"), 1)
                for c in range(SC):
                    dve.wait_ge(s("a_silu"), SC * i + c + 1)
                    nc.vector.tensor_tensor(hT[:, c, :], probs[0:DP0, (c % 4) // 2, (c % 2) * 256:(c % 2) * 256 + 256],
                                            (S0, S1, O0, O1)[c % 4][0:DP0, 256:512], ALU.mult).then_inc(s("a_h"), 1)
                link(nc.vector.tensor_scalar(sig[:, :, :], mask[:, :, :], -4096.0, 4096.0, ALU.mult, ALU.add))
                dve.wait_ge(s("a_pos"), i + 1)
                link(nc.vector.tensor_tensor(pos[:, :, :], two(M1[:, 0:2 * E0]), sig[:, :, :], ALU.add))
                for t in range(2):
                    ins = nc.vector.tensor_tensor(onehot[t][:, :, 0:CAP],
                                                  cst("iota_slot").unsqueeze(1).to_broadcast([P, E0, CAP]),
                                                  pos[:, t, :].unsqueeze(2).to_broadcast([P, E0, CAP]), ALU.is_equal)
                ins.then_inc(s("a_onehot"), 1)
                for t in range(2):
                    link(nc.vector.tensor_tensor(before0[:, :], before0[:, :], mask_b[:, t, :], ALU.add))
                dve.wait_ge(s("a_ids"), i + 1)
                link(nc.vector.tensor_tensor(ids_acc[:, :, :], ids_acc[:, :, :],
                                             T1[:, 0:3 * NPAIR].rearrange("p (j n) -> p j n", n=3), ALU.add))
                link(nc.vector.tensor_scalar(tokinfo[:, :, 0], tokinfo[:, :, 0], 2.0, None, ALU.add))
                dve.wait_ge(s("a_shared"), i + 1)
                link(nc.vector.tensor_tensor(image_x(i), image_x(i), two(M0[:, 0:2 * C]), ALU.add))
                nc.vector.tensor_copy(rden[:, 0, 0:1], cst("neg")[:, 0:1]).then_inc(s("a_done"), 1)
                link.end()

            nc.vector.scalar_tensor_tensor(ids_f[:, :], ids_acc[:, :, 0], float(P), ids_acc[:, :, 1], ALU.mult, ALU.add)\
                .then_inc(s("b_link"), 1)
            dve.wait_ge(s("b_link"), 1)
            nc.vector.tensor_copy(ids_rel[:, :], ids_f[:, :])
            nc.vector.tensor_copy(ids_i[:, :], ids_f[:, :]).then_inc(s("b_idf"), 1)
            with dve.Fori(0, NPAIR // 2) as jj:
                link = Links(dve, s("b_done"), jj, LINKS["B"])
                for r in range(2):
                    dve.wait_ge(s(f"xs{r}"), 16 * jj + 16)
                    link(nc.vector.tensor_tensor(wslot[:, r, 0:2], xs[:, r, bass.ds(4 * jj + 2 * r + C, 2)], cst("half"),
                                                 ALU.mult))
                    link(nc.vector.tensor_tensor(wsl[:, r, 0:1], wslot[:, r, 0:1], wslot[:, r, 1:2], ALU.add))
                    nc.vector.tensor_tensor(wsl[:, r, 1:2], wsl[:, r, 0:1],
                                            ids_acc[:, bass.ds(2 * jj + r, 1), 2], ALU.mult).then_inc(s(f"b_wslot{r}"), 1)
                for r in range(2):
                    dve.wait_ge(s(f"b_silu{r}"), jj + 1)
                    nc.vector.tensor_tensor(h_sb[:, r, :], h_sb[:, r, :], (S1, O1)[r][:, 0:I0], ALU.mult)\
                        .then_inc(s(f"b_h{r}"), 1)
                for r in range(2):
                    dve.wait_ge(s(f"b_y{r}"), jj + 1)
                    dve.wait_ge(s(f"b_wslot{r}"), jj + 1)

                    def part(k):
                        return y0_all[:, bass.ds(2 * jj + r, 1), k, :].rearrange("p a c -> p (a c)")
                    link(nc.vector.tensor_scalar(y_f[:, r, :], (M0, M1)[r][:, 256:256 + C], wsl[:, r, 1:2], None, ALU.mult))
                    link(nc.vector.tensor_copy(part(0), y_f[:, r, :]))
                    link(nc.vector.tensor_tensor(y_f[:, r, :], y_f[:, r, :], part(0), ALU.subtract))
                    link(nc.vector.tensor_copy(part(1), y_f[:, r, :]))
                    link(nc.vector.tensor_tensor(part(2), y_f[:, r, :], part(1), ALU.subtract))
                    nc.vector.tensor_copy(filled[:, r:r + 1], wsl[:, r, 1:2]).then_inc(s(f"b_yc{r}"), 1)
                link.end()

            dve.wait_ge(s("wc_loaded"), 16 * 3)
            dve.wait_ge(s("wf_loaded"), 16 * 4)
            with dve.Fori(0, B) as i:
                link = Links(dve, s("c_link"), i, LINKS["C"])
                for t in range(2):
                    for j in range(NPAIR):
                        ins = nc.vector.tensor_scalar(comb_s[:, t, j, :], cst("iota_tok"), ids_rel[:, j:j + 1], None,
                                                      ALU.is_equal)
                    ins.then_inc(s("c_onehot"), 1)
                    dve.wait_ge(s("c_onehot"), 2 * i + t + 1)
                    link(nc.vector.tensor_scalar(ids_rel[:, :], ids_rel[:, :], float(-P), None, ALU.add))
                dve.wait_ge(s("c_comb"), i + 1)
                link(nc.vector.tensor_tensor(image_x(i), image_x(i), two(M1[:, 0:2 * C]), ALU.add))
                ln_stats(link, i, s("c_var"))
                dve.wait_ge(s("c_rstd"), 4 * i + 1)
                dve.wait_ge(s("c_m"), i + 1)
                ln_apply(xn, i).then_inc(s("c_xn"), 1)
                conv_qkv_dve(dve, WINDOW, brow, i)
                qk_copies_dve(dve, WINDOW, i)
                attention_dve(dve, WINDOW, i, link)
                await_(dve, WINDOW, "proj", i, 1)
                link(nc.vector.tensor_tensor(tmp[:, :, :], two(M1[:, 0:2 * C]),
                                             brow[:, 3 * C:4 * C].unsqueeze(1).to_broadcast([P, 2, C]), ALU.add))
                link(nc.vector.tensor_tensor(image_x(i), image_x(i), tmp[:, :, :], ALU.add))
                ln_stats(link, i, s("c_var"))
                dve.wait_ge(s("c_rstd"), 4 * i + 2)
                link(ln_apply(u_sb, i))
                link(nc.vector.tensor_tensor(image_x(i), image_x(i), u_sb[:, :, :], ALU.add))
                nc.vector.tensor_copy(filled[:, 0:1], wsl[:, 0, 1:2]).then_inc(s("c_u"), 1)

                def rms(n):
                    dve.wait_ge(s("c_rstd"), 4 * i + 3 + n)
                    for t in range(2):
                        ins = nc.vector.scalar_tensor_tensor(xn[:, t, :], u_sb[:, t, :], rstd[:, t:t + 1], norm_w[:, n, :],
                                                             ALU.mult, ALU.mult)
                    ins.then_inc(s("c_xn"), 1)
                rms(0)
                nq = 15 * HD
                for t, bank in ((0, M1), (1, M0)):
                    await_(dve, CAUSAL, "qkv", i, t + 1)
                    qk = bank[:, 0:nq].rearrange("p (h e) -> p h e", e=HD)
                    pad = qk_pad[:, t, 0:15, :]
                    for dst, tab in ((rope_c, "cos"), (rope_s, "sin")):
                        link(nc.vector.tensor_tensor(dst, qk, cst(tab)[:, t * HD:(t + 1) * HD].unsqueeze(1)
                                                     .to_broadcast([P, 15, HD]), ALU.mult))
                    h = HD // 2
                    nc.vector.tensor_tensor(pad[:, :, 0:h], rope_c[:, :, 0:h], rope_s[:, :, h:HD], ALU.subtract)
                    link(nc.vector.tensor_tensor(pad[:, :, h:HD], rope_s[:, :, 0:h], rope_c[:, :, h:HD], ALU.add))
                    nc.vector.tensor_copy(v_sb[:, t, 0:NKV, 0:HD],
                                          bank[:, nq:nq + NKV * HD].rearrange("p (h e) -> p h e", e=HD))\
                        .then_inc(psem("pad"), 1)
                qk_copies_dve(dve, CAUSAL, i)
                attention_dve(dve, CAUSAL, i, link)
                await_(dve, CAUSAL, "proj", i, 1)
                link(nc.vector.tensor_tensor(u_sb[:, :, :], u_sb[:, :, :], two(M1[:, 0:2 * C]), ALU.add))
                link(nc.vector.tensor_tensor(image_x(i), image_x(i), two(M1[:, 0:2 * C]), ALU.add))
                nc.vector.tensor_copy(filled[:, 0:1], wsl[:, 0, 1:2]).then_inc(s("c_u"), 1)
                rms(1)
                dve.wait_ge(s("c_logits"), i + 1)
                nc.vector.tensor_reduce(wsum[:, :, 0], two(M1[:, 0:2 * E1]), AX, ALU.max, negate=True)\
                    .then_inc(s("c_negmax"), 1)
                dve.wait_ge(s("c_expl"), i + 1)
                link(nc.vector.reciprocal(wsum[:, :, 1], wsum[:, :, 1]))
                q0 = E0 - E1
                for t in range(2):
                    link(nc.vector.tensor_scalar(choice[:, t, 0, q0:E0], expl[:, t, 0:E1], wsum[:, t, 1:2], None, ALU.mult))
                settle()
                for t in range(2):
                    for k in range(2):
                        n = E0 + 6 + k
                        (link if t + k == 2 else link.inc)(nc.vector.max(top8[:, t, k, :], choice[:, t, 0, q0:n]))
                settle()
                for t in range(2):
                    for k in range(2):
                        n = E0 + 6 + k
                        (link if t + k == 2 else link.inc)(nc.vector.match_replace(left[:, t, k, q0:n], top8[:, t, k, :], choice[:, t, 0, q0:n], NEG))
                for t in range(2):
                    for k in range(2):
                        link(nc.vector.tensor_scalar(
                            mask12_all[:, bass.ds(2 * i + t, 1), k, :].rearrange("p a e -> p (a e)"),
                            left[:, t, k, q0:E0], NEG / 2, None, ALU.is_le))
                    link(nc.vector.tensor_tensor(before_all[:, bass.ds(2 * i + t + 1, 1), :],
                                                 before_all[:, bass.ds(2 * i + t, 1), :],
                                                 mask12_all[:, bass.ds(2 * i + t, 1), 0, :], ALU.add))
                link(nc.vector.tensor_tensor(wsum[:, :, 0], top8[:, :, 0, 7], top8[:, :, 1, 7], ALU.add))
                link(nc.vector.reciprocal(wsum[:, :, 1], wsum[:, :, 0]))
                for k in range(2):
                    ins = nc.vector.tensor_tensor(w12_all[:, bass.ds(2 * i, 2), k], top8[:, :, 1 - k, 7], wsum[:, :, 1],
                                                  ALU.mult)
                ins.then_inc(s("c_done"), 1)
                link.end()

            if UPTO != "G":
                dve.wait_ge(s("c_done"), B)
                for n in range(NT):
                    nc.vector.tensor_copy(filled[:, 0:1], wsl[:, 0, 1:2]).then_inc(s("g_out"), 1)
                return
            done = [0]

            def elink(ins):
                done[0] += 1
                ins.then_inc(s("e_link"), 1)
                dve.wait_ge(s("e_link"), done[0])

            dve.wait_ge(s("e_pos"), 1)
            elink(nc.vector.tensor_copy(counts[:, 0, :], T1[:, 0:E1]))
            elink(nc.vector.tensor_tensor(cmp[:, :, :], counts[:, 0, :].unsqueeze(2).to_broadcast([P, E1, 16]),
                                          cst("tiles").unsqueeze(1).to_broadcast([P, E1, 16]), ALU.is_gt))
            elink(nc.vector.tensor_reduce(counts[:, 1, :], cmp[:, :, :], AX, ALU.add))
            elink(nc.vector.tensor_copy(counts[:, 2, :], counts[:, 1, :]))
            cur, step = 2, 1
            while step < E1:
                nxt = 5 - cur
                elink(nc.vector.tensor_copy(counts[:, nxt, 0:step], counts[:, cur, 0:step]))
                elink(nc.vector.tensor_tensor(counts[:, nxt, step:E1], counts[:, cur, step:E1],
                                              counts[:, cur, 0:E1 - step], ALU.add))
                cur, step = nxt, 2 * step
            elink(nc.vector.tensor_tensor(counts[:, 4, :], counts[:, cur, :], counts[:, 1, :], ALU.subtract))
            elink(nc.vector.tensor_scalar(counts[:, 5, :], counts[:, 4, :], float(P), None, ALU.mult))
            elink(nc.vector.tensor_tensor(slot_g[:, :, :], T0[:, 0:NT * E1].rearrange("p (n e) -> p n e", e=E1),
                                          counts[:, 5, :].unsqueeze(1).to_broadcast([P, NT, E1]), ALU.add))
            elink(nc.vector.tensor_tensor(cmp[:, :, :], slot_g[:, :, :], mask12_all[:, :, 1, :], ALU.mult))
            elink(nc.vector.tensor_reduce(slots[:, 0, :], cmp[:, :, :], AX, ALU.add))
            elink(nc.vector.tensor_tensor(cmp[:, :, :], slot_g[:, :, :], mask12_all[:, :, 0, :], ALU.mult))
            elink(nc.vector.tensor_reduce(slots[:, 1, :], cmp[:, :, :], AX, ALU.add))
            elink(nc.vector.tensor_tensor(slots[:, 1, :], slots[:, 1, :], slots[:, 0, :], ALU.subtract))
            nc.vector.tensor_copy(slots_i[:, :, :], slots[:, :, :]).then_inc(s("e_slots"), 1)
            dve.wait_ge(s("zeroed"), 16 * 12)
            elink(nc.vector.tensor_tensor(cmp2[:, :, :], counts[:, cur, :].unsqueeze(1).to_broadcast([P, NSORT, E1]),
                                          cst("sorted").unsqueeze(2).to_broadcast([P, NSORT, E1]), ALU.is_le))
            elink(nc.vector.tensor_reduce(tile_e[:, :], cmp2[:, :, :], AX, ALU.add))
            elink(nc.vector.tensor_scalar(tile_e[:, :], tile_e[:, :], float(E1 - 1), None, ALU.min))
            nc.vector.tensor_copy(tile_ei[:, :], tile_e[:, :]).then_inc(s("e_tiles"), 1)
            with dve.Fori(0, NSORT // 2) as n:
                for r in range(2):
                    dve.wait_ge(s(f"f_silu{r}"), n + 1)
                    nc.vector.tensor_tensor(h_sb[:, r, 0:FF], h_sb[:, r, 0:FF], (S1, O1)[r][:, 0:FF], ALU.mult)\
                        .then_inc(s(f"f_h{r}"), 1)
                for r in range(2):
                    dve.wait_ge(s(f"f_y{r}"), n + 1)
                    dve.wait_ge(s(f"f_stored{r}"), 16 * n + 16)
                    nc.vector.tensor_copy(y_f[:, r, :], (M0, M1)[r][:, 256:256 + C]).then_inc(s(f"f_yc{r}"), 1)
            for n in range(NT):
                r = n % 2
                dve.wait_ge(s(f"g_got{r}"), 32 * (n // 2 + 1))
                nc.vector.scalar_tensor_tensor(x_all[:, n, :], xs[:, r, 0:C], w12_all[:, n, 0:1], x_all[:, n, :],
                                               ALU.mult, ALU.add).then_inc(s("g_link"), 1)
                dve.wait_ge(s("g_link"), n + 1)
                nc.vector.scalar_tensor_tensor(x_all[:, n, :], y_f[:, r, :], w12_all[:, n, 1:2], x_all[:, n, :],
                                               ALU.mult, ALU.add).then_inc(s("g_out"), 1)
                dve.wait_ge(s("g_out"), n + 1)
                nc.vector.tensor_copy(filled[:, r:r + 1], w12_all[:, n, 0:1]).then_inc(s(f"g_used{r}"), 1)

        @block.tensor
        def _(pe):
            pe.wait_ge(s("const_loaded"), 32)
            pe.wait_ge(s("wa_loaded"), 16 * 8)
            pe.wait_ge(s("set"), 1)
            with pe.Fori(0, B) as i:
                pe.wait_ge(s("a_xn"), i + 1)
                transpose_pair(pe, xn).then_inc(s("a_xT"), 1)
                pe.wait_ge(s("a_xTc"), 2 * i + 1)
                conv_qkv_pe(pe, NEIGH, wqkv, i)
                attention_pe(pe, NEIGH, i)
                project(pe, NEIGH, wproj, i)
                pe.wait_ge(s("a_tn"), i + 1)
                transpose_pair(pe, row0).then_inc(s("a_xT"), 1)
                pe.wait_ge(s("a_xTc"), 2 * i + 2)
                for t in range(2):
                    for k in range(KC):
                        ins = nc.tensor.matmul(M1[:, t * E0:(t + 1) * E0], xnT[:, k, t * P:(t + 1) * P], wg0[:, k, :],
                                               start=(k == 0), stop=(k == KC - 1))
                ins.then_inc(s("a_logits"), 1)
                for c in range(SC):
                    bank = (S0, S1, O0, O1)[c % 4]
                    if c >= 4:
                        pe.wait_ge(s("a_h"), SC * i + c - 3)
                    for half, w in ((0, wsg), (1, wsu)):
                        for k in range(KC):
                            ins = nc.tensor.matmul(bank[0:DP0, half * 256:(half + 1) * 256],
                                                   w[:, k, c * DP0:(c + 1) * DP0], xnT[:, k, :],
                                                   start=(k == 0), stop=(k == KC - 1))
                    ins.then_inc(s("a_gu"), 1)
                pe.wait_ge(s("a_mask"), i + 1)
                tri, ones = cstb("tri"), cstb("ones")
                nc.tensor.matmul(M1[:, 0:E0], tri, mask_b[:, 0, :], start=True, stop=False)
                nc.tensor.matmul(M1[:, 0:E0], ones, before0[:, :], start=False, stop=True)
                nc.tensor.matmul(M1[:, E0:2 * E0], tri, mask_b[:, 1, :], start=True, stop=False)
                nc.tensor.matmul(M1[:, E0:2 * E0], ones, mask_b[:, 0, :], start=False, stop=False)
                nc.tensor.matmul(M1[:, E0:2 * E0], ones, before0[:, :], start=False, stop=True)\
                    .then_inc(s("a_pos"), 1)
                pe.wait_ge(s("a_onehot"), i + 1)
                for j in range(NPAIR):
                    for t in range(2):
                        ins = nc.tensor.matmul(T1[:, 3 * j:3 * j + 3],
                                               onehot[t][:, 2 * j:2 * j + 2, :].rearrange("p a b -> p (a b)"),
                                               tokinfo[:, t, :], start=(t == 0), stop=(t == 1))
                ins.then_inc(s("a_ids"), 1)
                pe.wait_ge(s("a_h"), SC * i + SC)
                for t in range(2):
                    for c in range(SC):
                        ins = nc.tensor.matmul(M0[:, t * C:(t + 1) * C], hT[:, c, t * P:(t + 1) * P], wsd[:, c, :],
                                               start=(c == 0), stop=(c == SC - 1))
                ins.then_inc(s("a_shared"), 1)

            pe.wait_ge(s("a_done"), B)
            with pe.Fori(0, NPAIR // 2) as jj:
                for r in range(2):
                    pe.wait_ge(s(f"xs{r}"), 16 * jj + 16)
                    pe.wait_ge(s(f"b_yc{r}"), jj + 1)
                    for k in range(KC):
                        ins = nc.tensor.transpose((M0, M1)[r][0:KP, k * P:(k + 1) * P],
                                                  xs[:, r, 0:C].rearrange("p (f k) -> p k f", k=KC)[:, k, :], ident)
                    ins.then_inc(s(f"b_xT{r}"), 1)
                for r in range(2):
                    pe.wait_ge(s(f"ring{r}"), 32 * jj + 32)
                    pe.wait_ge(s(f"b_xTc{r}"), jj + 1)
                    for part, bank in enumerate(((S0, S1), (O0, O1))[r]):
                        for h in range(2):
                            for k in range(KC):
                                ins = nc.tensor.matmul(bank[h * SLOT:(h + 1) * SLOT, 0:I0],
                                                       xsT[:, r, k, h * SLOT:(h + 1) * SLOT],
                                                       ring_gu[r][:, h, k, part * I0:(part + 1) * I0],
                                                       start=(k == 0), stop=(k == KC - 1))
                    ins.then_inc(s(f"b_gu{r}"), 1)
                for r in range(2):
                    pe.wait_ge(s(f"b_h{r}"), jj + 1)
                    for c in range(DC0):
                        ins = nc.tensor.transpose(PT[r][0:DP0, c * P:(c + 1) * P],
                                                  h_sb[:, r, :].rearrange("p (f c) -> p c f", c=DC0)[:, c, :], ident)
                    ins.then_inc(s(f"b_hT{r}"), 1)
                for r in range(2):
                    pe.wait_ge(s(f"b_hTc{r}"), jj + 1)
                    for h in range(2):
                        for c in range(DC0):
                            ins = nc.tensor.matmul((M0, M1)[r][h * SLOT:(h + 1) * SLOT, 256:256 + C],
                                                   hTs[0:DP0, r, c * P + h * SLOT:c * P + (h + 1) * SLOT],
                                                   ring_dn[r][:, h, c, :], start=(c == 0), stop=(c == DC0 - 1))
                    ins.then_inc(s(f"b_y{r}"), 1)

            for r in range(2):
                pe.wait_ge(s(f"b_yc{r}"), NPAIR // 2 + 1)
            pe.wait_ge(s("wc_loaded"), 16 * 3)
            pe.wait_ge(s("wf_loaded"), 16 * 4)
            with pe.Fori(0, B) as i:
                for t in range(2):
                    pe.wait_ge(s("c_onehot"), 2 * i + t + 1)
                    for j in range(NPAIR):
                        for k in range(3):
                            ins = nc.tensor.matmul(M1[:, t * C:(t + 1) * C], comb_s[:, t, j, :], y0_all[:, j, k, :],
                                                   start=(j == 0 and k == 0), stop=(j == NPAIR - 1 and k == 2))
                ins.then_inc(s("c_comb"), 1)
                pe.wait_ge(s("c_xn"), 3 * i + 1)
                transpose_pair(pe, xn).then_inc(s("c_xT"), 1)
                pe.wait_ge(s("c_xTc"), 3 * i + 1)
                conv_qkv_pe(pe, WINDOW, wqkv, i)
                attention_pe(pe, WINDOW, i)
                project(pe, WINDOW, wproj, i)
                pe.wait_ge(s("c_xn"), 3 * i + 2)
                transpose_pair(pe, xn).then_inc(s("c_xT"), 1)
                pe.wait_ge(s("c_xTc"), 3 * i + 2)
                for t, bank in ((0, M1), (1, M0)):
                    for k in range(KC):
                        ins = nc.tensor.matmul(bank[:, 0:18 * HD], xnT[:, k, t * P:(t + 1) * P], wqkvf[:, k, :],
                                               start=(k == 0), stop=(k == KC - 1))
                    ins.then_inc(psem("qkv"), 1)
                attention_pe(pe, CAUSAL, i)
                project(pe, CAUSAL, wof, i)
                pe.wait_ge(s("c_xn"), 3 * i + 3)
                transpose_pair(pe, xn).then_inc(s("c_xT"), 1)
                pe.wait_ge(s("c_xTc"), 3 * i + 3)
                for t in range(2):
                    for k in range(KC):
                        ins = nc.tensor.matmul(M1[:, t * E1:(t + 1) * E1], xnT[:, k, t * P:(t + 1) * P], wr1[:, k, :],
                                               start=(k == 0), stop=(k == KC - 1))
                ins.then_inc(s("c_logits"), 1)
            if UPTO != "G":
                return
            pe.wait_ge(s("c_done"), B)
            tri, ones = cstb("tri"), cstb("ones")
            for n in range(NT):
                nc.tensor.matmul(T0[:, n * E1:(n + 1) * E1], tri, mask12_all[:, n, 0, :], start=True, stop=False)
                nc.tensor.matmul(T0[:, n * E1:(n + 1) * E1], ones, before_all[:, n, :], start=False, stop=True)
            nc.tensor.matmul(T1[:, 0:E1], ones, before_all[:, NT, :], start=True, stop=True).then_inc(s("e_pos"), 1)
            pe.wait_ge(s("e_tiles"), 1)
            pe.wait_ge(s("ffn1_loaded"), 16 * 3)
            with pe.Fori(0, NSORT // 2) as n:
                for r in range(2):
                    pe.wait_ge(s(f"f_loaded{r}"), 16 * n + 16)
                    pe.wait_ge(s(f"f_yc{r}"), n + 1)
                    for k in range(KC):
                        ins = nc.tensor.transpose((M0, M1)[r][0:KP, k * P:(k + 1) * P],
                                                  xs[:, r, 0:C].rearrange("p (f k) -> p k f", k=KC)[:, k, :], ident)
                    ins.then_inc(s(f"f_xT{r}"), 1)
                expert = []
                for r in range(2):
                    e = pe.value_load(tile_ei[0:1, bass.ds(2 * n + r, 1)], min_val=0, max_val=E1 - 1)
                    expert.append(e)
                    pe.wait_ge(s(f"f_xTc{r}"), n + 1)
                    for part, bank in enumerate(((S0, S1), (O0, O1))[r]):
                        for k in range(KC):
                            ins = nc.tensor.matmul(bank[:, 0:FF], xsT[:, r, k, :],
                                                   gu1_all[:, bass.ds(e, 1), k, part * FF:(part + 1) * FF]
                                                   .rearrange("p a f -> p (a f)"),
                                                   start=(k == 0), stop=(k == KC - 1))
                    ins.then_inc(s(f"f_gu{r}"), 1)
                for r in range(2):
                    pe.wait_ge(s(f"f_h{r}"), n + 1)
                    for c in range(DC1):
                        ins = nc.tensor.transpose(PT[r][:, c * P:(c + 1) * P],
                                                  h_sb[:, r, 0:FF].rearrange("p (f c) -> p c f", c=DC1)[:, c, :], ident)
                    ins.then_inc(s(f"f_hT{r}"), 1)
                for r in range(2):
                    pe.wait_ge(s(f"f_hTc{r}"), n + 1)
                    for c in range(DC1):
                        ins = nc.tensor.matmul((M0, M1)[r][:, 256:256 + C], hTs[:, r, c * P:(c + 1) * P],
                                               dn1_all[:, bass.ds(expert[r], 1), c, :].rearrange("p a f -> p (a f)"),
                                               start=(c == 0), stop=(c == DC1 - 1))
                    ins.then_inc(s(f"f_y{r}"), 1)


SHAPES = {"x": (TOK, C), "cf": (P, NCF), "cb": (P, NCB), "L0_conv_w_qkv": (C, 3 * C), "L0_conv_w_proj": (C, C),
          "brow0": (P, 4 * C), "L0_ffn_Wg": (C, E0), "ebias": (P, E0), "L0_ffn_Wsg": (C, IS0), "L0_ffn_Wsu": (C, IS0),
          "L0_ffn_Wsd": (IS0, C), "L0_ffn_W_gate_up": (E0, C, 2 * I0), "L0_ffn_W_down": (E0, I0, C),
          "L1_conv_w": (C, 3 * C), "L1_conv_Wo": (C, C), "brow1": (P, 4 * C), "L1_ffn_w_qkv": (C, 18 * HD),
          "L1_ffn_w_out": (C, C), "norm_w": (P, 2 * C), "L1_ffn_w_router": (C, E1),
          "L1_ffn_w_gate_up": (E1, C, 2 * FF), "L1_ffn_w_down": (E1, FF, C)}


def kernel(**inputs):
    import concourse.bacc as _bacc
    from concourse import mybir as _mybir
    from concourse.bass_utils import run_bass_kernel_spmd as _run

    a = {k: np.asarray(v) for k, v in inputs.items()}
    cf, cb = constants()

    def rows(*vs):
        return np.ascontiguousarray(np.broadcast_to(np.concatenate(vs)[None], (P, sum(len(v) for v in vs))))

    even_odd = np.concatenate([np.arange(0, HD, 2), np.arange(1, HD, 2)])
    order = [(kv * REP + r) * HD + even_odd for r in range(REP) for kv in range(NKV)]
    order += [(NH + kv) * HD + even_odd for kv in range(NKV)]
    order += [np.arange((NH + NKV) * HD, (NH + 2 * NKV) * HD)]
    conv = [part * C + (slot * REP + r) * HD + np.arange(HD) for part in range(2) for r in range(REP) for slot in range(3)]
    conv = np.concatenate(conv + [np.arange(2 * C, 3 * C)])
    data = {
        "x": a["x"].reshape(TOK, C), "cf": cf, "cb": cb,
        "L0_conv_w_qkv": a["L0_conv_w_qkv"].T[:, conv], "L0_conv_w_proj": a["L0_conv_w_proj"].T,
        "brow0": rows(a["L0_conv_b_qkv"][conv], a["L0_conv_b_proj"]), "L0_ffn_Wg": a["L0_ffn_Wg"].T,
        "ebias": rows(a["L0_ffn_e_bias"]), "L0_ffn_Wsg": a["L0_ffn_Wsg"], "L0_ffn_Wsu": a["L0_ffn_Wsu"],
        "L0_ffn_Wsd": a["L0_ffn_Wsd"], "L0_ffn_W_gate_up": a["L0_ffn_W_gate_up"], "L0_ffn_W_down": a["L0_ffn_W_down"],
        "L1_conv_w": np.concatenate([a["L1_conv_Wq"], a["L1_conv_Wk"], a["L1_conv_Wv"]], 1)[:, conv],
        "L1_conv_Wo": a["L1_conv_Wo"],
        "brow1": rows(np.concatenate([a["L1_conv_bq"], a["L1_conv_bk"], a["L1_conv_bv"]])[conv], a["L1_conv_bo"]),
        "L1_ffn_w_qkv": a["L1_ffn_w_qkv"][:, np.concatenate(order)], "L1_ffn_w_out": a["L1_ffn_w_out"],
        "norm_w": rows(a["L1_ffn_norm1_w"], a["L1_ffn_norm2_w"]), "L1_ffn_w_router": a["L1_ffn_w_router"],
        "L1_ffn_w_gate_up": a["L1_ffn_w_gate_up"], "L1_ffn_w_down": a["L1_ffn_w_down"],
    }
    nc = _bacc.Bacc("TRN2", target_bir_lowering=False, num_devices=1)
    arrays, d = {}, {}
    for name, shape in SHAPES.items():
        v = np.ascontiguousarray(data[name])
        assert v.shape == shape, (name, v.shape)
        arrays[f"in_{name}"] = v
        d[name] = nc.dram_tensor(f"in_{name}", v.shape, _mybir.dt.from_np(v.dtype), kind="ExternalInput").ap()
    out = nc.dram_tensor("out_x", (TOK, C), F32, kind="ExternalOutput").ap()
    build(nc, d, out)
    r = _run(nc, [arrays], core_ids=[0])
    return r.results[0]["out_x"].reshape(B, IMG, IMG, C)
```

```python
from contextlib import ExitStack

import numpy as np

import concourse.bass as bass
from concourse import mybir

P = 128
B, IMG, C = 8, 16, 192
NT = B * IMG * IMG // P
TOK = NT * P
NH, HD = 12, 16
WIN = 7
KC, KP = 2, C // 2
E0, I0, IS0, TOP0, CAP = 32, 464, 928, 6, 48
SLOT = 64
NPAIR = E0 // 2
DC0 = 4
DP0 = I0 // DC0
SC = IS0 // DP0
E1, FF, NKV = 16, 384, 3
REP = NH // NKV
DC1 = FF // P
NSORT = 2 * TOK // P + E1
KW0 = 11 * IMG
BIG = 3.0e38
NEG = -1.0e30
RING = 2

F32 = mybir.dt.float32
BF16 = mybir.dt.bfloat16
I32 = mybir.dt.int32
U32 = mybir.dt.uint32
ALU = mybir.AluOpType
ACT = mybir.ActivationFunctionType
AX = mybir.AxisListType.X

CF = {}
CB = {}


def _lay(table, items):
    at = 0
    for name, n in items:
        table[name] = (at, n)
        at += n
    return at


NCF = _lay(CF, [("ident", P), ("iota_slot", CAP), ("iota_tok", P), ("cos", 2 * HD), ("sin", 2 * HD),
                ("pick", E0), ("tiles", 16), ("sorted", NSORT), ("half", 2), ("neg", 10), ("back", 1)])
NCB = _lay(CB, [("identb", P), ("tri", P), ("ones", P), ("mask_n", 4 * KW0), ("mask_w", 512),
                ("mask_c0", 512), ("mask_c1", 512), ("tokinfo", 6)])


def constants():
    f = np.zeros((P, NCF), np.float32)
    b = np.zeros((P, NCB), np.float32)
    p = np.arange(P)

    def put(arr, table, name, val):
        at, n = table[name]
        arr[:, at:at + n] = np.asarray(val, np.float32).reshape(P, n) if np.ndim(val) > 1 else val
    put(f, CF, "ident", np.eye(P))
    put(f, CF, "iota_slot", np.arange(CAP))
    put(f, CF, "iota_tok", np.arange(P))
    s = np.arange(2)[None, :, None] * P + p[:, None, None]
    inv = (1.0 / np.float32(10000.0) ** (np.arange(0, HD, 2, dtype=np.float32) / HD)).astype(np.float32)
    ang = (s.astype(np.float32) * inv[None, None, :]).astype(np.float32)
    put(f, CF, "cos", np.concatenate([np.cos(ang), np.cos(ang)], 2).reshape(P, -1))
    put(f, CF, "sin", np.concatenate([np.sin(ang), np.sin(ang)], 2).reshape(P, -1))
    put(f, CF, "tiles", np.arange(16) * P)
    put(f, CF, "sorted", np.arange(NSORT))
    put(f, CF, "half", np.stack([p < SLOT, p >= SLOT], 1))
    put(f, CF, "neg", np.repeat([-0.5, 1.0, 1.0 / C, 1e-6, 1e-5], 2))
    put(f, CF, "back", -P)
    put(b, CB, "identb", np.eye(P))
    put(b, CB, "tri", (p[:, None] < p[None, :]))
    put(b, CB, "ones", 1.0)
    start = np.clip(np.arange(IMG) - WIN // 2, 0, IMG - WIN)
    m = np.zeros((P, 2, 2, KW0))
    for t, k0 in ((0, 0), (1, 2 * P - KW0)):
        q, k = t * P + p, k0 + np.arange(KW0)
        qr, qc, kr, kc = q // IMG, q % IMG, k // IMG, k % IMG
        seen = ((kr[None] >= start[qr][:, None]) & (kr[None] < start[qr][:, None] + WIN)
                & (kc[None] >= start[qc][:, None]) & (kc[None] < start[qc][:, None] + WIN))
        m[:, t] = np.where(seen, 0.0, NEG)[:, None, :]
    put(b, CB, "mask_n", m.reshape(P, -1))
    w = np.where(p[:, None] // IMG == p[None] // IMG, 0.0, NEG)
    put(b, CB, "mask_w", np.tile(w, (1, 4)))
    c0 = np.where(p[:, None] >= p[None], 0.0, NEG)
    put(b, CB, "mask_c0", np.tile(c0, (1, 4)))
    k2 = np.arange(2 * P)
    put(b, CB, "mask_c1", np.tile(np.where(P + p[:, None] >= k2[None], 0.0, NEG), (1, 2)))
    put(b, CB, "tokinfo", np.stack([np.zeros(P), p, np.ones(P), np.ones(P), p, np.ones(P)], 1))
    return f, b


ONE, PER_C, EPS6, EPS5 = 2, 4, 6, 8


class Attention:

    def __init__(self, name, kinds, dve_links):
        self.name = name
        self.groups = []
        self.last_of_tile = {}
        for t, width, k0, kw, pieces, mask in kinds:
            for h0 in range(0, NH, width):
                self.groups.append((t, list(range(h0, h0 + width)), k0, kw, pieces, mask))
            self.last_of_tile[t] = len(self.groups) - 1
        self.n = len(self.groups)
        self.by_dve = (self.n + 1) // 2
        self.by_act = self.n // 2


NEIGH = Attention("n", [(0, 2, 0, KW0, [(0, P, 0), (P, KW0 - P, 1)], ("mask_n", 0)),
                        (1, 2, 2 * P - KW0, KW0, [(0, KW0 - P, 2), (KW0 - P, P, 1)], ("mask_n", 2 * KW0))], 0)
WINDOW = Attention("w", [(0, 4, 0, P, [(0, P, 0)], ("mask_w", 0)),
                         (1, 4, P, P, [(0, P, 1)], ("mask_w", 0))], 0)
CAUSAL = Attention("c", [(0, 4, 0, P, [(0, P, 0)], ("mask_c0", 0)),
                         (1, 2, 0, 2 * P, [(0, P, 0), (P, P, 1)], ("mask_c1", 0))], 0)

LINKS = {"A": 32, "B": 5, "C": 54}
UPTO = "G"


def build(nc, d, out):
    ctx = ExitStack()
    with ctx:
        def sb(name, shape, dt=F32):
            return ctx.enter_context(nc.sbuf_tensor(name, shape, dt))

        def sem(name):
            return ctx.enter_context(nc.semaphore(name))

        cf = sb("cf", [P, NCF])
        cb = sb("cb", [P, NCB], BF16)

        def cst(name):
            at, n = CF[name]
            return cf[:, at:at + n]

        def cstb(name, off=0, n=None):
            at, m = CB[name]
            return cb[:, at + off:at + off + (n if n is not None else m - off)]

        ident = cst("ident")

        x_all = sb("x_all", [P, NT, C])
        m_all = sb("m_all", [P, NT, C])
        mask12_all = sb("mask12_all", [P, NT, 2, E1], BF16)
        before_all = sb("before_all", [P, NT + 1, E1], BF16)
        w12_all = sb("w12_all", [P, NT, 2])

        wqkv = sb("wqkv", [KP, KC, 3 * C])
        wproj = sb("wproj", [KP, KC, C])
        brow = sb("brow", [P, 4 * C])
        wg0 = sb("wg0", [KP, KC, E0])
        ebias = sb("ebias", [P, E0])
        wqkvf = sb("wqkvf", [KP, KC, (NH + 2 * NKV) * HD])
        wof = sb("wof", [KP, KC, C])
        norm_w = sb("norm_w", [P, 2, C])
        wr1 = sb("wr1", [KP, KC, E1])

        GU0 = KC * 2 * I0
        DN0 = DC0 * C
        GU1 = KC * 2 * FF
        DN1 = DC1 * C
        R = sb("R", [P, E1 * (GU1 + DN1)])
        gu1_all = R[0:KP, 0:E1 * GU1].rearrange("p (e k f) -> p e k f", e=E1, k=KC)
        dn1_all = R[:, E1 * GU1:E1 * (GU1 + DN1)].rearrange("p (e c f) -> p e c f", e=E1, c=DC1)
        low, high = [0], [E1 * (GU1 + DN1)]

        def carve(words, at_end):
            if at_end:
                high[0] -= words
                start = high[0]
            else:
                start = low[0]
                low[0] += words
            assert low[0] <= high[0], (low, high)
            return R[:, start:start + words]

        ring_gu = [carve(2 * GU0, False)[0:KP, :].rearrange("p (h k f) -> p h k f", h=2, k=KC) for _ in range(RING)]
        ring_dn = [carve(2 * DN0, False)[0:DP0, :].rearrange("p (h c f) -> p h c f", h=2, c=DC0) for _ in range(RING)]
        rows_at = low[0]
        wsg = carve(KC * IS0, False)[0:KP, :].rearrange("p (k f) -> p k f", k=KC)
        wsu = carve(KC * IS0, False)[0:KP, :].rearrange("p (k f) -> p k f", k=KC)
        wsd = carve(SC * C, False)[0:DP0, :].rearrange("p (c f) -> p c f", c=SC)
        ROW = C + E0
        assert rows_at + NPAIR * ROW + 2 * NPAIR <= low[0]
        slot_rows = R[:, rows_at:rows_at + NPAIR * ROW].rearrange("p (j c) -> p j c", j=NPAIR)
        pair_w = R[:, rows_at + C:rows_at + C + NPAIR * (ROW + 2)].rearrange("p (j c) -> p j c", j=NPAIR)[:, :, 0:2]

        xn = carve(2 * C, True).rearrange("p (t c) -> p t c", t=2)
        xnT = carve(KC * 2 * P, True)[0:KP, :].rearrange("p (k t) -> p k t", k=KC)
        qk_parts = carve(4 * NH * P // 2, True).bitcast(BF16).rearrange("p (r s e) -> p r s e", s=8, e=HD)
        qkT = carve(2 * NH * P, True).bitcast(BF16).rearrange("p (h t) -> p h t", h=2 * NH)
        v_sb = carve(3 * NH * (HD + 1), True).rearrange("p (v h e) -> p v h e", v=3, h=NH)
        probs = carve(3 * 512, True).rearrange("p (b k) -> p b k", b=3)
        probsT = carve(2 * 512, True).rearrange("p (b k) -> p b k", b=2)
        o_sb = carve(2 * C, True).rearrange("p (t c) -> p t c", t=2)
        row0 = carve(2 * (C + E0), True).rearrange("p (t c) -> p t c", t=2)
        y0_words = carve(NPAIR * 3 * C // 2, True)
        y0_all = y0_words.bitcast(BF16).rearrange("p (j s c) -> p j s c", j=NPAIR, s=3)
        onehot = [y0_words[:, t * E0 * SLOT // 2:(t + 1) * E0 * SLOT // 2].bitcast(BF16)
                  .rearrange("p (e s) -> p e s", e=E0) for t in range(2)]
        hT_words = carve(SC * 2 * P, True)
        hT = hT_words[0:DP0, :].rearrange("p (c t) -> p c t", c=SC)
        comb_s = hT_words.bitcast(BF16).rearrange("p (t j k) -> p t j k", t=2, j=NPAIR)

        neg_max = sb("neg_max", [P, 4, 4])
        rden = sb("rden", [P, 2, NH])
        stats = sb("stats", [P, 2, 6])
        mean_var = sb("mean_var", [P, 2, 2])
        rstd = sb("rstd", [P, 2])
        sumsq = sb("sumsq", [P, 2])
        expl = sb("expl", [P, 2, E0])
        sig = sb("sig", [P, 2, E0])
        choice = sb("choice", [P, 2, 2, E0 + 8])
        top8 = sb("top8", [P, 2, 2, 8])
        left = sb("left", [P, 2, 2, E0 + 8])
        mask = sb("mask", [P, 2, E0])
        mask_b = sb("mask_b", [P, 2, E0], BF16)
        before0 = sb("before0", [P, E0], BF16)
        tokinfo = sb("tokinfo", [P, 2, 3], BF16)
        wsum = sb("wsum", [P, 2, 2])
        pos = sb("pos", [P, 2, E0])
        ids_acc = sb("ids_acc", [P, NPAIR, 3])
        ids_f = sb("ids_f", [P, NPAIR])
        ids_i = sb("ids_i", [P, NPAIR], I32)
        ids_rel = sb("ids_rel", [P, NPAIR])
        scratch = sb("scratch", [P, 16])
        filled = sb("filled", [P, 2])
        h_words = sb("h_words", [P, 2 * I0])
        h_sb = h_words[:, :].rearrange("p (r f) -> p r f", r=2)
        tmp = h_words[:, 0:2 * C].rearrange("p (t c) -> p t c", t=2)
        u_sb = h_words[:, 2 * C:4 * C].rearrange("p (t c) -> p t c", t=2)
        hTs_words = sb("hTs_words", [P, 2 * 4 * P])
        hTs = hTs_words[:, :].rearrange("p (r t) -> p r t", r=2)
        qk = hTs_words[:, 0:4 * NH * HD].rearrange("p (r e) -> p r e", e=HD)
        xs_words = sb("xs_words", [P, 2 * C])
        xs = xs_words[:, :].rearrange("p (r c) -> p r c", r=2)
        rope_c = xs_words[:, 0:15 * HD].rearrange("p (h e) -> p h e", e=HD)
        rope_s = sb("rope_s", [P, 15, HD])[:, :, :]
        v_causal = sb("v_causal", [P, 2, NKV, HD + 1])
        xsT = sb("xsT", [KP, 2, KC, P])
        wslot = sb("wslot", [P, NPAIR, 2])
        wsl = sb("wsl", [P, NPAIR])
        y_f = sb("y_f", [P, 2, C])
        counts = sb("counts", [P, 6, E1])
        cmp = sb("cmp", [P, E1, 16])
        cmp2 = sb("cmp2", [P, NSORT, E1])
        slot_g = sb("slot_g", [P, NT, E1])
        slots = sb("slots", [P, 2, NT])
        slots_i = sb("slots_i", [P, 2, NT], I32)
        tile_e = sb("tile_e", [P, NSORT])
        tile_ei = sb("tile_ei", [P, NSORT], I32)

        BK = [ctx.enter_context(nc.psum_tensor(f"bank{j}", [P, 512], F32)) for j in range(8)]
        S0, S1, T0, T1, O0, O1, M0, M1 = BK
        SCORE, PT, OB = [S0, S1, M0, M1], [T0, T1], [O0, O1]

        GATE = [T0, T1, O0, O1, S0, S1]

        def gate_act(c):
            return probs[0:DP0, (c % 6) // 2, (c % 2) * 256:(c % 2) * 256 + 256]

        rows0 = nc.dram_tensor("rows0", [TOK, C + E0], F32)
        sorted_x = nc.dram_tensor("sorted_x", [NSORT * P, C], F32)
        sorted_y = nc.dram_tensor("sorted_y", [NSORT * P, C], F32)
        rows0_t = rows0[:, :].rearrange("(i t p) c -> i p t c", t=2, p=P)

        S = {}

        def s(name):
            if name not in S:
                S[name] = sem(name)
            return S[name]

        def per_image(a, name):
            return {"scores": a.n, "max": a.n, "exp": a.n, "pt": a.n, "pv": a.n, "pta": a.by_act, "ptd": a.by_dve,
                    "read": 2, "norm": 2, "qkT": 4 if a is CAUSAL else 6, "qkTa": 3,
                    "qkTd": 1 if a is CAUSAL else 3, "qkv": 2 if a is CAUSAL else 3,
                    "v": 0 if a is CAUSAL else 1}.get(name, 1)

        def psem(name):
            return s(f"att_{name}")

        def count(a, name, i, k):
            if a is NEIGH:
                return i * per_image(a, name) + k
            turn = per_image(WINDOW, name) + per_image(CAUSAL, name)
            before = B * per_image(NEIGH, name) + (per_image(WINDOW, name) if a is CAUSAL else 0)
            return i * turn + (before + k)

        def await_(eng, a, name, i, k):
            eng.wait_ge(psem(name), count(a, name, i, k))

        for n in ("const_loaded", "x_loaded", "wa_loaded", "wc_loaded", "wf_loaded", "ffn1_loaded", "row_stored", "set",
                  "a_var", "a_rstd", "a_xn", "a_tn", "a_xT", "a_xTc", "a_logits", "a_expl", "a_mask", "a_pos",
                  "a_onehot", "a_ids", "a_gu", "a_silu", "a_h", "a_shared", "a_row", "a_link", "a_pool", "a_done",
                  "b_idf", "b_x", "b_rows_first", "b_rows_rest", "b_weights", "b_link", "b_done",
                  "c_onehot", "c_comb", "c_link", "c_var", "c_u", "c_ss", "c_rstd", "c_xn", "c_xT", "c_xTc",
                  "c_mr", "a_tT", "a_tTc", "b_xT", "b_xTc", "b_y", "b_yc", "f_xT", "f_xTc", "f_y", "f_yc", "f_stored",
                  "c_logits", "c_negmax", "c_expl", "c_pool", "c_m", "c_done", "c_sq",
                  "e_pos", "e_link", "e_slots", "e_tiles", "scattered", "zeroed", "g_link", "g_out", "stored"):
            s(n)
        for r in range(2):
            for n in ("ring_gu", "ring_dn", "b_gu", "b_silu", "b_h", "b_hT", "b_hTc",
                      "f_loaded", "f_gu", "f_silu", "f_h", "f_hT", "f_hTc", "g_got", "g_used"):
                s(f"{n}{r}")
        for n in ("qkv", "read", "parts", "v", "qkT", "qkTa", "qkTd", "scores", "max", "exp", "pt", "pta", "ptd", "pv",
                  "norm", "oT", "oTc", "proj"):
            psem(n)

        block = ctx.enter_context(nc.Block())

        def settle():
            nc.vector.memset(scratch[:, 0:1], 0.0)

        class Links:

            def __init__(self, eng, sm, i, per):
                self.eng, self.sm, self.base, self.k, self.per = eng, sm, i * per, 0, per

            def inc(self, ins):
                self.k += 1
                ins.then_inc(self.sm, 1)

            def __call__(self, ins):
                self.inc(ins)
                self.eng.wait_ge(self.sm, self.base + self.k)

            def end(self):
                assert self.k == self.per, (self.sm, self.k)

        def qk_rows(a, t):
            nk = NKV if a is CAUSAL else NH
            return t * NH, 2 * NH + t * nk, nk

        def q_ap(h, t):
            return qkT[:, h, t * P:(t + 1) * P]

        def k_ap(a, h, k0, kw):
            return qkT[:, NH + (h // REP if a is CAUSAL else h), k0:k0 + kw]

        def v_ap(a, h, n, vt):
            return v_causal[0:n, vt, h // REP, :] if a is CAUSAL else v_sb[0:n, vt, h, :]

        def head_groups(a):
            q = [(False, h, 4, (S0, S1)[n % 2]) for n, h in enumerate(range(0, NH, 4))]
            k = [(True, NH, NKV, T0)] if a is CAUSAL else \
                [(True, NH + h, 4, (T0, T1)[n % 2]) for n, h in enumerate(range(0, NH, 4))]
            order = []
            while q or k:
                order += q[:1] + k[:1]
                q, k = q[1:], k[1:]
            return order

        def run(steps):
            for step in steps:
                step()

        def split_qk(a, i, link):
            nq, nk = 2 * NH, 2 * qk_rows(a, 0)[2]
            f = qk[:, 0:nq + nk, :]

            def part(side, at, n=1, step=1):
                r0, rows = ((0, nq), (nq, nk), (0, nq + nk))[side]
                return qk_parts[:, r0:r0 + rows, at:at + (n - 1) * step + 1:step, :]

            def one(side, at):
                return part(side, at).rearrange("p r s e -> p r (s e)")

            def first():
                await_(nc.vector, a, "read", i, 2)
                if a is WINDOW and not isinstance(i, int):
                    await_(nc.vector, CAUSAL, "qkT", i - 1, per_image(CAUSAL, "qkT"))
                link(nc.vector.tensor_copy(one(2, 0), f))

            def last():
                link.inc(nc.vector.tensor_tensor(one(0, 5), f[:, 0:nq], one(0, 1), ALU.subtract))
                link(nc.vector.tensor_tensor(one(1, 4), f[:, nq:nq + nk], one(1, 1), ALU.subtract))

            def places_q():
                nc.vector.tensor_copy(part(0, 2, 2), part(0, 0, 2))
                nc.vector.tensor_copy(part(0, 4, 2, 2), part(0, 0, 2))
                nc.vector.tensor_copy(one(0, 7), one(0, 5))

            def places_k():
                nc.vector.tensor_copy(part(1, 3, 2, 2), part(1, 0).to_broadcast([P, nk, 2, HD]))
                nc.vector.tensor_copy(part(1, 2, 2, 5), part(1, 1).to_broadcast([P, nk, 2, HD]))
                nc.vector.tensor_copy(one(1, 6), one(1, 4)).then_inc(psem("parts"), 1)
            return [first,
                    lambda: link(nc.vector.tensor_tensor(f, f, one(2, 0), ALU.subtract)),
                    lambda: link(nc.vector.tensor_copy(one(2, 1), f)),
                    last, places_q, places_k]

        def transpose_qk(pe, a, i):
            await_(pe, a, "parts", i, 1)
            done = {False: 0, True: 0}
            for is_k, h0, heads, bank in head_groups(a):
                if done[is_k] >= 2:
                    await_(pe, a, "qkTd" if is_k else "qkTa", i, done[is_k] - 1)
                done[is_k] += 1
                for h in range(heads):
                    for t in range(2):
                        q0, k0, _ = qk_rows(a, t)
                        row = k0 + h0 - NH + h if is_k else q0 + h0 + h
                        ins = nc.tensor.transpose(bank[:, :].bitcast(BF16)[:, (h * 2 + t) * P:(h * 2 + t + 1) * P],
                                                  qk_parts[:, row, :, :].rearrange("p s e -> p (s e)"), cstb("identb"))
                ins.then_inc(psem("qkT"), 1)

        def attention_pe(pe, a, i, routed=None):
            await_(pe, a, "qkTa", i, per_image(a, "qkTa"))
            await_(pe, a, "qkTd", i, per_image(a, "qkTd"))

            def scores(u):
                t, heads, k0, kw, _, (mname, moff) = a.groups[u]
                if u >= 4:
                    await_(pe, a, "exp", i, u - 3)
                if u == 2 and a is NEIGH:
                    pe.wait_ge(s("a_done"), i + 1)
                if u == 3 and routed is not None:
                    pe.wait_ge(s("c_expl"), routed)
                bank = SCORE[u % 4]
                nc.tensor.matmul(bank[:, 0:len(heads) * kw], cstb("identb"), cstb(mname, moff, len(heads) * kw),
                                 start=True, stop=False)
                for g, h in enumerate(heads):
                    ins = nc.tensor.matmul(bank[:, g * kw:(g + 1) * kw], q_ap(h, t), k_ap(a, h, k0, kw),
                                           start=False, stop=(g == len(heads) - 1))
                ins.then_inc(psem("scores"), 1)

            def transposes(u):
                t, heads, k0, kw, pieces, _ = a.groups[u]
                await_(pe, a, "exp", i, u + 1)
                if u >= 2:
                    if u % 2 == 0:
                        await_(pe, a, "ptd", i, u // 2)
                    else:
                        await_(pe, a, "pta", i, u // 2)
                for c, (c0, n, _) in sorted(enumerate(pieces), key=lambda e: -e[1][1]):
                    for g in range(len(heads)):
                        col = (c * len(heads) + g) * P
                        ins = nc.tensor.transpose(PT[u % 2][0:n, col:col + P],
                                                  probs[:, u % 3, g * kw + c0:g * kw + c0 + n], ident)
                ins.then_inc(psem("pt"), 1)

            def pv(u):
                t, heads, k0, kw, pieces, _ = a.groups[u]
                if u == 0 and a is not CAUSAL:
                    await_(pe, a, "v", i, 1)
                if u % 2 == 0:
                    await_(pe, a, "ptd", i, u // 2 + 1)
                else:
                    await_(pe, a, "pta", i, u // 2 + 1)
                for g, h in enumerate(heads):
                    for c, (c0, n, vt) in enumerate(pieces):
                        col = (c * len(heads) + g) * P
                        ins = nc.tensor.matmul(OB[t][:, h * (HD + 1):(h + 1) * (HD + 1)],
                                               probsT[0:n, u % 2, col:col + P], v_ap(a, h, n, vt),
                                               start=(c == 0), stop=(c == len(pieces) - 1))
                ins.then_inc(psem("pv"), 1)

            for u in range(a.n + 3):
                if u < a.n:
                    scores(u)
                if 2 <= u < a.n + 2:
                    transposes(u - 2)
                if u >= 3:
                    pv(u - 3)
            for t in range(2):
                await_(pe, a, "norm", i, t + 1)
                for k in range(KC):
                    ins = nc.tensor.transpose(M0[0:KP, k * 256 + t * P:k * 256 + (t + 1) * P],
                                              o_sb[:, t, :].rearrange("p (f k) -> p k f", k=KC)[:, k, :], ident)
            ins.then_inc(psem("oT"), 1)

        def project(pe, a, w, i):
            await_(pe, a, "oTc", i, 1)
            for t in range(2):
                for k in range(KC):
                    ins = nc.tensor.matmul(M1[:, t * C:(t + 1) * C], xnT[:, k, t * P:(t + 1) * P], w[:, k, :],
                                           start=(k == 0), stop=(k == KC - 1))
            ins.then_inc(psem("proj"), 1)

        def attention_dve(dve, a, i, link, between={}):
            def copy_pt(u):
                _, heads, _, _, pieces, _ = a.groups[u]
                await_(dve, a, "pt", i, u + 1)
                if u >= 2:
                    await_(dve, a, "pv", i, u - 1)
                w = len(heads) * P
                for c, (_, n, _) in enumerate(pieces):
                    ins = nc.vector.tensor_copy(probsT[0:n, u % 2, c * w:(c + 1) * w], PT[u % 2][0:n, c * w:(c + 1) * w])
                ins.then_inc(psem("ptd"), 1)

            def normalise(t):
                await_(dve, a, "pv", i, a.last_of_tile[t] + 1)
                ov = OB[t][:, 0:NH * (HD + 1)].rearrange("p (h e) -> p h e", e=HD + 1)
                link(nc.vector.reciprocal(rden[:, t, :], ov[:, :, HD]))
                nc.vector.tensor_tensor(o_sb[:, t, :].rearrange("p (h e) -> p h e", e=HD), ov[:, :, 0:HD],
                                        rden[:, t, :].unsqueeze(2).to_broadcast([P, NH, HD]), ALU.mult)\
                    .then_inc(psem("norm"), 1)

            for u in range(a.n + 4):
                if u < a.n:
                    _, heads, _, kw, _, _ = a.groups[u]
                    await_(dve, a, "scores", i, u + 1)
                    g = len(heads)
                    nc.vector.tensor_reduce(neg_max[:, u % 4, 0:g],
                                            SCORE[u % 4][:, 0:g * kw].rearrange("p (g k) -> p g k", g=g),
                                            AX, ALU.max, negate=True).then_inc(psem("max"), 1)
                if 2 <= u < a.n + 2 and u % 2 == 0:
                    copy_pt(u - 2)
                if u in between:
                    between[u]()
                for t in range(2):
                    if u - 4 == a.last_of_tile[t]:
                        normalise(t)

        def attention_act(act, a, i):
            for u in range(a.n + 2):
                if u < a.n:
                    _, heads, _, kw, _, _ = a.groups[u]
                    await_(act, a, "max", i, u + 1)
                    if u >= 3:
                        await_(act, a, "pt", i, u - 2)
                    for g in range(len(heads)):
                        ins = nc.scalar.activation(probs[:, u % 3, g * kw:(g + 1) * kw],
                                                   SCORE[u % 4][:, g * kw:(g + 1) * kw], ACT.Exp,
                                                   bias=neg_max[:, u % 4, g:g + 1])
                    ins.then_inc(psem("exp"), 1)
                if u >= 2 and u % 2 == 1:
                    v = u - 2
                    _, heads, _, _, pieces, _ = a.groups[v]
                    await_(act, a, "pt", i, v + 1)
                    if v >= 2:
                        await_(act, a, "pv", i, v - 1)
                    w = len(heads) * P
                    for c, (_, n, _) in enumerate(pieces):
                        ins = nc.scalar.activation(probsT[0:n, v % 2, c * w:(c + 1) * w], PT[v % 2][0:n, c * w:(c + 1) * w],
                                                   ACT.Copy)
                    ins.then_inc(psem("pta"), 1)
            await_(act, a, "oT", i, 1)
            nc.scalar.activation(xnT[:, :, :], M0[0:KP, :].rearrange("p (k t) -> p k t", k=KC), ACT.Copy)\
                .then_inc(psem("oTc"), 1)

        def qk_copies_act(act, a, i):
            for n, (is_k, h0, heads, bank) in enumerate(head_groups(a)):
                if not is_k:
                    await_(act, a, "qkT", i, n + 1)
                    nc.scalar.activation(qkT[:, h0:h0 + heads, :].rearrange("p h t -> p (h t)"),
                                         bank[:, :].bitcast(BF16)[:, 0:heads * 256], ACT.Copy,
                                         scale=float(HD) ** -0.5).then_inc(psem("qkTa"), 1)

        def qk_copies_dve(dve, a, i):
            for n, (is_k, h0, heads, bank) in enumerate(head_groups(a)):
                if is_k:
                    await_(dve, a, "qkT", i, n + 1)
                    nc.vector.tensor_copy(qkT[:, h0:h0 + heads, :].rearrange("p h t -> p (h t)"),
                                          bank[:, :].bitcast(BF16)[:, 0:heads * 256]).then_inc(psem("qkTd"), 1)

        def transpose_pair(pe, src):
            for t in range(2):
                for k in range(KC):
                    ins = nc.tensor.transpose(M0[0:KP, k * 256 + t * P:k * 256 + (t + 1) * P],
                                              src[:, t, 0:C].rearrange("p (f k) -> p k f", k=KC)[:, k, :], ident)
            return ins

        def copy_pair(dst):
            return nc.scalar.activation(dst[:, :, :], M0[0:KP, :].rearrange("p (k t) -> p k t", k=KC), ACT.Copy)

        def qk_banks(a):
            return enumerate((S0, S1) if a is NEIGH else (T1, M1))

        def conv_qkv_pe(pe, a, w, i):
            for t, bank in qk_banks(a):
                for k in range(KC):
                    ins = nc.tensor.matmul(bank[:, 0:2 * C], xnT[:, k, t * P:(t + 1) * P], w[:, k, 0:2 * C],
                                           start=(k == 0), stop=(k == KC - 1))
                ins.then_inc(psem("qkv"), 1)
            for t in range(2):
                for k in range(KC):
                    ins = nc.tensor.matmul(OB[t][:, 0:C], xnT[:, k, t * P:(t + 1) * P], w[:, k, 2 * C:3 * C],
                                           start=(k == 0), stop=(k == KC - 1))
            if a is NEIGH:
                n = KW0 - P
                for k in range(KC):
                    ins = nc.tensor.matmul(O0[0:n, C:2 * C], xnT[:, k, P - n:P], w[:, k, 2 * C:3 * C],
                                           start=(k == 0), stop=(k == KC - 1))
            ins.then_inc(psem("qkv"), 1)

        def conv_qkv_dve(dve, a, brow, i):
            for t, bank in qk_banks(a):
                await_(dve, a, "qkv", i, t + 1)
                nc.vector.tensor_tensor(qk.rearrange("p (s t h) e -> p s t (h e)", s=2, t=2)[:, :, t, :],
                                        bank[:, 0:2 * C].rearrange("p (s n) -> p s n", s=2),
                                        brow[:, 0:2 * C].rearrange("p (s n) -> p s n", s=2), ALU.add)\
                    .then_inc(psem("read"), 1)
            await_(dve, a, "qkv", i, 3)
            parts = [(P, 0, O0[:, 0:C]), (P, 1, O1[:, 0:C])]
            if a is NEIGH:
                parts.append((KW0 - P, 2, O0[0:KW0 - P, C:2 * C]))
            for n, vt, src in parts:
                ins = nc.vector.tensor_tensor(v_sb[0:n, vt, :, 0:HD], src.rearrange("p (h e) -> p h e", e=HD),
                                              brow[0:n, 2 * C:3 * C].rearrange("p (h e) -> p h e", e=HD), ALU.add)
            ins.then_inc(psem("v"), 1)


        def turns(eng, n, body, first=0):
            with eng.Fori(first, n - 1) as i:
                body(i, True)
            body(n - 1, False)

        def tile_x(i, t):
            return x_all[:, bass.ds(2 * i + t, 1), :].rearrange("p a c -> p (a c)")

        def image_x(i):
            return x_all[:, bass.ds(2 * i, 2), :]

        def two(psum_cols):
            return psum_cols.rearrange("p (t c) -> p t c", t=2)

        def ln_stats(link, i, ready):
            settle()
            for t in range(2):
                (link if t else link.inc)(nc.vector.bn_stats(stats[:, t, :], tile_x(i, t)))
            settle()
            for t in range(2):
                ins = nc.vector.bn_aggr(mean_var[:, t, :], stats[:, t, :])
            ins.then_inc(ready, 1)

        def ln_apply(dst, i):
            for t in range(2):
                ins = nc.vector.tensor_scalar(dst[:, t, 0:C], tile_x(i, t), mean_var[:, t, 0:1], rstd[:, t:t + 1],
                                              ALU.subtract, ALU.mult)
            return ins

        EARLY = high[0] // GU1
        gu1_d = d["L1_ffn_w_gate_up"].rearrange("e (p k) f -> p e (k f)", k=KC)
        dn1_d = d["L1_ffn_w_down"].rearrange("e (p c) f -> p e (c f)", c=DC1)
        gu0_d = d["L0_ffn_W_gate_up"].rearrange("(j r h) (p k) f -> r j p h (k f)", r=2, h=2, k=KC)
        dn0_d = d["L0_ffn_W_down"].rearrange("(j r h) (p c) f -> r j p h (c f)", r=2, h=2, c=DC0)
        gu1_flat = R[0:KP, 0:E1 * GU1].rearrange("p (e w) -> p e w", e=E1)
        dn1_flat = R[:, E1 * GU1:E1 * (GU1 + DN1)].rearrange("p (e w) -> p e w", e=E1)
        sx = sorted_x[:, :].rearrange("(n r p) c -> r n p c", r=2, p=P)
        sy = sorted_y[:, :].rearrange("(n r p) c -> n p r c", r=2, p=P)

        def chunked(w):
            return w.rearrange("(p k) n -> p k n", k=KC)

        @block.sync
        def _(sp):
            sp.dma_start(cf[:, :], d["cf"]).then_inc(s("const_loaded"), 16)
            sp.dma_start(y0_words[:, 0:NCB], d["cb"]).then_inc(s("const_loaded"), 16)
            sp.dma_start(x_all[:, :, :], d["x"].rearrange("(n p) c -> p n c", p=P)).then_inc(s("x_loaded"), 16)
            for dst, src in ((wqkv, chunked(d["L0_conv_w_qkv"])), (wproj, chunked(d["L0_conv_w_proj"])),
                             (brow, d["brow0"]), (wg0, chunked(d["L0_ffn_Wg"])), (ebias, d["ebias"]),
                             (wsg, chunked(d["L0_ffn_Wsg"])), (wsu, chunked(d["L0_ffn_Wsu"])),
                             (wsd, d["L0_ffn_Wsd"].rearrange("(c p) n -> p c n", p=DP0))):
                sp.dma_start(dst[:, :] if len(dst.shape) == 2 else dst[:, :, :], src).then_inc(s("wa_loaded"), 16)

            def load_pair(jj, r):
                sp.dma_start(ring_gu[r].rearrange("p h k f -> p h (k f)"), gu0_d[r][jj]).then_inc(s(f"ring_gu{r}"), 16)
                sp.dma_start(ring_dn[r].rearrange("p h c f -> p h (c f)"), dn0_d[r][jj]).then_inc(s(f"ring_dn{r}"), 16)

            for r in range(2):
                load_pair(0, r)
            for dst, src in ((wqkvf, chunked(d["L1_ffn_w_qkv"])), (wof, chunked(d["L1_ffn_w_out"])),
                             (norm_w, d["norm_w"]), (wr1, chunked(d["L1_ffn_w_router"]))):
                sp.dma_start(dst[:, :, :], src).then_inc(s("wf_loaded"), 16)
            with sp.Fori(0, B) as i:
                sp.wait_ge(s("a_row"), i + 1)
                sp.dma_start(rows0_t[bass.ds(i, 1), :, :, :].rearrange("a p t c -> (a p) t c"), row0)\
                    .then_inc(s("row_stored"), 16)
            sp.wait_ge(s("a_done"), B + 1)
            for dst, src in ((wqkv, chunked(d["L1_conv_w"])), (wproj, chunked(d["L1_conv_Wo"])), (brow, d["brow1"])):
                sp.dma_start(dst[:, :] if len(dst.shape) == 2 else dst[:, :, :], src).then_inc(s("wc_loaded"), 16)
            with sp.Fori(1, NPAIR // 2) as jj:
                for r in range(2):
                    sp.wait_ge(s(f"b_gu{r}"), jj)
                    sp.dma_start(ring_gu[r].rearrange("p h k f -> p h (k f)"),
                                 gu0_d[r][bass.ds(jj, 1)].rearrange("a p h w -> (a p) h w"))\
                        .then_inc(s(f"ring_gu{r}"), 16)
                sp.wait_ge(s("b_y"), jj)
                for r in range(2):
                    sp.dma_start(ring_dn[r].rearrange("p h c f -> p h (c f)"),
                                 dn0_d[r][bass.ds(jj, 1)].rearrange("a p h w -> (a p) h w"))\
                        .then_inc(s(f"ring_dn{r}"), 16)
            sp.wait_ge(s("b_y"), NPAIR // 2)
            sp.dma_start(gu1_flat[:, 0:EARLY, :], gu1_d[:, 0:EARLY, :]).then_inc(s("ffn1_loaded"), 16)
            sp.wait_ge(s("c_done"), B)
            sp.wait_ge(s("c_m"), B + 1)
            sp.dma_start(gu1_flat[:, EARLY:E1, :], gu1_d[:, EARLY:E1, :]).then_inc(s("ffn1_loaded"), 16)
            sp.dma_start(dn1_flat[:, :, :], dn1_d).then_inc(s("ffn1_loaded"), 16)
            if UPTO == "G":
                with sp.Fori(0, NSORT // 2) as n:
                    sp.wait_ge(s("f_yc"), n + 2)
                    sp.dma_start(sy[bass.ds(n, 1)].rearrange("a p r c -> (a p) r c"), y_f[:, :, :])\
                        .then_inc(s("f_stored"), 16)
            o = out.rearrange("(n p) c -> p n c", p=P)
            for n in range(NT):
                sp.wait_ge(s("g_out"), n + 1)
                sp.dma_start(o[:, n, :], x_all[:, n, :]).then_inc(s("stored"), 16)
            sp.wait_ge(s("stored"), 16 * NT)

        @block.gpsimd
        def _(pool):
            def root(link, src, scale, eps):
                link(nc.gpsimd.tensor_tensor(rstd[:, :], src, cst("neg")[:, scale:scale + 2], ALU.mult))
                link(nc.gpsimd.tensor_tensor(rstd[:, :], rstd[:, :], cst("neg")[:, eps:eps + 2], ALU.add))
                return nc.gpsimd.tensor_tensor(rstd[:, :], rstd[:, :], cst("neg")[:, 0:2], ALU.pow)

            pool.wait_ge(s("const_loaded"), 32)
            link = Links(pool, s("a_pool"), 0, 0)

            def a_root(link, k, eps):
                pool.wait_ge(s("a_var"), k)
                root(link, mean_var[:, :, 1], ONE, eps).then_inc(s("a_rstd"), 1)
            a_root(link, 1, EPS6)

            def a_body(i, more):
                link = Links(pool, s("a_pool"), i, 4)
                link.base = link.base + 2
                if more:
                    a_root(link, 2 * i + 2, EPS6)
                    a_root(link, 2 * i + 3, EPS5)
                else:
                    a_root(link, 2 * i + 2, EPS5)
            turns(pool, B, a_body)
            zero = cmp2[:, :, :].rearrange("p a b -> p (a b)")
            pool.wait_ge(s("set"), 1)
            zx = sorted_x[:, :].rearrange("(p a) c -> p (a c)", p=P)
            nz = NSORT * E1
            for z in range(NSORT * C // nz):
                pool.dma_start(zx[:, z * nz:(z + 1) * nz], zero).then_inc(s("zeroed"), 16)

            pool.wait_ge(s("b_idf"), 1)
            pool.wait_ge(s("row_stored"), 16 * B + 16)
            for j in range(NPAIR):
                pool.indirect_dma_start(out=slot_rows[:, j, :], out_offset=None, in_=rows0[:, :],
                                        in_offset=bass.IndirectOffsetOnAxis(ids_i[:, j:j + 1], 0))\
                    .then_inc(s("b_rows_first" if j < 2 else "b_rows_rest"), 16)

            def b_x(jj):
                nc.gpsimd.tensor_copy(xs[:, :, :], slot_rows[:, bass.ds(2 * jj, 2), 0:C]).then_inc(s("b_x"), 1)
            pool.wait_ge(s("b_rows_first"), 16 * 2)
            b_x(0)
            pool.wait_ge(s("b_rows_rest"), 16 * (NPAIR - 2))
            with pool.Fori(1, NPAIR // 2) as jj:
                pool.wait_ge(s("b_xT"), jj)
                b_x(jj)

            def c_root(link, name, k, src, scale, eps):
                pool.wait_ge(s(name), k)
                root(link, src, scale, eps).then_inc(s("c_rstd"), 1)
            mv, ss = mean_var[:, :, 1], sumsq[:, :]

            def c_onehot(link, i):
                for t in range(2):
                    nc.gpsimd.tensor_tensor(scratch[:, 9:10], cst("back"), cst("back"), ALU.add)
                    for j in range(NPAIR):
                        ins = nc.gpsimd.tensor_scalar(comb_s[:, t, j, :], cst("iota_tok"), ids_rel[:, j:j + 1], None,
                                                      ALU.is_equal)
                    ins.then_inc(s("c_onehot"), 1)
                    pool.wait_ge(s("c_onehot"), 2 * i + t + 1)
                    link(nc.gpsimd.tensor_tensor(ids_rel[:, :], ids_rel[:, :], cst("back").to_broadcast([P, NPAIR]),
                                                 ALU.add))
            link = Links(pool, s("c_pool"), 0, 6)
            c_onehot(link, 0)
            pool.wait_ge(s("c_comb"), 1)
            c_root(link, "c_var", 1, mv, ONE, EPS6)
            c_onehot(link, 1)
            link.end()

            def c_body(i, more):
                link = Links(pool, s("c_pool"), i, 10)
                link.base = link.base + 6
                c_root(link, "c_var", 2 * i + 2, mv, ONE, EPS5)
                c_root(link, "c_ss", 2 * i + 1, ss, PER_C, EPS6)
                if more:
                    pool.wait_ge(s("c_comb"), i + 2)
                    c_root(link, "c_var", 2 * i + 3, mv, ONE, EPS6)
                    c_onehot(link, i + 2)
                c_root(link, "c_ss", 2 * i + 2, ss, PER_C, EPS6)
                pool.wait_ge(s("c_mr"), i + 1)
                nc.gpsimd.tensor_copy(m_all[:, bass.ds(2 * i, 2), :], row0[:, :, 0:C]).then_inc(s("c_m"), 1)
            turns(pool, B, c_body)
            if UPTO == "G":
                pool.wait_ge(s("e_slots"), 1)
                pool.wait_ge(s("c_m"), B + 1)
                pool.wait_ge(s("zeroed"), 16 * (NSORT * C // nz))
                for n in range(NT):
                    for k in range(2):
                        pool.indirect_dma_start(out=sorted_x[:, :],
                                                out_offset=bass.IndirectOffsetOnAxis(slots_i[:, k, n:n + 1], 0),
                                                in_=m_all[:, n, :], in_offset=None).then_inc(s("scattered"), 16)
                pool.wait_ge(s("scattered"), 16 * 2 * NT)
                with pool.Fori(0, NSORT // 2) as n:
                    for r in range(2):
                        pool.wait_ge(s("f_xT"), n + 1)
                        pool.dma_start(xs[:, r, 0:C], sx[r][bass.ds(n, 1)].rearrange("a p c -> (a p) c"))\
                            .then_inc(s(f"f_loaded{r}"), 16)
                pool.wait_ge(s("f_stored"), 16 * (NSORT // 2) + 16)
                for n in range(NT):
                    r = n % 2
                    if n >= 2:
                        pool.wait_ge(s(f"g_used{r}"), n // 2)
                    for k in range(2):
                        pool.indirect_dma_start(out=(xs[:, r, 0:C], y_f[:, r, :])[k], out_offset=None,
                                                in_=sorted_y[:, :],
                                                in_offset=bass.IndirectOffsetOnAxis(slots_i[:, k, n:n + 1], 0))\
                            .then_inc(s(f"g_got{r}"), 16)

        @block.scalar
        def _(act):
            act.wait_ge(s("const_loaded"), 32)
            act.wait_ge(s("wa_loaded"), 16 * 8)
            def a_head(i, k):
                act.wait_ge(s("a_xT"), k)
                copy_pair(xnT).then_inc(s("a_xTc"), 1)
            a_head(0, 1)
            qk_copies_act(act, NEIGH, 0)

            def a_body(i, more):
                attention_act(act, NEIGH, i)
                if more:
                    a_head(i + 1, i + 2)
                act.wait_ge(s("a_tT"), i + 1)
                copy_pair(xnT).then_inc(s("a_tTc"), 1)
                act.wait_ge(s("a_logits"), i + 1)
                nc.scalar.activation(expl[:, :, :], two(M1[:, 0:2 * E0]), ACT.Exp, scale=-1.0).then_inc(s("a_expl"), 1)
                for c in range(SC):
                    act.wait_ge(s("a_gu"), SC * i + c + 1)
                    if c >= 6:
                        act.wait_ge(s("a_h"), SC * i + c - 5)
                    nc.scalar.activation(gate_act(c), GATE[c % 6][0:DP0, 0:256], ACT.Silu).then_inc(s("a_silu"), 1)
                if more:
                    qk_copies_act(act, NEIGH, i + 1)
            turns(act, B, a_body)

            def b_rows(jj):
                act.wait_ge(s("b_xT"), jj + 1)
                nc.scalar.activation(xsT[:, :, :, :], M0[0:KP, :].rearrange("p (r k t) -> p r k t", r=2, k=KC),
                                     ACT.Copy).then_inc(s("b_xTc"), 1)
            b_rows(0)

            def b_body(jj, more):
                for r in range(2):
                    act.wait_ge(s(f"b_gu{r}"), jj + 1)
                    nc.scalar.activation(h_sb[:, r, :], (S0, O0)[r][:, 0:I0], ACT.Silu).then_inc(s(f"b_silu{r}"), 1)
                if more:
                    b_rows(jj + 1)
                act.wait_ge(s("b_hT0"), jj + 1)
                nc.scalar.activation(hTs[0:DP0, 0, :], PT[0][0:DP0, :], ACT.Copy).then_inc(s("b_hTc0"), 1)
            turns(act, NPAIR // 2, b_body)

            def c_copy(k):
                act.wait_ge(s("c_xT"), k)
                copy_pair(xnT).then_inc(s("c_xTc"), 1)
            c_copy(1)
            qk_copies_act(act, WINDOW, 0)
            attention_act(act, WINDOW, 0)

            def c_body(i, more):
                def squares(n):
                    act.wait_ge(s("c_u"), 2 * i + n + 1)
                    for t in range(2):
                        ins = nc.scalar.activation(tmp[:, t, :], u_sb[:, t, :], ACT.Square, accum_out=sumsq[:, t:t + 1])
                    ins.then_inc(s("c_ss"), 1)
                squares(0)
                c_copy(3 * i + 2)
                if more:
                    c_copy(3 * i + 3)
                qk_copies_act(act, CAUSAL, i)
                attention_act(act, CAUSAL, i)
                squares(1)
                if more:
                    qk_copies_act(act, WINDOW, i + 1)
                c_copy(3 * i + (4 if more else 3))
                act.wait_ge(s("c_negmax"), i + 1)
                for t in range(2):
                    ins = nc.scalar.activation(expl[:, t, 0:E1], M1[:, t * E1:(t + 1) * E1], ACT.Exp,
                                               bias=wsum[:, t, 0:1], accum_out=wsum[:, t, 1:2])
                ins.then_inc(s("c_expl"), 1)
                if more:
                    attention_act(act, WINDOW, i + 1)
            turns(act, B, c_body)
            if UPTO == "G":
                def f_rows(n):
                    act.wait_ge(s("f_xT"), n + 2)
                    nc.scalar.activation(xsT[:, :, :, :], M0[0:KP, :].rearrange("p (r k t) -> p r k t", r=2, k=KC),
                                         ACT.Copy).then_inc(s("f_xTc"), 1)
                f_rows(0)

                def f_body(n, more):
                    for r in range(2):
                        act.wait_ge(s(f"f_gu{r}"), n + 1)
                        nc.scalar.activation(h_sb[:, r, 0:FF], (S0, O0)[r][:, 0:FF], ACT.Silu)\
                            .then_inc(s(f"f_silu{r}"), 1)
                    if more:
                        f_rows(n + 1)
                    act.wait_ge(s("f_hT0"), n + 1)
                    nc.scalar.activation(hTs[:, 0, 0:FF], PT[0][:, 0:FF], ACT.Copy).then_inc(s("f_hTc0"), 1)
                turns(act, NSORT // 2, f_body)

        @block.vector
        def _(dve):
            dve.wait_ge(s("const_loaded"), 32)
            nc.vector.memset(v_sb[:, :, :, :], 1.0)
            nc.vector.memset(v_causal[:, :, :, :], 1.0)
            nc.vector.memset(choice[:, :, :, :], BIG)
            nc.vector.memset(before0[:, :], 0.0)
            nc.vector.memset(before_all[:, 0, :], 0.0)
            nc.vector.memset(ids_acc[:, :, :], 0.0)
            nc.vector.tensor_copy(cb[:, :], y0_words[:, 0:NCB])
            nc.vector.tensor_copy(tokinfo[:, :, :], y0_words[:, CB["tokinfo"][0]:NCB].rearrange("p (t n) -> p t n", t=2))
            nc.vector.memset(cmp2[:, :, :], 0.0).then_inc(s("set"), 1)
            dve.wait_ge(s("set"), 1)
            nc.vector.memset(onehot[0][:, :, :], 0.0)
            nc.vector.memset(onehot[1][:, :, :], 0.0)
            ahead = [("a_done", 1), ("c_m", 1), ("row_stored", 16), ("b_yc", 1), ("f_xT", 1), ("f_yc", 1), ("f_stored", 16)]
            for n, (name, by) in enumerate(ahead):
                nc.vector.memset(scratch[:, n + 1:n + 2], 0.0).then_inc(s(name), by)
            dve.wait_ge(s("set"), 1)
            dve.wait_ge(s("x_loaded"), 16)
            dve.wait_ge(s("wa_loaded"), 16 * 8)

            def a_norm(link, i, k):
                return (lambda: ln_stats(link, i, s("a_var")),
                        lambda: (dve.wait_ge(s("a_rstd"), k), ln_apply(xn, i).then_inc(s("a_xn"), 1)))

            link = Links(dve, s("a_link"), 0, 7)
            run(a_norm(link, 0, 1))
            conv_qkv_dve(dve, NEIGH, brow, 0)
            run(split_qk(NEIGH, 0, link))
            link.end()
            qk_copies_dve(dve, NEIGH, 0)

            def a_body(i, more):
                link = Links(dve, s("a_link"), i, LINKS["A"])
                link.base = link.base + 7
                attention_dve(dve, NEIGH, i, link,
                              dict(zip((4, 6), a_norm(link, i + 1, 2 * i + 2))) if more else {})
                await_(dve, NEIGH, "proj", i, 1)
                link(nc.vector.tensor_tensor(tmp[:, :, :], two(M1[:, 0:2 * C]),
                                             brow[:, 3 * C:4 * C].unsqueeze(1).to_broadcast([P, 2, C]), ALU.add))
                link(nc.vector.tensor_tensor(image_x(i), image_x(i), tmp[:, :, :], ALU.add))
                ln_stats(link, i, s("a_var"))
                if more:
                    conv_qkv_dve(dve, NEIGH, brow, i + 1)
                dve.wait_ge(s("a_rstd"), 2 * i + (3 if more else 2))
                dve.wait_ge(s("row_stored"), 16 * i + 16)
                ln_apply(row0, i).then_inc(s("a_tn"), 1)
                if more:
                    run(split_qk(NEIGH, i + 1, link))
                dve.wait_ge(s("a_expl"), i + 1)
                link(nc.vector.tensor_scalar(sig[:, :, :], expl[:, :, :], 1.0, None, ALU.add))
                link(nc.vector.reciprocal(sig[:, :, :], sig[:, :, :]))
                link(nc.vector.tensor_tensor(choice[:, :, 0, 0:E0], sig[:, :, :],
                                             ebias[:, :].unsqueeze(1).to_broadcast([P, 2, E0]), ALU.add))
                n = E0 + 8 - TOP0
                settle()
                for t in range(2):
                    (link if t else link.inc)(nc.vector.max(top8[:, t, 0, :], choice[:, t, 0, 0:n]))
                settle()
                for t in range(2):
                    (link if t else link.inc)(nc.vector.match_replace(left[:, t, 0, 0:n], top8[:, t, 0, :], choice[:, t, 0, 0:n], NEG))
                link(nc.vector.tensor_scalar(mask[:, :, :], left[:, :, 0, 0:E0], NEG / 2, None, ALU.is_le))
                nc.vector.tensor_copy(mask_b[:, :, :], mask[:, :, :]).then_inc(s("a_mask"), 1)
                link(nc.vector.tensor_tensor(expl[:, :, :], sig[:, :, :], mask[:, :, :], ALU.mult))
                link(nc.vector.tensor_reduce(wsum[:, :, 0], expl[:, :, :], AX, ALU.add))
                link(nc.vector.tensor_scalar(wsum[:, :, 0], wsum[:, :, 0], 1e-20, None, ALU.add))
                link(nc.vector.reciprocal(wsum[:, :, 1], wsum[:, :, 0]))
                for t in range(2):
                    ins = nc.vector.tensor_scalar(row0[:, t, C:C + E0], expl[:, t, :], wsum[:, t, 1:2], 2.5,
                                                  ALU.mult, ALU.mult)
                ins.then_inc(s("a_row"), 1)
                for c in range(SC):
                    dve.wait_ge(s("a_silu"), SC * i + c + 1)
                    nc.vector.tensor_tensor(hT[:, c, :], gate_act(c), GATE[c % 6][0:DP0, 256:512], ALU.mult).then_inc(s("a_h"), 1)
                if more:
                    qk_copies_dve(dve, NEIGH, i + 1)
                link(nc.vector.tensor_scalar(sig[:, :, :], mask[:, :, :], -4096.0, 4096.0, ALU.mult, ALU.add))
                dve.wait_ge(s("a_pos"), i + 1)
                link(nc.vector.tensor_tensor(pos[:, :, :], two(M1[:, 0:2 * E0]), sig[:, :, :], ALU.add))
                for t in range(2):
                    ins = nc.vector.tensor_tensor(onehot[t][:, :, 0:CAP],
                                                  cst("iota_slot").unsqueeze(1).to_broadcast([P, E0, CAP]),
                                                  pos[:, t, :].unsqueeze(2).to_broadcast([P, E0, CAP]), ALU.is_equal)
                ins.then_inc(s("a_onehot"), 1)
                for t in range(2):
                    link(nc.vector.tensor_tensor(before0[:, :], before0[:, :], mask_b[:, t, :], ALU.add))
                dve.wait_ge(s("a_shared"), i + 1)
                link(nc.vector.tensor_tensor(image_x(i), image_x(i), two(M0[:, 0:2 * C]), ALU.add))
                dve.wait_ge(s("a_ids"), i + 1)
                link(nc.vector.tensor_tensor(ids_acc[:, :, :], ids_acc[:, :, :],
                                             M1[:, 64:64 + 3 * NPAIR].rearrange("p (j n) -> p j n", n=3), ALU.add))
                link(nc.vector.tensor_scalar(tokinfo[:, :, 0], tokinfo[:, :, 0], 2.0, None, ALU.add))
                nc.vector.memset(scratch[:, 15:16], 0.0).then_inc(s("a_done"), 1)
                if more:
                    link.end()
            turns(dve, B, a_body)

            nc.vector.scalar_tensor_tensor(ids_f[:, :], ids_acc[:, :, 0], float(P), ids_acc[:, :, 1], ALU.mult, ALU.add)\
                .then_inc(s("b_link"), 1)
            dve.wait_ge(s("b_link"), 1)
            nc.vector.tensor_copy(ids_rel[:, :], ids_f[:, :])
            nc.vector.tensor_copy(ids_i[:, :], ids_f[:, :]).then_inc(s("b_idf"), 1)

            def slot_weights(j0, j1, n):
                for step, ins in enumerate((
                        lambda: nc.vector.tensor_tensor(wslot[:, j0:j1, :], pair_w[:, j0:j1, :],
                                                        cst("half").unsqueeze(1).to_broadcast([P, j1 - j0, 2]), ALU.mult),
                        lambda: nc.vector.tensor_tensor(wsl[:, j0:j1], wslot[:, j0:j1, 0], wslot[:, j0:j1, 1], ALU.add),
                        lambda: nc.vector.tensor_tensor(wsl[:, j0:j1], wsl[:, j0:j1], ids_acc[:, j0:j1, 2], ALU.mult))):
                    ins().then_inc(s("b_weights"), 1)
                    dve.wait_ge(s("b_weights"), 3 * n + step + 1)

            def b_body(jj, more):
                link = Links(dve, s("b_done"), jj, LINKS["B"])
                for r in range(2):
                    dve.wait_ge(s(f"b_silu{r}"), jj + 1)
                    nc.vector.tensor_tensor(h_sb[:, r, :], h_sb[:, r, :], (S1, O1)[r][:, 0:I0], ALU.mult)\
                        .then_inc(s(f"b_h{r}"), 1)
                dve.wait_ge(s("b_hT1"), jj + 1)
                nc.vector.tensor_copy(hTs[0:DP0, 1, :], PT[1][0:DP0, :]).then_inc(s("b_hTc1"), 1)
                dve.wait_ge(s("b_y"), jj + 1)
                link(nc.vector.tensor_tensor(y_f[:, :, :], two(M1[:, 0:2 * C]),
                                             wsl[:, bass.ds(2 * jj, 2)].unsqueeze(2).to_broadcast([P, 2, C]), ALU.mult))

                def part(k):
                    return y0_all[:, bass.ds(2 * jj, 2), k, :]
                nc.vector.memset(scratch[:, 14:15], 0.0).then_inc(s("b_yc"), 1)
                link(nc.vector.tensor_copy(part(0), y_f[:, :, :]))
                link(nc.vector.tensor_tensor(y_f[:, :, :], y_f[:, :, :], part(0), ALU.subtract))
                link(nc.vector.tensor_copy(part(1), y_f[:, :, :]))
                link(nc.vector.tensor_tensor(part(2), y_f[:, :, :], part(1), ALU.subtract))
                link.end()
            dve.wait_ge(s("b_rows_first"), 16 * 2)
            slot_weights(0, 2, 0)
            b_body(0, True)
            dve.wait_ge(s("b_rows_rest"), 16 * (NPAIR - 2))
            slot_weights(2, NPAIR, 1)
            turns(dve, NPAIR // 2, b_body, first=1)

            dve.wait_ge(s("wc_loaded"), 16 * 3)
            dve.wait_ge(s("wf_loaded"), 16 * 4)
            def c_combine(link, i):
                dve.wait_ge(s("c_comb"), i + 1)
                link(nc.vector.tensor_tensor(image_x(i), image_x(i), two(T0[:, 0:2 * C]), ALU.add))
                ln_stats(link, i, s("c_var"))

            def c_norm(i, k):
                dve.wait_ge(s("c_rstd"), k)
                ln_apply(xn, i).then_inc(s("c_xn"), 1)

            link = Links(dve, s("c_link"), 0, 10)
            c_combine(link, 0)
            c_norm(0, 1)
            conv_qkv_dve(dve, WINDOW, brow, 0)
            run(split_qk(WINDOW, 0, link))
            qk_copies_dve(dve, WINDOW, 0)
            attention_dve(dve, WINDOW, 0, link)
            link.end()

            def c_body(i, more):
                link = Links(dve, s("c_link"), i, LINKS["C"])
                link.base = link.base + 10
                await_(dve, WINDOW, "proj", i, 1)
                link(nc.vector.tensor_tensor(tmp[:, :, :], two(M1[:, 0:2 * C]),
                                             brow[:, 3 * C:4 * C].unsqueeze(1).to_broadcast([P, 2, C]), ALU.add))
                link(nc.vector.tensor_tensor(image_x(i), image_x(i), tmp[:, :, :], ALU.add))
                ln_stats(link, i, s("c_var"))
                dve.wait_ge(s("c_rstd"), 4 * i + 2)
                link(ln_apply(u_sb, i))
                nc.vector.memset(scratch[:, 13:14], 0.0).then_inc(s("c_u"), 1)
                link(nc.vector.tensor_tensor(image_x(i), image_x(i), u_sb[:, :, :], ALU.add))

                def rms(n, dst, k):
                    dve.wait_ge(s("c_rstd"), k)
                    for t in range(2):
                        ins = nc.vector.scalar_tensor_tensor(dst[:, t, 0:C], u_sb[:, t, :], rstd[:, t:t + 1],
                                                             norm_w[:, n, :], ALU.mult, ALU.mult)
                    return ins
                rms(0, xn, 4 * i + 3).then_inc(s("c_xn"), 1)
                if more:
                    c_combine(link, i + 1)
                    dve.wait_ge(s("c_xT"), 3 * i + 2)
                    c_norm(i + 1, 4 * i + 4)
                nq = 15 * HD
                for t, bank in ((0, S0), (1, S1)):
                    await_(dve, CAUSAL, "qkv", i, t + 1)
                    raw = bank[:, 0:nq].rearrange("p (h e) -> p h e", e=HD)
                    q0, k0, nk = qk_rows(CAUSAL, t)
                    for dst, tab in ((rope_c, "cos"), (rope_s, "sin")):
                        link(nc.vector.tensor_tensor(dst, raw, cst(tab)[:, t * HD:(t + 1) * HD].unsqueeze(1)
                                                     .to_broadcast([P, 15, HD]), ALU.mult))
                    h = HD // 2
                    for r0, h0, n in ((q0, 0, NH), (k0, NH, nk)):
                        c, sn = rope_c[:, h0:h0 + n, :], rope_s[:, h0:h0 + n, :]
                        link.inc(nc.vector.tensor_tensor(qk[:, r0:r0 + n, 0:h], c[:, :, 0:h], sn[:, :, h:HD], ALU.subtract))
                        (link if h0 else link.inc)(nc.vector.tensor_tensor(qk[:, r0:r0 + n, h:HD], sn[:, :, 0:h], c[:, :, h:HD], ALU.add))
                    nc.vector.tensor_copy(v_causal[:, t, :, 0:HD],
                                          bank[:, nq:nq + NKV * HD].rearrange("p (h e) -> p h e", e=HD))\
                        .then_inc(psem("read"), 1)
                run(split_qk(CAUSAL, i, link))
                if more:
                    conv_qkv_dve(dve, WINDOW, brow, i + 1)
                qk_copies_dve(dve, CAUSAL, i)
                attention_dve(dve, CAUSAL, i, link,
                              dict(zip(range(2, 8), split_qk(WINDOW, i + 1, link))) if more else {})
                await_(dve, CAUSAL, "proj", i, 1)
                link(nc.vector.tensor_tensor(u_sb[:, :, :], u_sb[:, :, :], two(M1[:, 0:2 * C]), ALU.add))
                nc.vector.memset(scratch[:, 13:14], 0.0).then_inc(s("c_u"), 1)
                link(nc.vector.tensor_tensor(image_x(i), image_x(i), two(M1[:, 0:2 * C]), ALU.add))
                if more:
                    qk_copies_dve(dve, WINDOW, i + 1)
                dve.wait_ge(s("c_m"), i + 1)
                rms(1, row0, 4 * i + (5 if more else 4)).then_inc(s("c_mr"), 1)
                dve.wait_ge(s("c_logits"), i + 1)
                nc.vector.tensor_reduce(wsum[:, :, 0], two(M1[:, 0:2 * E1]), AX, ALU.max, negate=True)\
                    .then_inc(s("c_negmax"), 1)
                q0 = E0 - E1

                def probabilities():
                    dve.wait_ge(s("c_expl"), i + 1)
                    link(nc.vector.reciprocal(wsum[:, :, 1], wsum[:, :, 1]))
                    for t in range(2):
                        (link if t else link.inc)(nc.vector.tensor_scalar(choice[:, t, 0, q0:E0], expl[:, t, 0:E1],
                                                                          wsum[:, t, 1:2], None, ALU.mult))

                def highest():
                    settle()
                    for t in range(2):
                        for k in range(2):
                            (link if t + k == 2 else link.inc)(
                                nc.vector.max(top8[:, t, k, :], choice[:, t, 0, q0:E0 + 6 + k]))

                def strike():
                    settle()
                    for t in range(2):
                        for k in range(2):
                            (link if t + k == 2 else link.inc)(
                                nc.vector.match_replace(left[:, t, k, q0:E0 + 6 + k], top8[:, t, k, :],
                                                        choice[:, t, 0, q0:E0 + 6 + k], NEG))

                def masks():
                    for k in range(2):
                        (link if k else link.inc)(nc.vector.tensor_scalar(
                            mask12_all[:, bass.ds(2 * i, 2), k, :], left[:, :, k, q0:E0], NEG / 2, None, ALU.is_le))

                def earlier():
                    for t in range(2):
                        link(nc.vector.tensor_tensor(before_all[:, bass.ds(2 * i + t + 1, 1), :],
                                                     before_all[:, bass.ds(2 * i + t, 1), :],
                                                     mask12_all[:, bass.ds(2 * i + t, 1), 0, :], ALU.add))

                def weights():
                    link(nc.vector.tensor_tensor(wsum[:, :, 0], top8[:, :, 0, 7], top8[:, :, 1, 7], ALU.add))
                    link(nc.vector.reciprocal(wsum[:, :, 1], wsum[:, :, 0]))
                    for k in range(2):
                        ins = nc.vector.tensor_tensor(w12_all[:, bass.ds(2 * i, 2), k], top8[:, :, 1 - k, 7],
                                                      wsum[:, :, 1], ALU.mult)
                    ins.then_inc(s("c_done"), 1)
                router = [probabilities, highest, strike, masks, earlier, weights]
                if more:
                    attention_dve(dve, WINDOW, i + 1, link, dict(zip(range(1, 7), router)))
                    link.end()
                else:
                    run(router)
            turns(dve, B, c_body)

            if UPTO != "G":
                dve.wait_ge(s("c_done"), B)
                for n in range(NT):
                    nc.vector.tensor_copy(filled[:, 0:1], wsl[:, 0:1]).then_inc(s("g_out"), 1)
                return
            done = [0]

            def elink(ins):
                done[0] += 1
                ins.then_inc(s("e_link"), 1)
                dve.wait_ge(s("e_link"), done[0])

            dve.wait_ge(s("e_pos"), 1)
            elink(nc.vector.tensor_copy(counts[:, 0, :], T1[:, 0:E1]))
            elink(nc.vector.tensor_tensor(cmp[:, :, :], counts[:, 0, :].unsqueeze(2).to_broadcast([P, E1, 16]),
                                          cst("tiles").unsqueeze(1).to_broadcast([P, E1, 16]), ALU.is_gt))
            elink(nc.vector.tensor_reduce(counts[:, 1, :], cmp[:, :, :], AX, ALU.add))
            elink(nc.vector.tensor_copy(counts[:, 2, :], counts[:, 1, :]))
            cur, step = 2, 1
            while step < E1:
                nxt = 5 - cur
                elink(nc.vector.tensor_copy(counts[:, nxt, 0:step], counts[:, cur, 0:step]))
                elink(nc.vector.tensor_tensor(counts[:, nxt, step:E1], counts[:, cur, step:E1],
                                              counts[:, cur, 0:E1 - step], ALU.add))
                cur, step = nxt, 2 * step
            elink(nc.vector.tensor_tensor(counts[:, 4, :], counts[:, cur, :], counts[:, 1, :], ALU.subtract))
            elink(nc.vector.tensor_scalar(counts[:, 5, :], counts[:, 4, :], float(P), None, ALU.mult))
            elink(nc.vector.tensor_tensor(slot_g[:, :, :], T0[:, 0:NT * E1].rearrange("p (n e) -> p n e", e=E1),
                                          counts[:, 5, :].unsqueeze(1).to_broadcast([P, NT, E1]), ALU.add))
            elink(nc.vector.tensor_tensor(cmp[:, :, :], slot_g[:, :, :], mask12_all[:, :, 1, :], ALU.mult))
            elink(nc.vector.tensor_reduce(slots[:, 0, :], cmp[:, :, :], AX, ALU.add))
            elink(nc.vector.tensor_tensor(cmp[:, :, :], slot_g[:, :, :], mask12_all[:, :, 0, :], ALU.mult))
            elink(nc.vector.tensor_reduce(slots[:, 1, :], cmp[:, :, :], AX, ALU.add))
            elink(nc.vector.tensor_tensor(slots[:, 1, :], slots[:, 1, :], slots[:, 0, :], ALU.subtract))
            nc.vector.tensor_copy(slots_i[:, :, :], slots[:, :, :]).then_inc(s("e_slots"), 1)
            dve.wait_ge(s("zeroed"), 16 * 12)
            elink(nc.vector.tensor_tensor(cmp2[:, :, :], counts[:, cur, :].unsqueeze(1).to_broadcast([P, NSORT, E1]),
                                          cst("sorted").unsqueeze(2).to_broadcast([P, NSORT, E1]), ALU.is_le))
            elink(nc.vector.tensor_reduce(tile_e[:, :], cmp2[:, :, :], AX, ALU.add))
            elink(nc.vector.tensor_scalar(tile_e[:, :], tile_e[:, :], float(E1 - 1), None, ALU.min))
            nc.vector.tensor_copy(tile_ei[:, :], tile_e[:, :]).then_inc(s("e_tiles"), 1)
            def f_body(n, more):
                for r in range(2):
                    dve.wait_ge(s(f"f_silu{r}"), n + 1)
                    nc.vector.tensor_tensor(h_sb[:, r, 0:FF], h_sb[:, r, 0:FF], (S1, O1)[r][:, 0:FF], ALU.mult)\
                        .then_inc(s(f"f_h{r}"), 1)
                dve.wait_ge(s("f_hT1"), n + 1)
                nc.vector.tensor_copy(hTs[:, 1, 0:FF], PT[1][:, 0:FF]).then_inc(s("f_hTc1"), 1)
                dve.wait_ge(s("f_y"), n + 1)
                dve.wait_ge(s("f_stored"), 16 * n + 16)
                nc.vector.tensor_copy(y_f[:, :, :], two(M1[:, 0:2 * C])).then_inc(s("f_yc"), 1)
            turns(dve, NSORT // 2, f_body)
            for n in range(NT):
                r = n % 2
                dve.wait_ge(s(f"g_got{r}"), 32 * (n // 2 + 1))
                nc.vector.scalar_tensor_tensor(x_all[:, n, :], xs[:, r, 0:C], w12_all[:, n, 0:1], x_all[:, n, :],
                                               ALU.mult, ALU.add).then_inc(s("g_link"), 1)
                dve.wait_ge(s("g_link"), n + 1)
                nc.vector.scalar_tensor_tensor(x_all[:, n, :], y_f[:, r, :], w12_all[:, n, 1:2], x_all[:, n, :],
                                               ALU.mult, ALU.add).then_inc(s("g_out"), 1)
                dve.wait_ge(s("g_out"), n + 1)
                nc.vector.tensor_copy(filled[:, r:r + 1], w12_all[:, n, 0:1]).then_inc(s(f"g_used{r}"), 1)

        @block.tensor
        def _(pe):
            pe.wait_ge(s("const_loaded"), 32)
            pe.wait_ge(s("wa_loaded"), 16 * 8)
            pe.wait_ge(s("set"), 1)
            def a_head(i):
                pe.wait_ge(s("a_xn"), i + 1)
                transpose_pair(pe, xn).then_inc(s("a_xT"), 1)
                pe.wait_ge(s("a_xTc"), i + 1)
                conv_qkv_pe(pe, NEIGH, wqkv, i)
            a_head(0)
            transpose_qk(pe, NEIGH, 0)

            def a_body(i, more):
                attention_pe(pe, NEIGH, i)
                project(pe, NEIGH, wproj, i)
                if more:
                    a_head(i + 1)
                pe.wait_ge(s("a_tn"), i + 1)
                transpose_pair(pe, row0).then_inc(s("a_tT"), 1)
                pe.wait_ge(s("a_tTc"), i + 1)
                for t in range(2):
                    for k in range(KC):
                        ins = nc.tensor.matmul(M1[:, t * E0:(t + 1) * E0], xnT[:, k, t * P:(t + 1) * P], wg0[:, k, :],
                                               start=(k == 0), stop=(k == KC - 1))
                ins.then_inc(s("a_logits"), 1)
                for c in range(SC):
                    if c == 2 and more:
                        await_(pe, NEIGH, "v", i + 1, 1)
                    if c == 4 and more:
                        await_(pe, NEIGH, "read", i + 1, 2)
                    if c >= 6:
                        pe.wait_ge(s("a_h"), SC * i + c - 5)
                    for half, w in ((0, wsg), (1, wsu)):
                        for k in range(KC):
                            ins = nc.tensor.matmul(GATE[c % 6][0:DP0, half * 256:(half + 1) * 256],
                                                   w[:, k, c * DP0:(c + 1) * DP0], xnT[:, k, :],
                                                   start=(k == 0), stop=(k == KC - 1))
                    ins.then_inc(s("a_gu"), 1)
                pe.wait_ge(s("a_mask"), i + 1)
                tri, ones = cstb("tri"), cstb("ones")
                nc.tensor.matmul(M1[:, 0:E0], tri, mask_b[:, 0, :], start=True, stop=False)
                nc.tensor.matmul(M1[:, 0:E0], ones, before0[:, :], start=False, stop=True)
                nc.tensor.matmul(M1[:, E0:2 * E0], tri, mask_b[:, 1, :], start=True, stop=False)
                nc.tensor.matmul(M1[:, E0:2 * E0], ones, mask_b[:, 0, :], start=False, stop=False)
                nc.tensor.matmul(M1[:, E0:2 * E0], ones, before0[:, :], start=False, stop=True)\
                    .then_inc(s("a_pos"), 1)
                pe.wait_ge(s("a_h"), SC * i + SC)
                if more:
                    transpose_qk(pe, NEIGH, i + 1)
                for t in range(2):
                    for c in range(SC):
                        ins = nc.tensor.matmul(M0[:, t * C:(t + 1) * C], hT[:, c, t * P:(t + 1) * P], wsd[:, c, :],
                                               start=(c == 0), stop=(c == SC - 1))
                ins.then_inc(s("a_shared"), 1)
                pe.wait_ge(s("a_onehot"), i + 1)
                for j in range(NPAIR):
                    for t in range(2):
                        ins = nc.tensor.matmul(M1[:, 64 + 3 * j:67 + 3 * j],
                                               onehot[t][:, 2 * j:2 * j + 2, :].rearrange("p a b -> p (a b)"),
                                               tokinfo[:, t, :], start=(t == 0), stop=(t == 1))
                ins.then_inc(s("a_ids"), 1)
            turns(pe, B, a_body)

            pe.wait_ge(s("a_done"), B + 1)

            def b_rows(jj):
                pe.wait_ge(s("b_x"), jj + 1)
                for r in range(2):
                    for k in range(KC):
                        ins = nc.tensor.transpose(M0[0:KP, r * 256 + k * P:r * 256 + (k + 1) * P],
                                                  xs[:, r, :].rearrange("p (f k) -> p k f", k=KC)[:, k, :], ident)
                ins.then_inc(s("b_xT"), 1)
            def b_gate_up(jj):
                for r in range(2):
                    pe.wait_ge(s(f"ring_gu{r}"), 16 * jj + 16)
                    if r == 0:
                        pe.wait_ge(s("b_xTc"), jj + 1)
                    for part, bank in enumerate(((S0, S1), (O0, O1))[r]):
                        for k in range(KC):
                            for h in range(2):
                                ins = nc.tensor.matmul(bank[h * SLOT:(h + 1) * SLOT, 0:I0],
                                                       xsT[:, r, k, h * SLOT:(h + 1) * SLOT],
                                                       ring_gu[r][:, h, k, part * I0:(part + 1) * I0],
                                                       start=(k == 0), stop=(k == KC - 1))
                    ins.then_inc(s(f"b_gu{r}"), 1)
            b_rows(0)
            b_gate_up(0)

            def b_body(jj, more):
                if more:
                    b_rows(jj + 1)
                for r in range(2):
                    pe.wait_ge(s(f"b_h{r}"), jj + 1)
                    for c in range(DC0):
                        ins = nc.tensor.transpose(PT[r][0:DP0, c * P:(c + 1) * P],
                                                  h_sb[:, r, :].rearrange("p (f c) -> p c f", c=DC0)[:, c, :], ident)
                    ins.then_inc(s(f"b_hT{r}"), 1)
                pe.wait_ge(s("b_yc"), jj + 1)
                for r in range(2):
                    pe.wait_ge(s(f"b_hTc{r}"), jj + 1)
                    pe.wait_ge(s(f"ring_dn{r}"), 16 * jj + 16)
                    for c in range(DC0):
                        for h in range(2):
                            ins = nc.tensor.matmul(M1[h * SLOT:(h + 1) * SLOT, r * C:(r + 1) * C],
                                                   hTs[0:DP0, r, c * P + h * SLOT:c * P + (h + 1) * SLOT],
                                                   ring_dn[r][:, h, c, :], start=(c == 0), stop=(c == DC0 - 1))
                ins.then_inc(s("b_y"), 1)
                if more:
                    b_gate_up(jj + 1)
            turns(pe, NPAIR // 2, b_body)

            pe.wait_ge(s("b_done"), LINKS["B"] * (NPAIR // 2))
            pe.wait_ge(s("wc_loaded"), 16 * 3)
            pe.wait_ge(s("wf_loaded"), 16 * 4)
            def c_comb(i):
                for t in range(2):
                    pe.wait_ge(s("c_onehot"), 2 * i + t + 1)
                    for j in range(NPAIR):
                        for k in range(3):
                            ins = nc.tensor.matmul(T0[:, t * C:(t + 1) * C], comb_s[:, t, j, :], y0_all[:, j, k, :],
                                                   start=(j == 0 and k == 0), stop=(j == NPAIR - 1 and k == 2))
                ins.then_inc(s("c_comb"), 1)

            def c_norm(src, k):
                pe.wait_ge(*src)
                transpose_pair(pe, row0 if src[0] is s("c_mr") else xn).then_inc(s("c_xT"), 1)
                pe.wait_ge(s("c_xTc"), k)

            c_comb(0)
            c_norm((s("c_xn"), 1), 1)
            conv_qkv_pe(pe, WINDOW, wqkv, 0)
            transpose_qk(pe, WINDOW, 0)
            attention_pe(pe, WINDOW, 0)
            project(pe, WINDOW, wproj, 0)

            def c_body(i, more):
                if more:
                    c_comb(i + 1)
                c_norm((s("c_xn"), 2 * i + 2), 3 * i + 2)
                for t, bank in ((0, S0), (1, S1)):
                    for k in range(KC):
                        ins = nc.tensor.matmul(bank[:, 0:18 * HD], xnT[:, k, t * P:(t + 1) * P], wqkvf[:, k, :],
                                               start=(k == 0), stop=(k == KC - 1))
                    ins.then_inc(psem("qkv"), 1)
                if more:
                    c_norm((s("c_xn"), 2 * i + 3), 3 * i + 3)
                    conv_qkv_pe(pe, WINDOW, wqkv, i + 1)
                transpose_qk(pe, CAUSAL, i)
                if more:
                    await_(pe, WINDOW, "v", i + 1, 1)
                attention_pe(pe, CAUSAL, i)
                project(pe, CAUSAL, wof, i)
                if more:
                    transpose_qk(pe, WINDOW, i + 1)
                c_norm((s("c_mr"), i + 1), 3 * i + (4 if more else 3))
                for t in range(2):
                    for k in range(KC):
                        ins = nc.tensor.matmul(M1[:, t * E1:(t + 1) * E1], xnT[:, k, t * P:(t + 1) * P], wr1[:, k, :],
                                               start=(k == 0), stop=(k == KC - 1))
                ins.then_inc(s("c_logits"), 1)
                if more:
                    attention_pe(pe, WINDOW, i + 1, i + 1)
                    project(pe, WINDOW, wproj, i + 1)
            turns(pe, B, c_body)
            if UPTO != "G":
                return
            pe.wait_ge(s("c_done"), B)
            tri, ones = cstb("tri"), cstb("ones")
            for n in range(NT):
                nc.tensor.matmul(T0[:, n * E1:(n + 1) * E1], tri, mask12_all[:, n, 0, :], start=True, stop=False)
                nc.tensor.matmul(T0[:, n * E1:(n + 1) * E1], ones, before_all[:, n, :], start=False, stop=True)
            nc.tensor.matmul(T1[:, 0:E1], ones, before_all[:, NT, :], start=True, stop=True).then_inc(s("e_pos"), 1)
            pe.wait_ge(s("e_tiles"), 1)
            pe.wait_ge(s("ffn1_loaded"), 16 * 3)
            def f_rows(n):
                for r in range(2):
                    pe.wait_ge(s(f"f_loaded{r}"), 16 * n + 16)
                    for k in range(KC):
                        ins = nc.tensor.transpose(M0[0:KP, r * 256 + k * P:r * 256 + (k + 1) * P],
                                                  xs[:, r, 0:C].rearrange("p (f k) -> p k f", k=KC)[:, k, :], ident)
                ins.then_inc(s("f_xT"), 1)

            def experts(n):
                return [pe.value_load(tile_ei[0:1, bass.ds(2 * n + r, 1)], min_val=0, max_val=E1 - 1)
                        for r in range(2)]

            def f_gate_up(n, expert):
                pe.wait_ge(s("f_xTc"), n + 1)
                for r in range(2):
                    for part, bank in enumerate(((S0, S1), (O0, O1))[r]):
                        for k in range(KC):
                            ins = nc.tensor.matmul(bank[:, 0:FF], xsT[:, r, k, :],
                                                   gu1_all[:, bass.ds(expert[r], 1), k, part * FF:(part + 1) * FF]
                                                   .rearrange("p a f -> p (a f)"),
                                                   start=(k == 0), stop=(k == KC - 1))
                    ins.then_inc(s(f"f_gu{r}"), 1)
            f_rows(0)
            f_gate_up(0, experts(0))

            def f_body(n, more):
                expert = experts(n)
                if more:
                    following = experts(n + 1)
                    f_rows(n + 1)
                for r in range(2):
                    pe.wait_ge(s(f"f_h{r}"), n + 1)
                    for c in range(DC1):
                        ins = nc.tensor.transpose(PT[r][:, c * P:(c + 1) * P],
                                                  h_sb[:, r, 0:FF].rearrange("p (f c) -> p c f", c=DC1)[:, c, :], ident)
                    ins.then_inc(s(f"f_hT{r}"), 1)
                pe.wait_ge(s("f_yc"), n + 1)
                for r in range(2):
                    pe.wait_ge(s(f"f_hTc{r}"), n + 1)
                    for c in range(DC1):
                        ins = nc.tensor.matmul(M1[:, r * C:(r + 1) * C], hTs[:, r, c * P:(c + 1) * P],
                                               dn1_all[:, bass.ds(expert[r], 1), c, :].rearrange("p a f -> p (a f)"),
                                               start=(c == 0), stop=(c == DC1 - 1))
                ins.then_inc(s("f_y"), 1)
                if more:
                    f_gate_up(n + 1, following)
            turns(pe, NSORT // 2, f_body)


SHAPES = {"x": (TOK, C), "cf": (P, NCF), "cb": (P, NCB), "L0_conv_w_qkv": (C, 3 * C), "L0_conv_w_proj": (C, C),
          "brow0": (P, 4 * C), "L0_ffn_Wg": (C, E0), "ebias": (P, E0), "L0_ffn_Wsg": (C, IS0), "L0_ffn_Wsu": (C, IS0),
          "L0_ffn_Wsd": (IS0, C), "L0_ffn_W_gate_up": (E0, C, 2 * I0), "L0_ffn_W_down": (E0, I0, C),
          "L1_conv_w": (C, 3 * C), "L1_conv_Wo": (C, C), "brow1": (P, 4 * C), "L1_ffn_w_qkv": (C, 18 * HD),
          "L1_ffn_w_out": (C, C), "norm_w": (P, 2 * C), "L1_ffn_w_router": (C, E1),
          "L1_ffn_w_gate_up": (E1, C, 2 * FF), "L1_ffn_w_down": (E1, FF, C)}


def kernel(**inputs):
    import concourse.bacc as _bacc
    from concourse import mybir as _mybir
    from concourse.bass_utils import run_bass_kernel_spmd as _run

    a = {k: np.asarray(v) for k, v in inputs.items()}
    cf, cb = constants()

    def rows(*vs):
        return np.ascontiguousarray(np.broadcast_to(np.concatenate(vs)[None], (P, sum(len(v) for v in vs))))

    even_odd = np.concatenate([np.arange(0, HD, 2), np.arange(1, HD, 2)])
    order = [h * HD + even_odd for h in range(NH + NKV)] + [np.arange((NH + NKV) * HD, (NH + 2 * NKV) * HD)]
    data = {
        "x": a["x"].reshape(TOK, C), "cf": cf, "cb": cb,
        "L0_conv_w_qkv": a["L0_conv_w_qkv"].T, "L0_conv_w_proj": a["L0_conv_w_proj"].T,
        "brow0": rows(a["L0_conv_b_qkv"], a["L0_conv_b_proj"]), "L0_ffn_Wg": a["L0_ffn_Wg"].T,
        "ebias": rows(a["L0_ffn_e_bias"]), "L0_ffn_Wsg": a["L0_ffn_Wsg"], "L0_ffn_Wsu": a["L0_ffn_Wsu"],
        "L0_ffn_Wsd": a["L0_ffn_Wsd"], "L0_ffn_W_gate_up": a["L0_ffn_W_gate_up"], "L0_ffn_W_down": a["L0_ffn_W_down"],
        "L1_conv_w": np.concatenate([a["L1_conv_Wq"], a["L1_conv_Wk"], a["L1_conv_Wv"]], 1),
        "L1_conv_Wo": a["L1_conv_Wo"],
        "brow1": rows(np.concatenate([a["L1_conv_bq"], a["L1_conv_bk"], a["L1_conv_bv"]]), a["L1_conv_bo"]),
        "L1_ffn_w_qkv": a["L1_ffn_w_qkv"][:, np.concatenate(order)], "L1_ffn_w_out": a["L1_ffn_w_out"],
        "norm_w": rows(a["L1_ffn_norm1_w"], a["L1_ffn_norm2_w"]), "L1_ffn_w_router": a["L1_ffn_w_router"],
        "L1_ffn_w_gate_up": a["L1_ffn_w_gate_up"], "L1_ffn_w_down": a["L1_ffn_w_down"],
    }
    nc = _bacc.Bacc("TRN2", target_bir_lowering=False, num_devices=1)
    arrays, d = {}, {}
    for name, shape in SHAPES.items():
        v = np.ascontiguousarray(data[name])
        assert v.shape == shape, (name, v.shape)
        arrays[f"in_{name}"] = v
        d[name] = nc.dram_tensor(f"in_{name}", v.shape, _mybir.dt.from_np(v.dtype), kind="ExternalInput").ap()
    out = nc.dram_tensor("out_x", (TOK, C), F32, kind="ExternalOutput").ap()
    build(nc, d, out)
    r = _run(nc, [arrays], core_ids=[0])
    return r.results[0]["out_x"].reshape(B, IMG, IMG, C)
```

```python
from contextlib import ExitStack

import numpy as np

import concourse.bass as bass
from concourse import mybir

P = 128
B, IMG, C = 8, 16, 192
NT = B * IMG * IMG // P
TOK = NT * P
NH, HD = 12, 16
WIN = 7
KC, KP = 2, C // 2
E0, I0, IS0, TOP0, CAP = 32, 464, 928, 6, 48
SLOT = 64
NPAIR = E0 // 2
DC0 = 4
DP0 = I0 // DC0
SC = IS0 // DP0
E1, FF, NKV = 16, 384, 3
REP = NH // NKV
DC1 = FF // P
NSORT = 2 * TOK // P + E1
KW0 = 11 * IMG
BIG = 3.0e38
NEG = -1.0e30
RING = 2

F32 = mybir.dt.float32
BF16 = mybir.dt.bfloat16
I32 = mybir.dt.int32
U32 = mybir.dt.uint32
ALU = mybir.AluOpType
ACT = mybir.ActivationFunctionType
AX = mybir.AxisListType.X

CF = {}
CB = {}


def _lay(table, items):
    at = 0
    for name, n in items:
        table[name] = (at, n)
        at += n
    return at


NCF = _lay(CF, [("ident", P), ("iota_slot", CAP), ("iota_tok", P), ("cos", 2 * HD), ("sin", 2 * HD),
                ("tiles", 16), ("sorted", NSORT), ("half", 2), ("neg", 6), ("back", 1)])
NCB = _lay(CB, [("identb", P), ("tri", P), ("ones", P), ("mask_n", 4 * KW0), ("mask_w", 512),
                ("mask_c0", 512), ("mask_c1", 512), ("tokinfo", 6)])


def constants():
    f = np.zeros((P, NCF), np.float32)
    b = np.zeros((P, NCB), np.float32)
    p = np.arange(P)

    def put(arr, table, name, val):
        at, n = table[name]
        arr[:, at:at + n] = np.asarray(val, np.float32).reshape(P, n) if np.ndim(val) > 1 else val
    put(f, CF, "ident", np.eye(P))
    put(f, CF, "iota_slot", np.arange(CAP))
    put(f, CF, "iota_tok", np.arange(P))
    s = np.arange(2)[None, :, None] * P + p[:, None, None]
    inv = (1.0 / np.float32(10000.0) ** (np.arange(0, HD, 2, dtype=np.float32) / HD)).astype(np.float32)
    ang = (s.astype(np.float32) * inv[None, None, :]).astype(np.float32)
    put(f, CF, "cos", np.concatenate([np.cos(ang), np.cos(ang)], 2).reshape(P, -1))
    put(f, CF, "sin", np.concatenate([np.sin(ang), np.sin(ang)], 2).reshape(P, -1))
    put(f, CF, "tiles", np.arange(16) * P)
    put(f, CF, "sorted", np.arange(NSORT))
    put(f, CF, "half", np.stack([p < SLOT, p >= SLOT], 1))
    put(f, CF, "neg", np.repeat([-0.5, 1e-6, 1e-5], 2))
    put(f, CF, "back", -P)
    put(b, CB, "identb", np.eye(P))
    put(b, CB, "tri", (p[:, None] < p[None, :]))
    put(b, CB, "ones", 1.0)
    start = np.clip(np.arange(IMG) - WIN // 2, 0, IMG - WIN)
    m = np.zeros((P, 2, 2, KW0))
    for t, k0 in ((0, 0), (1, 2 * P - KW0)):
        q, k = t * P + p, k0 + np.arange(KW0)
        qr, qc, kr, kc = q // IMG, q % IMG, k // IMG, k % IMG
        seen = ((kr[None] >= start[qr][:, None]) & (kr[None] < start[qr][:, None] + WIN)
                & (kc[None] >= start[qc][:, None]) & (kc[None] < start[qc][:, None] + WIN))
        m[:, t] = np.where(seen, 0.0, NEG)[:, None, :]
    put(b, CB, "mask_n", m.reshape(P, -1))
    w = np.where(p[:, None] // IMG == p[None] // IMG, 0.0, NEG)
    put(b, CB, "mask_w", np.tile(w, (1, 4)))
    c0 = np.where(p[:, None] >= p[None], 0.0, NEG)
    put(b, CB, "mask_c0", np.tile(c0, (1, 4)))
    k2 = np.arange(2 * P)
    put(b, CB, "mask_c1", np.tile(np.where(P + p[:, None] >= k2[None], 0.0, NEG), (1, 2)))
    put(b, CB, "tokinfo", np.stack([np.zeros(P), p, np.ones(P), np.ones(P), p, np.ones(P)], 1))
    return f, b


EPS6, EPS5 = 2, 4


class Attention:

    def __init__(self, kinds):
        self.groups = []
        self.last_of_tile = {}
        for t, width, k0, kw, pieces, mask in kinds:
            for h0 in range(0, NH, width):
                self.groups.append((t, list(range(h0, h0 + width)), k0, kw, pieces, mask))
            self.last_of_tile[t] = len(self.groups) - 1
        self.n = len(self.groups)
        self.by_dve = (self.n + 1) // 2
        self.by_act = self.n // 2


NEIGH = Attention([(0, 2, 0, KW0, [(0, P, 0), (P, KW0 - P, 1)], ("mask_n", 0)),
                   (1, 2, 2 * P - KW0, KW0, [(0, KW0 - P, 2), (KW0 - P, P, 1)], ("mask_n", 2 * KW0))])
WINDOW = Attention([(0, 4, 0, P, [(0, P, 0)], ("mask_w", 0)),
                    (1, 4, P, P, [(0, P, 1)], ("mask_w", 0))])
CAUSAL = Attention([(0, 4, 0, P, [(0, P, 0)], ("mask_c0", 0)),
                    (1, 2, 0, 2 * P, [(0, P, 0), (P, P, 1)], ("mask_c1", 0))])

A_FIRST, A_TAIL, C_FIRST = 7, 3, 14
LINKS = {"A": 32, "B": 5, "C": 57}


def build(nc, d, out):
    ctx = ExitStack()
    with ctx:
        def sb(name, shape, dt=F32):
            return ctx.enter_context(nc.sbuf_tensor(name, shape, dt))

        def sem(name):
            return ctx.enter_context(nc.semaphore(name))

        cf = sb("cf", [P, NCF])
        cb = sb("cb", [P, NCB], BF16)

        def cst(name):
            at, n = CF[name]
            return cf[:, at:at + n]

        def cstb(name, off=0, n=None):
            at, m = CB[name]
            return cb[:, at + off:at + off + (n if n is not None else m - off)]

        ident = cst("ident")

        x_all = sb("x_all", [P, NT, C])
        m_all = sb("m_all", [P, NT, C])
        mask12_all = sb("mask12_all", [P, NT, 2, E1], BF16)
        before_all = sb("before_all", [P, NT + 1, E1], BF16)
        w12_all = sb("w12_all", [P, NT, 2])

        wqkv = sb("wqkv", [KP, KC, 3 * C])
        wproj = sb("wproj", [KP, KC, C])
        brow = sb("brow", [P, 4 * C])
        wg0 = sb("wg0", [KP, KC, E0])
        ebias = sb("ebias", [P, E0])
        wqkvf = sb("wqkvf", [KP, KC, (NH + 2 * NKV) * HD])
        wof = sb("wof", [KP, KC, C])
        norm_w = sb("norm_w", [P, 2, C])
        wr1 = sb("wr1", [KP, KC, E1])

        GU0 = KC * 2 * I0
        DN0 = DC0 * C
        GU1 = KC * 2 * FF
        DN1 = DC1 * C
        R = sb("R", [P, E1 * (GU1 + DN1)])
        gu1_all = R[0:KP, 0:E1 * GU1].rearrange("p (e k f) -> p e k f", e=E1, k=KC)
        dn1_all = R[:, E1 * GU1:E1 * (GU1 + DN1)].rearrange("p (e c f) -> p e c f", e=E1, c=DC1)
        low, high = [0], [E1 * (GU1 + DN1)]

        def carve(words, at_end):
            if at_end:
                high[0] -= words
                start = high[0]
            else:
                start = low[0]
                low[0] += words
            assert low[0] <= high[0], (low, high)
            return R[:, start:start + words]

        ring_gu = [carve(2 * GU0, False)[0:KP, :].rearrange("p (h k f) -> p h k f", h=2, k=KC) for _ in range(RING)]
        ring_dn = [carve(2 * DN0, False)[0:DP0, :].rearrange("p (h c f) -> p h c f", h=2, c=DC0) for _ in range(RING)]
        rows_at = low[0]
        wsg = carve(KC * IS0, False)[0:KP, :].rearrange("p (k f) -> p k f", k=KC)
        wsu = carve(KC * IS0, False)[0:KP, :].rearrange("p (k f) -> p k f", k=KC)
        wsd = carve(SC * C, False)[0:DP0, :].rearrange("p (c f) -> p c f", c=SC)
        ROW = C + E0
        assert rows_at + NPAIR * ROW + 2 * NPAIR <= low[0]
        slot_rows = R[:, rows_at:rows_at + NPAIR * ROW].rearrange("p (j c) -> p j c", j=NPAIR)
        pair_w = R[:, rows_at + C:rows_at + C + NPAIR * (ROW + 2)].rearrange("p (j c) -> p j c", j=NPAIR)[:, :, 0:2]

        xn = carve(2 * C, True).rearrange("p (t c) -> p t c", t=2)
        xnT = carve(KC * 2 * P, True)[0:KP, :].rearrange("p (k t) -> p k t", k=KC)
        qk_parts = carve(4 * NH * P // 2, True).bitcast(BF16).rearrange("p (r s e) -> p r s e", s=8, e=HD)
        qkT = carve(2 * NH * P, True).bitcast(BF16).rearrange("p (h t) -> p h t", h=2 * NH)
        v_sb = carve(3 * NH * (HD + 1), True).rearrange("p (v h e) -> p v h e", v=3, h=NH)
        probs = carve(3 * 512, True).rearrange("p (b k) -> p b k", b=3)
        probsT = carve(2 * 512, True).rearrange("p (b k) -> p b k", b=2)
        o_sb = carve(2 * C, True).rearrange("p (t c) -> p t c", t=2)
        row0 = carve(2 * (C + E0), True).rearrange("p (t c) -> p t c", t=2)
        y0_words = carve(NPAIR * 3 * C // 2, True)
        y0_all = y0_words.bitcast(BF16).rearrange("p (j s c) -> p j s c", j=NPAIR, s=3)
        onehot = [y0_words[:, t * E0 * SLOT // 2:(t + 1) * E0 * SLOT // 2].bitcast(BF16)
                  .rearrange("p (e s) -> p e s", e=E0) for t in range(2)]
        hT_words = carve(SC * 2 * P, True)
        hT = hT_words[0:DP0, :].rearrange("p (c t) -> p c t", c=SC)
        comb_s = hT_words.bitcast(BF16).rearrange("p (t j k) -> p t j k", t=2, j=NPAIR)

        neg_max = sb("neg_max", [P, 4, 4])
        rden = sb("rden", [P, 2, NH])
        stats = sb("stats", [P, 2, 6])
        mean_var = sb("mean_var", [P, 2, 2])
        rstd = sb("rstd", [P, 2])
        meansq = sb("meansq", [P, 2])
        expl = sb("expl", [P, 2, E0])
        sig = sb("sig", [P, 2, E0])
        choice = sb("choice", [P, 2, 2, E0 + 8])
        top8 = sb("top8", [P, 2, 2, 8])
        left = sb("left", [P, 2, 2, E0 + 8])
        mask = sb("mask", [P, 2, E0])
        mask_b = sb("mask_b", [P, 2, E0], BF16)
        before0 = sb("before0", [P, E0], BF16)
        tokinfo = sb("tokinfo", [P, 2, 3], BF16)
        wsum = sb("wsum", [P, 2, 2])
        pos = sb("pos", [P, 2, E0])
        ids_acc = sb("ids_acc", [P, NPAIR, 3])
        ids_f = sb("ids_f", [P, NPAIR])
        ids_i = sb("ids_i", [P, NPAIR], I32)
        ids_rel = sb("ids_rel", [P, NPAIR])
        scratch = sb("scratch", [P, 16])
        h_words = sb("h_words", [P, 2 * I0])
        h_sb = h_words[:, :].rearrange("p (r f) -> p r f", r=2)
        tmp = h_words[:, 0:2 * C].rearrange("p (t c) -> p t c", t=2)
        u_sb = h_words[:, 2 * C:4 * C].rearrange("p (t c) -> p t c", t=2)
        hTs_words = sb("hTs_words", [P, 2 * 4 * P])
        hTs = hTs_words[:, :].rearrange("p (r t) -> p r t", r=2)
        qk = hTs_words[:, 0:4 * NH * HD].rearrange("p (r e) -> p r e", e=HD)
        xs_words = sb("xs_words", [P, 2 * C])
        xs = xs_words[:, :].rearrange("p (r c) -> p r c", r=2)
        rope_c = xs_words[:, 0:15 * HD].rearrange("p (h e) -> p h e", e=HD)
        rope_s = sb("rope_s", [P, 15, HD])[:, :, :]
        v_causal = sb("v_causal", [P, 2, NKV, HD + 1])
        xsT = sb("xsT", [KP, 2, KC, P])
        wslot = sb("wslot", [P, NPAIR, 2])
        wsl = sb("wsl", [P, NPAIR])
        y_f = sb("y_f", [P, 2, C])
        counts = sb("counts", [P, 6, E1])
        cmp = sb("cmp", [P, E1, 16])
        cmp2 = sb("cmp2", [P, NSORT, E1])
        slot_g = sb("slot_g", [P, NT, E1])
        slots = sb("slots", [P, 2, NT])
        slots_i = sb("slots_i", [P, 2, NT], I32)
        tile_e = sb("tile_e", [P, NSORT])
        tile_ei = sb("tile_ei", [P, NSORT], I32)

        BK = [ctx.enter_context(nc.psum_tensor(f"bank{j}", [P, 512], F32)) for j in range(8)]
        S0, S1, T0, T1, O0, O1, M0, M1 = BK
        SCORE, PT, OB, COMB = [S0, S1, M0, M1], [T0, T1], [O0, O1], [T0, M1]

        GATE = [T0, T1, O0, O1, S0, S1]

        def gate_act(c):
            return probs[0:DP0, (c % 6) // 2, (c % 2) * 256:(c % 2) * 256 + 256]

        rows0 = nc.dram_tensor("rows0", [TOK, C + E0], F32)
        sorted_x = nc.dram_tensor("sorted_x", [NSORT * P, C], F32)
        sorted_y = nc.dram_tensor("sorted_y", [NSORT * P, C], F32)
        rows0_t = rows0[:, :].rearrange("(i t p) c -> i p t c", t=2, p=P)

        S = {}

        def s(name):
            if name not in S:
                S[name] = sem(name)
            return S[name]

        def per_image(a, name):
            return {"scores": a.n, "max": a.n, "exp": a.n, "pt": a.n, "pv": a.n, "pta": a.by_act, "ptd": a.by_dve,
                    "read": 2, "norm": 2, "qkT": 4 if a is CAUSAL else 6, "qkTa": 3,
                    "qkTd": 1 if a is CAUSAL else 3, "qkv": 2 if a is CAUSAL else 3,
                    "v": 0 if a is CAUSAL else 1}.get(name, 1)

        def psem(name):
            return s(f"att_{name}")

        def count(a, name, i, k):
            if a is NEIGH:
                return i * per_image(a, name) + k
            turn = per_image(WINDOW, name) + per_image(CAUSAL, name)
            before = B * per_image(NEIGH, name) + (per_image(WINDOW, name) if a is CAUSAL else 0)
            return i * turn + (before + k)

        def await_(eng, a, name, i, k):
            eng.wait_ge(psem(name), count(a, name, i, k))

        for n in ("cf_loaded", "cb_loaded", "x0_loaded", "x_loaded", "wqkv_loaded", "wa_loaded", "wc_loaded",
                  "wf_loaded", "ffn1_loaded", "row_stored", "set",
                  "a_var", "a_rstd", "a_xn", "a_tn", "a_xT", "a_xTc", "a_logits", "a_expl", "a_mask", "a_pos",
                  "a_onehot", "a_ids", "a_gu", "a_silu", "a_h", "a_shared", "a_row", "a_link", "a_pool", "a_done",
                  "b_idf", "b_x", "b_rows_first", "b_rows_rest", "b_weights", "b_link", "b_done",
                  "c_onehot", "c_comb", "c_link", "c_var", "c_u", "c_ss", "c_rstd", "c_xn", "c_xT", "c_xTc",
                  "c_mr", "a_tT", "a_tTc", "b_xT", "b_xTc", "b_y", "b_yc", "f_xT", "f_xTc", "f_y", "f_yc", "f_stored",
                  "c_logits", "c_negmax", "c_expl", "c_pool", "c_m", "c_done",
                  "e_pos", "e_link", "e_slots", "e_tiles", "scattered", "zeroed", "g_link", "g_out", "stored"):
            s(n)
        for r in range(2):
            for n in ("ring_gu", "ring_dn", "b_gu", "b_silu", "b_h", "b_hT", "b_hTc",
                      "f_loaded", "f_gu", "f_silu", "f_h", "f_hT", "f_hTc", "g_got", "g_used"):
                s(f"{n}{r}")
        for n in ("qkv", "read", "parts", "v", "qkT", "qkTa", "qkTd", "scores", "max", "exp", "pt", "pta", "ptd", "pv",
                  "norm", "oT", "oTc", "proj"):
            psem(n)

        block = ctx.enter_context(nc.Block())

        def settle():
            nc.vector.memset(scratch[:, 0:1], 0.0)

        class Links:

            def __init__(self, eng, sm, i, per):
                self.eng, self.sm, self.base, self.k, self.per = eng, sm, i * per, 0, per

            def inc(self, ins):
                self.k += 1
                ins.then_inc(self.sm, 1)

            def __call__(self, ins):
                self.inc(ins)
                self.eng.wait_ge(self.sm, self.base + self.k)

            def end(self):
                assert self.k == self.per, (self.sm, self.k)

        def qk_rows(a, t):
            nk = NKV if a is CAUSAL else NH
            return t * NH, 2 * NH + t * nk, nk

        def q_ap(h, t):
            return qkT[:, h, t * P:(t + 1) * P]

        def k_ap(a, h, k0, kw):
            return qkT[:, NH + (h // REP if a is CAUSAL else h), k0:k0 + kw]

        def v_ap(a, h, n, vt):
            return v_causal[0:n, vt, h // REP, :] if a is CAUSAL else v_sb[0:n, vt, h, :]

        def head_groups(a):
            q = [(False, h, 4, (S0, S1, O0)[n]) for n, h in enumerate(range(0, NH, 4))]
            k = [(True, NH, NKV, T1)] if a is CAUSAL else \
                [(True, NH + h, 4, (T0, T1, O1)[n]) for n, h in enumerate(range(0, NH, 4))]
            order = []
            while q or k:
                order += q[:1] + k[:1]
                q, k = q[1:], k[1:]
            return order

        def run(steps):
            for step in steps:
                step()

        def split_qk(a, i, link):
            nq, nk = 2 * NH, 2 * qk_rows(a, 0)[2]
            f = qk[:, 0:nq + nk, :]

            def part(side, at, n=1, step=1):
                r0, rows = ((0, nq), (nq, nk), (0, nq + nk))[side]
                return qk_parts[:, r0:r0 + rows, at:at + (n - 1) * step + 1:step, :]

            def one(side, at):
                return part(side, at).rearrange("p r s e -> p r (s e)")

            def first():
                await_(nc.vector, a, "read", i, 2)
                if a is WINDOW and not isinstance(i, int):
                    await_(nc.vector, CAUSAL, "qkT", i - 1, per_image(CAUSAL, "qkT"))
                link(nc.vector.tensor_copy(one(2, 0), f))

            def last():
                link.inc(nc.vector.tensor_tensor(one(0, 5), f[:, 0:nq], one(0, 1), ALU.subtract))
                link(nc.vector.tensor_tensor(one(1, 4), f[:, nq:nq + nk], one(1, 1), ALU.subtract))

            def places_q():
                nc.vector.tensor_copy(part(0, 2, 2), part(0, 0, 2))
                nc.vector.tensor_copy(part(0, 4, 2, 2), part(0, 0, 2))
                nc.vector.tensor_copy(one(0, 7), one(0, 5))

            def places_k():
                nc.vector.tensor_copy(part(1, 3, 2, 2), part(1, 0).to_broadcast([P, nk, 2, HD]))
                nc.vector.tensor_copy(part(1, 2, 2, 5), part(1, 1).to_broadcast([P, nk, 2, HD]))
                nc.vector.tensor_copy(one(1, 6), one(1, 4)).then_inc(psem("parts"), 1)
            return [first,
                    lambda: link(nc.vector.tensor_tensor(f, f, one(2, 0), ALU.subtract)),
                    lambda: link(nc.vector.tensor_copy(one(2, 1), f)),
                    last, places_q, places_k]

        def transpose_qk(pe, a, i):
            await_(pe, a, "parts", i, 1)
            for is_k, h0, heads, bank in head_groups(a):
                for h in range(heads):
                    for t in range(2):
                        q0, k0, _ = qk_rows(a, t)
                        row = k0 + h0 - NH + h if is_k else q0 + h0 + h
                        ins = nc.tensor.transpose(bank[:, :].bitcast(BF16)[:, (h * 2 + t) * P:(h * 2 + t + 1) * P],
                                                  qk_parts[:, row, :, :].rearrange("p s e -> p (s e)"), cstb("identb"))
                ins.then_inc(psem("qkT"), 1)

        def attention_pe(pe, a, i, routed=None, extra={}):

            def scores(u):
                t, heads, k0, kw, _, (mname, moff) = a.groups[u]
                if u >= 4:
                    await_(pe, a, "exp", i, u - 3)
                if u == 2 and a is NEIGH:
                    pe.wait_ge(s("a_done"), i + 1)
                if u == 3 and routed is not None:
                    pe.wait_ge(s("c_expl"), routed)
                if u < 2 or heads[0] % 4 == 0:
                    n = max(heads[0] // 4, u % 2 if u < 2 else 0) + 1
                    await_(pe, a, "qkTa", i, n)
                    await_(pe, a, "qkTd", i, min(n, per_image(a, "qkTd")))
                bank = SCORE[u % 4]
                nc.tensor.matmul(bank[:, 0:len(heads) * kw], cstb("identb"), cstb(mname, moff, len(heads) * kw),
                                 start=True, stop=False)
                for g, h in enumerate(heads):
                    ins = nc.tensor.matmul(bank[:, g * kw:(g + 1) * kw], q_ap(h, t), k_ap(a, h, k0, kw),
                                           start=False, stop=(g == len(heads) - 1))
                ins.then_inc(psem("scores"), 1)

            def transposes(u):
                t, heads, k0, kw, pieces, _ = a.groups[u]
                await_(pe, a, "exp", i, u + 1)
                if u >= 2:
                    if u % 2 == 0:
                        await_(pe, a, "ptd", i, u // 2)
                    else:
                        await_(pe, a, "pta", i, u // 2)
                for c, (c0, n, _) in sorted(enumerate(pieces), key=lambda e: -e[1][1]):
                    for g in range(len(heads)):
                        col = (c * len(heads) + g) * P
                        ins = nc.tensor.transpose(PT[u % 2][0:n, col:col + P],
                                                  probs[:, u % 3, g * kw + c0:g * kw + c0 + n], ident)
                ins.then_inc(psem("pt"), 1)

            def pv(u):
                t, heads, k0, kw, pieces, _ = a.groups[u]
                if u == 0:
                    await_(pe, a, "qkTa", i, per_image(a, "qkTa"))
                    await_(pe, a, "qkTd", i, per_image(a, "qkTd"))
                if u == 0 and a is not CAUSAL:
                    await_(pe, a, "v", i, 1)
                if u % 2 == 0:
                    await_(pe, a, "ptd", i, u // 2 + 1)
                else:
                    await_(pe, a, "pta", i, u // 2 + 1)
                for g, h in enumerate(heads):
                    for c, (c0, n, vt) in enumerate(pieces):
                        col = (c * len(heads) + g) * P
                        ins = nc.tensor.matmul(OB[t][:, h * (HD + 1):(h + 1) * (HD + 1)],
                                               probsT[0:n, u % 2, col:col + P], v_ap(a, h, n, vt),
                                               start=(c == 0), stop=(c == len(pieces) - 1))
                ins.then_inc(psem("pv"), 1)

            for u in range(a.n + 3):
                if u < a.n:
                    scores(u)
                if u in extra:
                    extra[u]()
                if 2 <= u < a.n + 2:
                    transposes(u - 2)
                if u >= 3:
                    pv(u - 3)
            for t in range(2):
                await_(pe, a, "norm", i, t + 1)
                for k in range(KC):
                    ins = nc.tensor.transpose(M0[0:KP, k * 256 + t * P:k * 256 + (t + 1) * P],
                                              o_sb[:, t, :].rearrange("p (f k) -> p k f", k=KC)[:, k, :], ident)
            ins.then_inc(psem("oT"), 1)

        def project(pe, a, w, i):
            await_(pe, a, "oTc", i, 1)
            for t in range(2):
                for k in range(KC):
                    ins = nc.tensor.matmul(M1[:, t * C:(t + 1) * C], xnT[:, k, t * P:(t + 1) * P], w[:, k, :],
                                           start=(k == 0), stop=(k == KC - 1))
            ins.then_inc(psem("proj"), 1)

        def attention_dve(dve, a, i, link, between={}):
            def copy_pt(u):
                _, heads, _, _, pieces, _ = a.groups[u]
                await_(dve, a, "pt", i, u + 1)
                if u >= 2:
                    await_(dve, a, "pv", i, u - 1)
                w = len(heads) * P
                for c, (_, n, _) in enumerate(pieces):
                    ins = nc.vector.tensor_copy(probsT[0:n, u % 2, c * w:(c + 1) * w], PT[u % 2][0:n, c * w:(c + 1) * w])
                ins.then_inc(psem("ptd"), 1)

            def normalise(t):
                await_(dve, a, "pv", i, a.last_of_tile[t] + 1)
                ov = OB[t][:, 0:NH * (HD + 1)].rearrange("p (h e) -> p h e", e=HD + 1)
                link(nc.vector.reciprocal(rden[:, t, :], ov[:, :, HD]))
                nc.vector.tensor_tensor(o_sb[:, t, :].rearrange("p (h e) -> p h e", e=HD), ov[:, :, 0:HD],
                                        rden[:, t, :].unsqueeze(2).to_broadcast([P, NH, HD]), ALU.mult)\
                    .then_inc(psem("norm"), 1)

            for u in range(a.n + 4):
                if u < a.n:
                    _, heads, _, kw, _, _ = a.groups[u]
                    await_(dve, a, "scores", i, u + 1)
                    g = len(heads)
                    nc.vector.tensor_reduce(neg_max[:, u % 4, 0:g],
                                            SCORE[u % 4][:, 0:g * kw].rearrange("p (g k) -> p g k", g=g),
                                            AX, ALU.max, negate=True).then_inc(psem("max"), 1)
                if 2 <= u < a.n + 2 and u % 2 == 0:
                    copy_pt(u - 2)
                if u in between:
                    between[u]()
                for t in range(2):
                    if u - 4 == a.last_of_tile[t]:
                        normalise(t)

        def attention_act(act, a, i, before={}):
            for u in range(a.n + 2):
                if u in before:
                    before[u]()
                if u < a.n:
                    _, heads, _, kw, _, _ = a.groups[u]
                    await_(act, a, "max", i, u + 1)
                    if u >= 3:
                        await_(act, a, "pt", i, u - 2)
                    for g in range(len(heads)):
                        ins = nc.scalar.activation(probs[:, u % 3, g * kw:(g + 1) * kw],
                                                   SCORE[u % 4][:, g * kw:(g + 1) * kw], ACT.Exp,
                                                   bias=neg_max[:, u % 4, g:g + 1])
                    ins.then_inc(psem("exp"), 1)
                if u >= 2 and u % 2 == 1:
                    v = u - 2
                    _, heads, _, _, pieces, _ = a.groups[v]
                    await_(act, a, "pt", i, v + 1)
                    if v >= 2:
                        await_(act, a, "pv", i, v - 1)
                    w = len(heads) * P
                    for c, (_, n, _) in enumerate(pieces):
                        ins = nc.scalar.activation(probsT[0:n, v % 2, c * w:(c + 1) * w], PT[v % 2][0:n, c * w:(c + 1) * w],
                                                   ACT.Copy)
                    ins.then_inc(psem("pta"), 1)
            await_(act, a, "oT", i, 1)
            nc.scalar.activation(xnT[:, :, :], M0[0:KP, :].rearrange("p (k t) -> p k t", k=KC), ACT.Copy)\
                .then_inc(psem("oTc"), 1)

        def qk_copies_act(act, a, i):
            def step(n, h0, heads, bank):
                await_(act, a, "qkT", i, n + 1)
                nc.scalar.activation(qkT[:, h0:h0 + heads, :].rearrange("p h t -> p (h t)"),
                                     bank[:, :].bitcast(BF16)[:, 0:heads * 256], ACT.Copy,
                                     scale=float(HD) ** -0.5).then_inc(psem("qkTa"), 1)
            return [lambda n=n, g=g: step(n, *g[1:]) for n, g in enumerate(head_groups(a)) if not g[0]]

        def qk_copies_dve(dve, a, i):
            def step(n, h0, heads, bank):
                await_(dve, a, "qkT", i, n + 1)
                nc.vector.tensor_copy(qkT[:, h0:h0 + heads, :].rearrange("p h t -> p (h t)"),
                                      bank[:, :].bitcast(BF16)[:, 0:heads * 256]).then_inc(psem("qkTd"), 1)
            return [lambda n=n, g=g: step(n, *g[1:]) for n, g in enumerate(head_groups(a)) if g[0]]

        def transpose_pair(pe, src):
            for t in range(2):
                for k in range(KC):
                    ins = nc.tensor.transpose(M0[0:KP, k * 256 + t * P:k * 256 + (t + 1) * P],
                                              src[:, t, 0:C].rearrange("p (f k) -> p k f", k=KC)[:, k, :], ident)
            return ins

        def copy_pair(dst):
            return nc.scalar.activation(dst[:, :, :], M0[0:KP, :].rearrange("p (k t) -> p k t", k=KC), ACT.Copy)

        def qk_banks(a):
            return enumerate((S0, S1) if a is NEIGH else (T1, M1))

        def conv_qkv_pe(pe, a, w, i):
            for t, bank in qk_banks(a):
                for k in range(KC):
                    ins = nc.tensor.matmul(bank[:, 0:2 * C], xnT[:, k, t * P:(t + 1) * P], w[:, k, 0:2 * C],
                                           start=(k == 0), stop=(k == KC - 1))
                ins.then_inc(psem("qkv"), 1)
            for t in range(2):
                for k in range(KC):
                    ins = nc.tensor.matmul(OB[t][:, 0:C], xnT[:, k, t * P:(t + 1) * P], w[:, k, 2 * C:3 * C],
                                           start=(k == 0), stop=(k == KC - 1))
            if a is NEIGH:
                n = KW0 - P
                for k in range(KC):
                    ins = nc.tensor.matmul(O0[0:n, C:2 * C], xnT[:, k, P - n:P], w[:, k, 2 * C:3 * C],
                                           start=(k == 0), stop=(k == KC - 1))
            ins.then_inc(psem("qkv"), 1)

        def conv_qkv_dve(dve, a, brow, i):
            for t, bank in qk_banks(a):
                await_(dve, a, "qkv", i, t + 1)
                nc.vector.tensor_tensor(qk.rearrange("p (s t h) e -> p s t (h e)", s=2, t=2)[:, :, t, :],
                                        bank[:, 0:2 * C].rearrange("p (s n) -> p s n", s=2),
                                        brow[:, 0:2 * C].rearrange("p (s n) -> p s n", s=2), ALU.add)\
                    .then_inc(psem("read"), 1)
            await_(dve, a, "qkv", i, 3)
            parts = [(P, 0, O0[:, 0:C]), (P, 1, O1[:, 0:C])]
            if a is NEIGH:
                parts.append((KW0 - P, 2, O0[0:KW0 - P, C:2 * C]))
            for n, vt, src in parts:
                ins = nc.vector.tensor_tensor(v_sb[0:n, vt, :, 0:HD], src.rearrange("p (h e) -> p h e", e=HD),
                                              brow[0:n, 2 * C:3 * C].rearrange("p (h e) -> p h e", e=HD), ALU.add)
            ins.then_inc(psem("v"), 1)


        def turns(eng, n, body, first=0):
            with eng.Fori(first, n - 1) as i:
                body(i, True)
            body(n - 1, False)

        def tile_x(i, t):
            return x_all[:, bass.ds(2 * i + t, 1), :].rearrange("p a c -> p (a c)")

        def image_x(i):
            return x_all[:, bass.ds(2 * i, 2), :]

        def two(psum_cols):
            return psum_cols.rearrange("p (t c) -> p t c", t=2)

        def add_bias(link, i):
            link(nc.vector.tensor_tensor(image_x(i), image_x(i),
                                         brow[:, 3 * C:4 * C].unsqueeze(1).to_broadcast([P, 2, C]), ALU.add))

        def ln_stats(link, i, ready):
            settle()
            for t in range(2):
                (link if t else link.inc)(nc.vector.bn_stats(stats[:, t, :], tile_x(i, t)))
            settle()
            for t in range(2):
                ins = nc.vector.bn_aggr(mean_var[:, t, :], stats[:, t, :])
            ins.then_inc(ready, 1)

        def ln_apply(dst, i):
            for t in range(2):
                ins = nc.vector.tensor_scalar(dst[:, t, 0:C], tile_x(i, t), mean_var[:, t, 0:1], rstd[:, t:t + 1],
                                              ALU.subtract, ALU.mult)
            return ins

        EARLY = high[0] // GU1
        gu1_d = d["L1_ffn_w_gate_up"].rearrange("e (p k) f -> p e (k f)", k=KC)
        dn1_d = d["L1_ffn_w_down"].rearrange("e (p c) f -> p e (c f)", c=DC1)
        gu0_d = d["L0_ffn_W_gate_up"].rearrange("(j r h) (p k) f -> r j p h (k f)", r=2, h=2, k=KC)
        dn0_d = d["L0_ffn_W_down"].rearrange("(j r h) (p c) f -> r j p h (c f)", r=2, h=2, c=DC0)
        gu1_flat = R[0:KP, 0:E1 * GU1].rearrange("p (e w) -> p e w", e=E1)
        dn1_flat = R[:, E1 * GU1:E1 * (GU1 + DN1)].rearrange("p (e w) -> p e w", e=E1)
        sx = sorted_x[:, :].rearrange("(n r p) c -> r n p c", r=2, p=P)
        sy = sorted_y[:, :].rearrange("(n r p) c -> n p r c", r=2, p=P)

        ZEROS = C // E1

        def chunked(w):
            return w.rearrange("(p k) n -> p k n", k=KC)

        @block.sync
        def _(sp):
            x_d = d["x"].rearrange("(n p) c -> p n c", p=P)
            sp.dma_start(x_all[:, 0:2, :], x_d[:, 0:2, :]).then_inc(s("x0_loaded"), 16)
            sp.dma_start(cf[:, :], d["cf"]).then_inc(s("cf_loaded"), 16)
            sp.dma_start(wqkv[:, :, :], chunked(d["L0_conv_w_qkv"])).then_inc(s("wqkv_loaded"), 16)
            sp.dma_start(brow[:, :], d["brow0"]).then_inc(s("wqkv_loaded"), 16)
            sp.dma_start(y0_words[:, 0:NCB], d["cb"]).then_inc(s("cb_loaded"), 16)
            sp.dma_start(x_all[:, 2:NT, :], x_d[:, 2:NT, :]).then_inc(s("x_loaded"), 16)
            for dst, src in ((wproj, chunked(d["L0_conv_w_proj"])),
                             (wg0, chunked(d["L0_ffn_Wg"])), (ebias, d["ebias"]),
                             (wsg, chunked(d["L0_ffn_Wsg"])), (wsu, chunked(d["L0_ffn_Wsu"])),
                             (wsd, d["L0_ffn_Wsd"].rearrange("(c p) n -> p c n", p=DP0))):
                sp.dma_start(dst[:, :] if len(dst.shape) == 2 else dst[:, :, :], src).then_inc(s("wa_loaded"), 16)

            def load_pair(jj, r):
                sp.dma_start(ring_gu[r].rearrange("p h k f -> p h (k f)"), gu0_d[r][jj]).then_inc(s(f"ring_gu{r}"), 16)
                sp.dma_start(ring_dn[r].rearrange("p h c f -> p h (c f)"), dn0_d[r][jj]).then_inc(s(f"ring_dn{r}"), 16)

            for r in range(2):
                load_pair(0, r)
            for dst, src in ((wqkvf, chunked(d["L1_ffn_w_qkv"])), (wof, chunked(d["L1_ffn_w_out"])),
                             (norm_w, d["norm_w"]), (wr1, chunked(d["L1_ffn_w_router"]))):
                sp.dma_start(dst[:, :, :], src).then_inc(s("wf_loaded"), 16)
            sp.wait_ge(s("set"), 1)
            for z in range(ZEROS):
                sp.dma_start(sorted_x[:, :].rearrange("(p a) c -> p (a c)", p=P)[:, z * NSORT * E1:(z + 1) * NSORT * E1],
                             cmp2[:, :, :].rearrange("p a b -> p (a b)")).then_inc(s("zeroed"), 16)
            with sp.Fori(0, B) as i:
                sp.wait_ge(s("a_row"), i + 1)
                sp.dma_start(rows0_t[bass.ds(i, 1), :, :, :].rearrange("a p t c -> (a p) t c"), row0)\
                    .then_inc(s("row_stored"), 16)
            sp.wait_ge(s("a_done"), B + 1)
            for dst, src in ((wqkv, chunked(d["L1_conv_w"])), (wproj, chunked(d["L1_conv_Wo"])), (brow, d["brow1"])):
                sp.dma_start(dst[:, :] if len(dst.shape) == 2 else dst[:, :, :], src).then_inc(s("wc_loaded"), 16)
            with sp.Fori(1, NPAIR // 2) as jj:
                for r in range(2):
                    sp.wait_ge(s(f"b_gu{r}"), 2 * jj)
                    sp.dma_start(ring_gu[r].rearrange("p h k f -> p h (k f)"),
                                 gu0_d[r][bass.ds(jj, 1)].rearrange("a p h w -> (a p) h w"))\
                        .then_inc(s(f"ring_gu{r}"), 16)
                sp.wait_ge(s("b_y"), jj)
                for r in range(2):
                    sp.dma_start(ring_dn[r].rearrange("p h c f -> p h (c f)"),
                                 dn0_d[r][bass.ds(jj, 1)].rearrange("a p h w -> (a p) h w"))\
                        .then_inc(s(f"ring_dn{r}"), 16)
            sp.wait_ge(s("b_y"), NPAIR // 2)
            sp.dma_start(gu1_flat[:, 0:EARLY, :], gu1_d[:, 0:EARLY, :]).then_inc(s("ffn1_loaded"), 16)
            sp.wait_ge(s("c_done"), B)
            sp.wait_ge(s("c_m"), B + 1)
            sp.dma_start(gu1_flat[:, EARLY:E1, :], gu1_d[:, EARLY:E1, :]).then_inc(s("ffn1_loaded"), 16)
            sp.dma_start(dn1_flat[:, :, :], dn1_d).then_inc(s("ffn1_loaded"), 16)
            with sp.Fori(0, NSORT // 2) as n:
                sp.wait_ge(s("f_yc"), n + 2)
                sp.dma_start(sy[bass.ds(n, 1)].rearrange("a p r c -> (a p) r c"), y_f[:, :, :])\
                    .then_inc(s("f_stored"), 16)
            o = out.rearrange("(n p) c -> p n c", p=P)
            for n in range(NT):
                sp.wait_ge(s("g_out"), n + 1)
                sp.dma_start(o[:, n, :], x_all[:, n, :]).then_inc(s("stored"), 16)
            sp.wait_ge(s("stored"), 16 * NT)

        @block.gpsimd
        def _(pool):
            def root(link, src, eps):
                link(nc.gpsimd.tensor_tensor(rstd[:, :], src, cst("neg")[:, eps:eps + 2], ALU.add))
                return nc.gpsimd.tensor_tensor(rstd[:, :], rstd[:, :], cst("neg")[:, 0:2], ALU.pow)

            pool.wait_ge(s("cf_loaded"), 16)
            link = Links(pool, s("a_pool"), 0, 0)

            def a_root(link, k, eps):
                pool.wait_ge(s("a_var"), k)
                root(link, mean_var[:, :, 1], eps).then_inc(s("a_rstd"), 1)
            a_root(link, 1, EPS6)

            def a_body(i, more):
                link = Links(pool, s("a_pool"), i, 2)
                link.base = link.base + 1
                if more:
                    a_root(link, 2 * i + 2, EPS6)
                    a_root(link, 2 * i + 3, EPS5)
                else:
                    a_root(link, 2 * i + 2, EPS5)
            turns(pool, B, a_body)
            pool.wait_ge(s("b_idf"), 1)
            pool.wait_ge(s("row_stored"), 16 * B + 16)
            for j in range(NPAIR):
                pool.indirect_dma_start(out=slot_rows[:, j, :], out_offset=None, in_=rows0[:, :],
                                        in_offset=bass.IndirectOffsetOnAxis(ids_i[:, j:j + 1], 0))\
                    .then_inc(s("b_rows_first" if j < 2 else "b_rows_rest"), 16)

            def b_x(jj):
                nc.gpsimd.tensor_copy(xs[:, :, :], slot_rows[:, bass.ds(2 * jj, 2), 0:C]).then_inc(s("b_x"), 1)
            pool.wait_ge(s("b_rows_rest"), 16 * (NPAIR - 2))
            with pool.Fori(1, NPAIR // 2) as jj:
                pool.wait_ge(s("b_xT"), jj)
                b_x(jj)

            def c_root(link, name, k, src, eps):
                pool.wait_ge(s(name), k)
                root(link, src, eps).then_inc(s("c_rstd"), 1)
            mv, ss = mean_var[:, :, 1], meansq[:, :]

            def c_onehot(link, i):
                for t in range(2):
                    nc.gpsimd.tensor_tensor(scratch[:, 9:10], cst("back"), cst("back"), ALU.add)
                    for j in range(NPAIR):
                        ins = nc.gpsimd.tensor_scalar(comb_s[:, t, j, :], cst("iota_tok"), ids_rel[:, j:j + 1], None,
                                                      ALU.is_equal)
                    ins.then_inc(s("c_onehot"), 1)
                    pool.wait_ge(s("c_onehot"), 2 * i + t + 1)
                    link(nc.gpsimd.tensor_tensor(ids_rel[:, :], ids_rel[:, :], cst("back").to_broadcast([P, NPAIR]),
                                                 ALU.add))
            link = Links(pool, s("c_pool"), 0, 5)
            c_onehot(link, 0)
            pool.wait_ge(s("c_comb"), 2)
            c_root(link, "c_var", 1, mv, EPS6)
            c_onehot(link, 1)
            link.end()

            def c_body(i, more):
                link = Links(pool, s("c_pool"), i, 6)
                link.base = link.base + 5
                c_root(link, "c_var", 2 * i + 2, mv, EPS5)
                c_root(link, "c_ss", 2 * i + 1, ss, EPS6)
                if more:
                    pool.wait_ge(s("c_comb"), 2 * i + 4)
                    c_root(link, "c_var", 2 * i + 3, mv, EPS6)
                    c_onehot(link, i + 2)
                c_root(link, "c_ss", 2 * i + 2, ss, EPS6)
                pool.wait_ge(s("c_mr"), i + 1)
                nc.gpsimd.tensor_copy(m_all[:, bass.ds(2 * i, 2), :], row0[:, :, 0:C]).then_inc(s("c_m"), 1)
            turns(pool, B, c_body)
            pool.wait_ge(s("e_slots"), 1)
            pool.wait_ge(s("c_m"), B + 1)
            pool.wait_ge(s("zeroed"), 16 * ZEROS)
            for n in range(NT):
                for k in range(2):
                    pool.indirect_dma_start(out=sorted_x[:, :],
                                            out_offset=bass.IndirectOffsetOnAxis(slots_i[:, k, n:n + 1], 0),
                                            in_=m_all[:, n, :], in_offset=None).then_inc(s("scattered"), 16)
            pool.wait_ge(s("scattered"), 16 * 2 * NT)
            with pool.Fori(0, NSORT // 2) as n:
                for r in range(2):
                    pool.wait_ge(s("f_xT"), n + 1)
                    pool.dma_start(xs[:, r, 0:C], sx[r][bass.ds(n, 1)].rearrange("a p c -> (a p) c"))\
                        .then_inc(s(f"f_loaded{r}"), 16)
            pool.wait_ge(s("f_stored"), 16 * (NSORT // 2) + 16)
            for n in range(NT):
                r = n % 2
                if n >= 2:
                    pool.wait_ge(s(f"g_used{r}"), n // 2)
                for k in range(2):
                    pool.indirect_dma_start(out=(xs[:, r, 0:C], y_f[:, r, :])[k], out_offset=None,
                                            in_=sorted_y[:, :],
                                            in_offset=bass.IndirectOffsetOnAxis(slots_i[:, k, n:n + 1], 0))\
                        .then_inc(s(f"g_got{r}"), 16)

        @block.scalar
        def _(act):
            def a_head(i, k):
                act.wait_ge(s("a_xT"), k)
                copy_pair(xnT).then_inc(s("a_xTc"), 1)
            a_head(0, 1)
            run(qk_copies_act(act, NEIGH, 0))

            def a_body(i, more):
                attention_act(act, NEIGH, i)
                if more:
                    a_head(i + 1, i + 2)
                act.wait_ge(s("a_tT"), i + 1)
                copy_pair(xnT).then_inc(s("a_tTc"), 1)
                act.wait_ge(s("a_logits"), i + 1)
                nc.scalar.activation(expl[:, :, :], two(M1[:, 0:2 * E0]), ACT.Exp, scale=-1.0).then_inc(s("a_expl"), 1)
                for c in range(SC):
                    act.wait_ge(s("a_gu"), SC * i + c + 1)
                    if c >= 6:
                        act.wait_ge(s("a_h"), SC * i + c - 5)
                    nc.scalar.activation(gate_act(c), GATE[c % 6][0:DP0, 0:256], ACT.Silu).then_inc(s("a_silu"), 1)
                if more:
                    run(qk_copies_act(act, NEIGH, i + 1))
            turns(act, B, a_body)

            def b_rows(jj):
                act.wait_ge(s("b_xT"), jj + 1)
                nc.scalar.activation(xsT[:, :, :, :], M0[0:KP, :].rearrange("p (r k t) -> p r k t", r=2, k=KC),
                                     ACT.Copy).then_inc(s("b_xTc"), 1)
            act.wait_ge(s("b_rows_first"), 16 * 2)
            nc.scalar.activation(xs[:, :, :], slot_rows[:, 0:2, 0:C], ACT.Copy).then_inc(s("b_x"), 1)
            b_rows(0)

            def b_body(jj, more):
                for r in range(2):
                    act.wait_ge(s(f"b_gu{r}"), 2 * jj + 1)
                    nc.scalar.activation(h_sb[:, r, :], (S0, O0)[r][:, 0:I0], ACT.Silu).then_inc(s(f"b_silu{r}"), 1)
                if more:
                    b_rows(jj + 1)
                act.wait_ge(s("b_hT0"), jj + 1)
                nc.scalar.activation(hTs[0:DP0, 0, :], PT[0][0:DP0, :], ACT.Copy).then_inc(s("b_hTc0"), 1)
            turns(act, NPAIR // 2, b_body)

            def c_copy(k):
                act.wait_ge(s("c_xT"), k)
                copy_pair(xnT).then_inc(s("c_xTc"), 1)
            c_copy(1)
            run(qk_copies_act(act, WINDOW, 0))
            attention_act(act, WINDOW, 0)

            def c_body(i, more):
                def squares(n):
                    act.wait_ge(s("c_u"), 2 * i + n + 1)
                    for t in range(2):
                        ins = nc.scalar.activation(tmp[:, t, :], u_sb[:, t, :], ACT.Square, scale=float(C) ** -0.5,
                                                   accum_out=meansq[:, t:t + 1])
                    ins.then_inc(s("c_ss"), 1)
                squares(0)
                c_copy(3 * i + 2)
                run(qk_copies_act(act, CAUSAL, i))
                attention_act(act, CAUSAL, i, {0: lambda: c_copy(3 * i + 3)} if more else {})
                squares(1)

                def router():
                    act.wait_ge(s("c_negmax"), i + 1)
                    for t in range(2):
                        ins = nc.scalar.activation(expl[:, t, 0:E1], M1[:, t * E1:(t + 1) * E1], ACT.Exp,
                                                   bias=wsum[:, t, 0:1], accum_out=wsum[:, t, 1:2])
                    ins.then_inc(s("c_expl"), 1)
                if more:
                    steps = qk_copies_act(act, WINDOW, i + 1)
                    run(steps[:1])
                    c_copy(3 * i + 4)
                    run(steps[1:])
                    attention_act(act, WINDOW, i + 1, {2: router})
                else:
                    c_copy(3 * i + 3)
                    router()
            turns(act, B, c_body)
            def f_rows(n):
                act.wait_ge(s("f_xT"), n + 2)
                nc.scalar.activation(xsT[:, :, :, :], M0[0:KP, :].rearrange("p (r k t) -> p r k t", r=2, k=KC),
                                     ACT.Copy).then_inc(s("f_xTc"), 1)
            f_rows(0)

            def f_body(n, more):
                for r in range(2):
                    act.wait_ge(s(f"f_gu{r}"), 2 * n + 1)
                    nc.scalar.activation(h_sb[:, r, 0:FF], (S0, O0)[r][:, 0:FF], ACT.Silu)\
                        .then_inc(s(f"f_silu{r}"), 1)
                act.wait_ge(s("f_hT0"), n + 1)
                nc.scalar.activation(hTs[:, 0, 0:FF], PT[0][:, 0:FF], ACT.Copy).then_inc(s("f_hTc0"), 1)
                if more:
                    f_rows(n + 1)
            turns(act, NSORT // 2, f_body)

        @block.vector
        def _(dve):
            nc.vector.memset(v_sb[:, :, :, :], 1.0)
            nc.vector.memset(v_causal[:, :, :, :], 1.0)
            nc.vector.memset(choice[:, :, :, :], BIG)
            nc.vector.memset(before0[:, :], 0.0)
            nc.vector.memset(before_all[:, 0, :], 0.0)
            nc.vector.memset(ids_acc[:, :, :], 0.0)
            ahead = [("a_done", 1), ("c_m", 1), ("row_stored", 16), ("b_yc", 1), ("f_xT", 1), ("f_yc", 1),
                     ("f_stored", 16)]
            for n, (name, by) in enumerate(ahead):
                nc.vector.memset(scratch[:, n + 1:n + 2], 0.0).then_inc(s(name), by)

            def a_norm(link, i, k):
                return (lambda: ln_stats(link, i, s("a_var")),
                        lambda: (dve.wait_ge(s("a_rstd"), k), ln_apply(xn, i).then_inc(s("a_xn"), 1)))

            link = Links(dve, s("a_link"), 0, A_FIRST)
            dve.wait_ge(s("cf_loaded"), 16)
            dve.wait_ge(s("x0_loaded"), 16)
            run(a_norm(link, 0, 1))
            dve.wait_ge(s("cb_loaded"), 16)
            nc.vector.tensor_copy(cb[:, :], y0_words[:, 0:NCB])
            nc.vector.tensor_copy(tokinfo[:, :, :], y0_words[:, CB["tokinfo"][0]:NCB].rearrange("p (t n) -> p t n", t=2))
            nc.vector.memset(cmp2[:, :, :], 0.0).then_inc(s("set"), 1)
            dve.wait_ge(s("wqkv_loaded"), 32)
            conv_qkv_dve(dve, NEIGH, brow, 0)
            run(split_qk(NEIGH, 0, link))
            link.end()
            dve.wait_ge(s("set"), 1)
            nc.vector.memset(onehot[0][:, :, :], 0.0)
            nc.vector.memset(onehot[1][:, :, :], 0.0)
            run(qk_copies_dve(dve, NEIGH, 0))
            dve.wait_ge(s("x_loaded"), 16)
            dve.wait_ge(s("wa_loaded"), 16 * 6)

            def a_tail(link, i):
                dve.wait_ge(s("a_shared"), i + 1)
                link(nc.vector.tensor_tensor(image_x(i), image_x(i), two(M0[:, 0:2 * C]), ALU.add))
                dve.wait_ge(s("a_ids"), i + 1)
                link(nc.vector.tensor_tensor(ids_acc[:, :, :], ids_acc[:, :, :],
                                             M1[:, 64:64 + 3 * NPAIR].rearrange("p (j n) -> p j n", n=3), ALU.add))
                link(nc.vector.tensor_scalar(tokinfo[:, :, 0], tokinfo[:, :, 0], 2.0, None, ALU.add))
                nc.vector.memset(scratch[:, 15:16], 0.0).then_inc(s("a_done"), 1)

            def a_body(i, more, first=False):
                link = Links(dve, s("a_link"), i, LINKS["A"])
                link.base = link.base + (A_FIRST if first else A_FIRST - A_TAIL)
                between = {} if first else {1: lambda: a_tail(link, i - 1)}
                if more:
                    between.update(zip((4, 6), a_norm(link, i + 1, 2 * i + 2)))
                between[8] = lambda: add_bias(link, i)
                attention_dve(dve, NEIGH, i, link, between)
                await_(dve, NEIGH, "proj", i, 1)
                link(nc.vector.tensor_tensor(image_x(i), image_x(i), two(M1[:, 0:2 * C]), ALU.add))
                ln_stats(link, i, s("a_var"))
                dve.wait_ge(s("a_rstd"), 2 * i + (3 if more else 2))
                dve.wait_ge(s("row_stored"), 16 * i + 16)
                ln_apply(row0, i).then_inc(s("a_tn"), 1)
                if more:
                    conv_qkv_dve(dve, NEIGH, brow, i + 1)
                    run(split_qk(NEIGH, i + 1, link))
                dve.wait_ge(s("a_expl"), i + 1)
                link(nc.vector.tensor_scalar(sig[:, :, :], expl[:, :, :], 1.0, None, ALU.add))
                link(nc.vector.reciprocal(sig[:, :, :], sig[:, :, :]))
                link(nc.vector.tensor_tensor(choice[:, :, 0, 0:E0], sig[:, :, :],
                                             ebias[:, :].unsqueeze(1).to_broadcast([P, 2, E0]), ALU.add))
                n = E0 + 8 - TOP0
                settle()
                for t in range(2):
                    (link if t else link.inc)(nc.vector.max(top8[:, t, 0, :], choice[:, t, 0, 0:n]))
                settle()
                for t in range(2):
                    (link if t else link.inc)(nc.vector.match_replace(left[:, t, 0, 0:n], top8[:, t, 0, :],
                                                                      choice[:, t, 0, 0:n], NEG))
                link(nc.vector.tensor_scalar(mask[:, :, :], left[:, :, 0, 0:E0], NEG / 2, None, ALU.is_le))
                nc.vector.tensor_copy(mask_b[:, :, :], mask[:, :, :]).then_inc(s("a_mask"), 1)
                link(nc.vector.tensor_tensor(expl[:, :, :], sig[:, :, :], mask[:, :, :], ALU.mult))
                link(nc.vector.tensor_reduce(wsum[:, :, 0], expl[:, :, :], AX, ALU.add))
                link(nc.vector.tensor_scalar(wsum[:, :, 0], wsum[:, :, 0], 1e-20, None, ALU.add))
                link(nc.vector.reciprocal(wsum[:, :, 1], wsum[:, :, 0]))
                for t in range(2):
                    ins = nc.vector.tensor_scalar(row0[:, t, C:C + E0], expl[:, t, :], wsum[:, t, 1:2], 2.5,
                                                  ALU.mult, ALU.mult)
                ins.then_inc(s("a_row"), 1)
                for c in range(SC):
                    dve.wait_ge(s("a_silu"), SC * i + c + 1)
                    nc.vector.tensor_tensor(hT[:, c, :], gate_act(c), GATE[c % 6][0:DP0, 256:512], ALU.mult)\
                        .then_inc(s("a_h"), 1)
                if more:
                    run(qk_copies_dve(dve, NEIGH, i + 1))
                link(nc.vector.tensor_scalar(sig[:, :, :], mask[:, :, :], -4096.0, 4096.0, ALU.mult, ALU.add))
                dve.wait_ge(s("a_pos"), i + 1)
                link(nc.vector.tensor_tensor(pos[:, :, :], two(M1[:, 0:2 * E0]), sig[:, :, :], ALU.add))
                for t in range(2):
                    ins = nc.vector.tensor_tensor(onehot[t][:, :, 0:CAP],
                                                  cst("iota_slot").unsqueeze(1).to_broadcast([P, E0, CAP]),
                                                  pos[:, t, :].unsqueeze(2).to_broadcast([P, E0, CAP]), ALU.is_equal)
                ins.then_inc(s("a_onehot"), 1)
                for t in range(2):
                    link(nc.vector.tensor_tensor(before0[:, :], before0[:, :], mask_b[:, t, :], ALU.add))
                if not more:
                    a_tail(link, i)
                elif not first:
                    link.end()
            a_body(0, True, True)
            turns(dve, B, a_body, first=1)

            nc.vector.scalar_tensor_tensor(ids_f[:, :], ids_acc[:, :, 0], float(P), ids_acc[:, :, 1], ALU.mult, ALU.add)\
                .then_inc(s("b_link"), 1)
            dve.wait_ge(s("b_link"), 1)
            nc.vector.tensor_copy(ids_rel[:, :], ids_f[:, :])
            nc.vector.tensor_copy(ids_i[:, :], ids_f[:, :]).then_inc(s("b_idf"), 1)

            def slot_weights(j0, j1, n):
                for step, ins in enumerate((
                        lambda: nc.vector.tensor_tensor(wslot[:, j0:j1, :], pair_w[:, j0:j1, :],
                                                        cst("half").unsqueeze(1).to_broadcast([P, j1 - j0, 2]), ALU.mult),
                        lambda: nc.vector.tensor_tensor(wsl[:, j0:j1], wslot[:, j0:j1, 0], wslot[:, j0:j1, 1], ALU.add),
                        lambda: nc.vector.tensor_tensor(wsl[:, j0:j1], wsl[:, j0:j1], ids_acc[:, j0:j1, 2], ALU.mult))):
                    ins().then_inc(s("b_weights"), 1)
                    dve.wait_ge(s("b_weights"), 3 * n + step + 1)

            def b_body(jj, more):
                link = Links(dve, s("b_done"), jj, LINKS["B"])
                for r in range(2):
                    dve.wait_ge(s(f"b_silu{r}"), jj + 1)
                    dve.wait_ge(s(f"b_gu{r}"), 2 * jj + 2)
                    nc.vector.tensor_tensor(h_sb[:, r, :], h_sb[:, r, :], (S1, O1)[r][:, 0:I0], ALU.mult)\
                        .then_inc(s(f"b_h{r}"), 1)
                dve.wait_ge(s("b_hT1"), jj + 1)
                nc.vector.tensor_copy(hTs[0:DP0, 1, :], PT[1][0:DP0, :]).then_inc(s("b_hTc1"), 1)
                dve.wait_ge(s("b_y"), jj + 1)
                link(nc.vector.tensor_tensor(y_f[:, :, :], two(M1[:, 0:2 * C]),
                                             wsl[:, bass.ds(2 * jj, 2)].unsqueeze(2).to_broadcast([P, 2, C]), ALU.mult))

                def part(k):
                    return y0_all[:, bass.ds(2 * jj, 2), k, :]
                nc.vector.memset(scratch[:, 14:15], 0.0).then_inc(s("b_yc"), 1)
                link(nc.vector.tensor_copy(part(0), y_f[:, :, :]))
                link(nc.vector.tensor_tensor(y_f[:, :, :], y_f[:, :, :], part(0), ALU.subtract))
                link(nc.vector.tensor_copy(part(1), y_f[:, :, :]))
                link(nc.vector.tensor_tensor(part(2), y_f[:, :, :], part(1), ALU.subtract))
                link.end()
            dve.wait_ge(s("b_rows_first"), 16 * 2)
            slot_weights(0, 2, 0)
            b_body(0, True)
            dve.wait_ge(s("b_rows_rest"), 16 * (NPAIR - 2))
            slot_weights(2, NPAIR, 1)
            turns(dve, NPAIR // 2, b_body, first=1)

            dve.wait_ge(s("wc_loaded"), 16 * 3)
            dve.wait_ge(s("wf_loaded"), 16 * 4)
            def c_combine(link, i):
                dve.wait_ge(s("c_comb"), 2 * i + 2)
                for k in range(2):
                    for t in range(2):
                        (link if t else link.inc)(nc.vector.tensor_tensor(tile_x(i, t), tile_x(i, t),
                                                                          COMB[t][:, k * C:(k + 1) * C], ALU.add))
                ln_stats(link, i, s("c_var"))

            def c_norm(i, k):
                dve.wait_ge(s("c_rstd"), k)
                ln_apply(xn, i).then_inc(s("c_xn"), 1)

            link = Links(dve, s("c_link"), 0, C_FIRST)
            c_combine(link, 0)
            c_norm(0, 1)
            conv_qkv_dve(dve, WINDOW, brow, 0)
            run(split_qk(WINDOW, 0, link))
            run(qk_copies_dve(dve, WINDOW, 0))
            attention_dve(dve, WINDOW, 0, link, {8: lambda: add_bias(link, 0)})
            link.end()

            def c_body(i, more):
                link = Links(dve, s("c_link"), i, LINKS["C"])
                link.base = link.base + C_FIRST
                await_(dve, WINDOW, "proj", i, 1)
                link(nc.vector.tensor_tensor(image_x(i), image_x(i), two(M1[:, 0:2 * C]), ALU.add))
                ln_stats(link, i, s("c_var"))
                dve.wait_ge(s("c_rstd"), 4 * i + 2)
                link(ln_apply(u_sb, i))
                nc.vector.memset(scratch[:, 13:14], 0.0).then_inc(s("c_u"), 1)
                link(nc.vector.tensor_tensor(image_x(i), image_x(i), u_sb[:, :, :], ALU.add))

                def rms(n, dst, k):
                    dve.wait_ge(s("c_rstd"), k)
                    for t in range(2):
                        ins = nc.vector.scalar_tensor_tensor(dst[:, t, 0:C], u_sb[:, t, :], rstd[:, t:t + 1],
                                                             norm_w[:, n, :], ALU.mult, ALU.mult)
                    return ins
                rms(0, xn, 4 * i + 3).then_inc(s("c_xn"), 1)
                nq = 15 * HD
                for t, bank in ((0, S0), (1, S1)):
                    await_(dve, CAUSAL, "qkv", i, t + 1)
                    raw = bank[:, 0:nq].rearrange("p (h e) -> p h e", e=HD)
                    q0, k0, nk = qk_rows(CAUSAL, t)
                    for wait, dst, tab in ((link.inc, rope_c, "cos"), (link, rope_s, "sin")):
                        wait(nc.vector.tensor_tensor(dst, raw, cst(tab)[:, t * HD:(t + 1) * HD].unsqueeze(1)
                                                     .to_broadcast([P, 15, HD]), ALU.mult))
                    h = HD // 2
                    for r0, h0, n in ((q0, 0, NH), (k0, NH, nk)):
                        c, sn = rope_c[:, h0:h0 + n, :], rope_s[:, h0:h0 + n, :]
                        link.inc(nc.vector.tensor_tensor(qk[:, r0:r0 + n, 0:h], c[:, :, 0:h], sn[:, :, h:HD],
                                                         ALU.subtract))
                        (link if h0 else link.inc)(nc.vector.tensor_tensor(qk[:, r0:r0 + n, h:HD], sn[:, :, 0:h],
                                                                           c[:, :, h:HD], ALU.add))
                    nc.vector.tensor_copy(v_causal[:, t, :, 0:HD],
                                          bank[:, nq:nq + NKV * HD].rearrange("p (h e) -> p h e", e=HD))\
                        .then_inc(psem("read"), 1)
                run(split_qk(CAUSAL, i, link))
                if more:
                    c_combine(link, i + 1)
                run(qk_copies_dve(dve, CAUSAL, i))
                if more:
                    c_norm(i + 1, 4 * i + 4)
                steps = [lambda: conv_qkv_dve(dve, WINDOW, brow, i + 1), lambda: None]
                if more:
                    steps += split_qk(WINDOW, i + 1, link)
                attention_dve(dve, CAUSAL, i, link, dict(zip(range(1, 9), steps)) if more else {})
                await_(dve, CAUSAL, "proj", i, 1)
                link(nc.vector.tensor_tensor(u_sb[:, :, :], u_sb[:, :, :], two(M1[:, 0:2 * C]), ALU.add))
                nc.vector.memset(scratch[:, 13:14], 0.0).then_inc(s("c_u"), 1)
                link(nc.vector.tensor_tensor(image_x(i), image_x(i), two(M1[:, 0:2 * C]), ALU.add))
                if more:
                    copies = qk_copies_dve(dve, WINDOW, i + 1)
                    run(copies[:1])
                dve.wait_ge(s("c_m"), i + 1)
                rms(1, row0, 4 * i + (5 if more else 4)).then_inc(s("c_mr"), 1)
                if more:
                    run(copies[1:])

                def highest_logit():
                    dve.wait_ge(s("c_logits"), i + 1)
                    nc.vector.tensor_reduce(wsum[:, :, 0], two(M1[:, 0:2 * E1]), AX, ALU.max, negate=True)\
                        .then_inc(s("c_negmax"), 1)
                q0 = E0 - E1

                def probabilities():
                    dve.wait_ge(s("c_expl"), i + 1)
                    link(nc.vector.reciprocal(wsum[:, :, 1], wsum[:, :, 1]))
                    for t in range(2):
                        (link if t else link.inc)(nc.vector.tensor_scalar(choice[:, t, 0, q0:E0], expl[:, t, 0:E1],
                                                                          wsum[:, t, 1:2], None, ALU.mult))

                def highest():
                    settle()
                    for t in range(2):
                        for k in range(2):
                            (link if t + k == 2 else link.inc)(
                                nc.vector.max(top8[:, t, k, :], choice[:, t, 0, q0:E0 + 6 + k]))

                def strike():
                    settle()
                    for t in range(2):
                        for k in range(2):
                            (link if t + k == 2 else link.inc)(
                                nc.vector.match_replace(left[:, t, k, q0:E0 + 6 + k], top8[:, t, k, :],
                                                        choice[:, t, 0, q0:E0 + 6 + k], NEG))

                def masks():
                    for k in range(2):
                        (link if k else link.inc)(nc.vector.tensor_scalar(
                            mask12_all[:, bass.ds(2 * i, 2), k, :], left[:, :, k, q0:E0], NEG / 2, None, ALU.is_le))

                def earlier():
                    for t in range(2):
                        link(nc.vector.tensor_tensor(before_all[:, bass.ds(2 * i + t + 1, 1), :],
                                                     before_all[:, bass.ds(2 * i + t, 1), :],
                                                     mask12_all[:, bass.ds(2 * i + t, 1), 0, :], ALU.add))

                def weights():
                    link(nc.vector.tensor_tensor(wsum[:, :, 0], top8[:, :, 0, 7], top8[:, :, 1, 7], ALU.add))
                    link(nc.vector.reciprocal(wsum[:, :, 1], wsum[:, :, 0]))
                    for k in range(2):
                        ins = nc.vector.tensor_tensor(w12_all[:, bass.ds(2 * i, 2), k], top8[:, :, 1 - k, 7],
                                                      wsum[:, :, 1], ALU.mult)
                    ins.then_inc(s("c_done"), 1)
                router = [highest_logit, probabilities, highest, strike, masks, earlier, weights]
                if more:
                    attention_dve(dve, WINDOW, i + 1, link,
                                  dict(zip(range(1, 9), router + [lambda: add_bias(link, i + 1)])))
                    link.end()
                else:
                    run(router)
            turns(dve, B, c_body)

            done = [0]

            def elink(ins):
                done[0] += 1
                ins.then_inc(s("e_link"), 1)
                dve.wait_ge(s("e_link"), done[0])

            dve.wait_ge(s("e_pos"), 1)
            elink(nc.vector.tensor_copy(counts[:, 0, :], T1[:, 0:E1]))
            elink(nc.vector.tensor_tensor(cmp[:, :, :], counts[:, 0, :].unsqueeze(2).to_broadcast([P, E1, 16]),
                                          cst("tiles").unsqueeze(1).to_broadcast([P, E1, 16]), ALU.is_gt))
            elink(nc.vector.tensor_reduce(counts[:, 1, :], cmp[:, :, :], AX, ALU.add))
            elink(nc.vector.tensor_copy(counts[:, 2, :], counts[:, 1, :]))
            cur, step = 2, 1
            while step < E1:
                nxt = 5 - cur
                elink(nc.vector.tensor_copy(counts[:, nxt, 0:step], counts[:, cur, 0:step]))
                elink(nc.vector.tensor_tensor(counts[:, nxt, step:E1], counts[:, cur, step:E1],
                                              counts[:, cur, 0:E1 - step], ALU.add))
                cur, step = nxt, 2 * step
            elink(nc.vector.tensor_tensor(counts[:, 4, :], counts[:, cur, :], counts[:, 1, :], ALU.subtract))
            elink(nc.vector.tensor_scalar(counts[:, 5, :], counts[:, 4, :], float(P), None, ALU.mult))
            elink(nc.vector.tensor_tensor(slot_g[:, :, :], T0[:, 0:NT * E1].rearrange("p (n e) -> p n e", e=E1),
                                          counts[:, 5, :].unsqueeze(1).to_broadcast([P, NT, E1]), ALU.add))
            elink(nc.vector.tensor_tensor(cmp[:, :, :], slot_g[:, :, :], mask12_all[:, :, 1, :], ALU.mult))
            elink(nc.vector.tensor_reduce(slots[:, 0, :], cmp[:, :, :], AX, ALU.add))
            elink(nc.vector.tensor_tensor(cmp[:, :, :], slot_g[:, :, :], mask12_all[:, :, 0, :], ALU.mult))
            elink(nc.vector.tensor_reduce(slots[:, 1, :], cmp[:, :, :], AX, ALU.add))
            elink(nc.vector.tensor_tensor(slots[:, 1, :], slots[:, 1, :], slots[:, 0, :], ALU.subtract))
            nc.vector.tensor_copy(slots_i[:, :, :], slots[:, :, :]).then_inc(s("e_slots"), 1)
            dve.wait_ge(s("zeroed"), 16 * ZEROS)
            elink(nc.vector.tensor_tensor(cmp2[:, :, :], counts[:, cur, :].unsqueeze(1).to_broadcast([P, NSORT, E1]),
                                          cst("sorted").unsqueeze(2).to_broadcast([P, NSORT, E1]), ALU.is_le))
            elink(nc.vector.tensor_reduce(tile_e[:, :], cmp2[:, :, :], AX, ALU.add))
            elink(nc.vector.tensor_scalar(tile_e[:, :], tile_e[:, :], float(E1 - 1), None, ALU.min))
            nc.vector.tensor_copy(tile_ei[:, :], tile_e[:, :]).then_inc(s("e_tiles"), 1)
            def f_body(n, more):
                for r in range(2):
                    dve.wait_ge(s(f"f_silu{r}"), n + 1)
                    dve.wait_ge(s(f"f_gu{r}"), 2 * n + 2)
                    nc.vector.tensor_tensor(h_sb[:, r, 0:FF], h_sb[:, r, 0:FF], (S1, O1)[r][:, 0:FF], ALU.mult)\
                        .then_inc(s(f"f_h{r}"), 1)
                dve.wait_ge(s("f_hT1"), n + 1)
                nc.vector.tensor_copy(hTs[:, 1, 0:FF], PT[1][:, 0:FF]).then_inc(s("f_hTc1"), 1)
                dve.wait_ge(s("f_y"), n + 1)
                dve.wait_ge(s("f_stored"), 16 * n + 16)
                nc.vector.tensor_copy(y_f[:, :, :], two(M1[:, 0:2 * C])).then_inc(s("f_yc"), 1)
            turns(dve, NSORT // 2, f_body)
            for n in range(NT):
                r = n % 2
                dve.wait_ge(s(f"g_got{r}"), 32 * (n // 2 + 1))
                nc.vector.scalar_tensor_tensor(x_all[:, n, :], xs[:, r, 0:C], w12_all[:, n, 0:1], x_all[:, n, :],
                                               ALU.mult, ALU.add).then_inc(s("g_link"), 1)
                dve.wait_ge(s("g_link"), n + 1)
                nc.vector.scalar_tensor_tensor(x_all[:, n, :], y_f[:, r, :], w12_all[:, n, 1:2], x_all[:, n, :],
                                               ALU.mult, ALU.add).then_inc(s("g_out"), 1)
                dve.wait_ge(s("g_out"), n + 1)
                nc.vector.memset(scratch[:, 12:13], 0.0).then_inc(s(f"g_used{r}"), 1)

        @block.tensor
        def _(pe):
            pe.wait_ge(s("cf_loaded"), 16)
            pe.wait_ge(s("wqkv_loaded"), 32)
            def a_head(i):
                pe.wait_ge(s("a_xn"), i + 1)
                transpose_pair(pe, xn).then_inc(s("a_xT"), 1)
                pe.wait_ge(s("a_xTc"), i + 1)
                conv_qkv_pe(pe, NEIGH, wqkv, i)
            a_head(0)
            pe.wait_ge(s("set"), 1)
            transpose_qk(pe, NEIGH, 0)
            pe.wait_ge(s("wa_loaded"), 16 * 6)

            attention_pe(pe, NEIGH, 0)
            project(pe, NEIGH, wproj, 0)

            def a_body(i, more):
                if more:
                    a_head(i + 1)
                pe.wait_ge(s("a_tn"), i + 1)
                transpose_pair(pe, row0).then_inc(s("a_tT"), 1)
                pe.wait_ge(s("a_tTc"), i + 1)
                for t in range(2):
                    for k in range(KC):
                        ins = nc.tensor.matmul(M1[:, t * E0:(t + 1) * E0], xnT[:, k, t * P:(t + 1) * P], wg0[:, k, :],
                                               start=(k == 0), stop=(k == KC - 1))
                ins.then_inc(s("a_logits"), 1)
                for c in range(SC):
                    if c == 2 and more:
                        await_(pe, NEIGH, "v", i + 1, 1)
                    if c == 4 and more:
                        await_(pe, NEIGH, "read", i + 1, 2)
                    if c >= 6:
                        pe.wait_ge(s("a_h"), SC * i + c - 5)
                    for half, w in ((0, wsg), (1, wsu)):
                        for k in range(KC):
                            ins = nc.tensor.matmul(GATE[c % 6][0:DP0, half * 256:(half + 1) * 256],
                                                   w[:, k, c * DP0:(c + 1) * DP0], xnT[:, k, :],
                                                   start=(k == 0), stop=(k == KC - 1))
                    ins.then_inc(s("a_gu"), 1)
                pe.wait_ge(s("a_mask"), i + 1)
                tri, ones = cstb("tri"), cstb("ones")
                nc.tensor.matmul(M1[:, 0:E0], tri, mask_b[:, 0, :], start=True, stop=False)
                nc.tensor.matmul(M1[:, 0:E0], ones, before0[:, :], start=False, stop=True)
                nc.tensor.matmul(M1[:, E0:2 * E0], tri, mask_b[:, 1, :], start=True, stop=False)
                nc.tensor.matmul(M1[:, E0:2 * E0], ones, mask_b[:, 0, :], start=False, stop=False)
                nc.tensor.matmul(M1[:, E0:2 * E0], ones, before0[:, :], start=False, stop=True)\
                    .then_inc(s("a_pos"), 1)
                pe.wait_ge(s("a_h"), SC * i + SC)
                if more:
                    transpose_qk(pe, NEIGH, i + 1)

                def shared_down(t):
                    for c in range(SC):
                        ins = nc.tensor.matmul(M0[:, t * C:(t + 1) * C], hT[:, c, t * P:(t + 1) * P], wsd[:, c, :],
                                               start=(c == 0), stop=(c == SC - 1))
                    return ins
                shared_down(0)

                def rest():
                    shared_down(1).then_inc(s("a_shared"), 1)
                    pe.wait_ge(s("a_onehot"), i + 1)
                    for j in range(NPAIR):
                        for t in range(2):
                            ins = nc.tensor.matmul(M1[:, 64 + 3 * j:67 + 3 * j],
                                                   onehot[t][:, 2 * j:2 * j + 2, :].rearrange("p a b -> p (a b)"),
                                                   tokinfo[:, t, :], start=(t == 0), stop=(t == 1))
                    ins.then_inc(s("a_ids"), 1)
                if more:
                    attention_pe(pe, NEIGH, i + 1, None, {1: rest})
                    project(pe, NEIGH, wproj, i + 1)
                else:
                    rest()
            turns(pe, B, a_body)

            pe.wait_ge(s("a_done"), B + 1)

            def b_rows(jj):
                pe.wait_ge(s("b_x"), jj + 1)
                for r in range(2):
                    for k in range(KC):
                        ins = nc.tensor.transpose(M0[0:KP, r * 256 + k * P:r * 256 + (k + 1) * P],
                                                  xs[:, r, :].rearrange("p (f k) -> p k f", k=KC)[:, k, :], ident)
                ins.then_inc(s("b_xT"), 1)
            def b_gate_up(jj):
                for r in range(2):
                    pe.wait_ge(s(f"ring_gu{r}"), 16 * jj + 16)
                    if r == 0:
                        pe.wait_ge(s("b_xTc"), jj + 1)
                    for part, bank in enumerate(((S0, S1), (O0, O1))[r]):
                        for k in range(KC):
                            for h in range(2):
                                ins = nc.tensor.matmul(bank[h * SLOT:(h + 1) * SLOT, 0:I0],
                                                       xsT[:, r, k, h * SLOT:(h + 1) * SLOT],
                                                       ring_gu[r][:, h, k, part * I0:(part + 1) * I0],
                                                       start=(k == 0), stop=(k == KC - 1))
                        ins.then_inc(s(f"b_gu{r}"), 1)
            b_rows(0)
            b_gate_up(0)

            def b_body(jj, more):
                if more:
                    b_rows(jj + 1)
                for r in range(2):
                    pe.wait_ge(s(f"b_h{r}"), jj + 1)
                    for c in range(DC0):
                        ins = nc.tensor.transpose(PT[r][0:DP0, c * P:(c + 1) * P],
                                                  h_sb[:, r, :].rearrange("p (f c) -> p c f", c=DC0)[:, c, :], ident)
                    ins.then_inc(s(f"b_hT{r}"), 1)
                pe.wait_ge(s("b_yc"), jj + 1)
                for r in range(2):
                    pe.wait_ge(s(f"b_hTc{r}"), jj + 1)
                    pe.wait_ge(s(f"ring_dn{r}"), 16 * jj + 16)
                    for c in range(DC0):
                        for h in range(2):
                            ins = nc.tensor.matmul(M1[h * SLOT:(h + 1) * SLOT, r * C:(r + 1) * C],
                                                   hTs[0:DP0, r, c * P + h * SLOT:c * P + (h + 1) * SLOT],
                                                   ring_dn[r][:, h, c, :], start=(c == 0), stop=(c == DC0 - 1))
                ins.then_inc(s("b_y"), 1)
                if more:
                    b_gate_up(jj + 1)
            turns(pe, NPAIR // 2, b_body)

            pe.wait_ge(s("b_done"), LINKS["B"] * (NPAIR // 2))
            pe.wait_ge(s("wc_loaded"), 16 * 3)
            pe.wait_ge(s("wf_loaded"), 16 * 4)
            def c_comb(i, t):
                pe.wait_ge(s("c_onehot"), 2 * i + t + 1)
                for j in range(NPAIR):
                    for k0, k1 in (((0, 2), (2, 3)) if j == 0 else ((2, 3), (0, 2))):
                        ins = nc.tensor.matmul(COMB[t][:, 0:(k1 - k0) * C], comb_s[:, t, j, :],
                                               y0_all[:, j, k0:k1, :].rearrange("p s c -> p (s c)"),
                                               start=(j == 0 and k0 == 0), stop=(j == NPAIR - 1 and k0 == 0))
                ins.then_inc(s("c_comb"), 1)

            def c_norm(src, k):
                pe.wait_ge(*src)
                transpose_pair(pe, xn).then_inc(s("c_xT"), 1)
                pe.wait_ge(s("c_xTc"), k)

            c_comb(0, 0)
            c_comb(0, 1)
            c_norm((s("c_xn"), 1), 1)
            conv_qkv_pe(pe, WINDOW, wqkv, 0)
            transpose_qk(pe, WINDOW, 0)
            attention_pe(pe, WINDOW, 0)
            project(pe, WINDOW, wproj, 0)

            def c_body(i, more):
                if more:
                    c_comb(i + 1, 0)
                c_norm((s("c_xn"), 2 * i + 2), 3 * i + 2)
                for t, bank in ((0, S0), (1, S1)):
                    for k in range(KC):
                        ins = nc.tensor.matmul(bank[:, 0:18 * HD], xnT[:, k, t * P:(t + 1) * P], wqkvf[:, k, :],
                                               start=(k == 0), stop=(k == KC - 1))
                    ins.then_inc(psem("qkv"), 1)
                if more:
                    c_comb(i + 1, 1)
                transpose_qk(pe, CAUSAL, i)

                def next_qkv():
                    c_norm((s("c_xn"), 2 * i + 3), 3 * i + 3)
                    await_(pe, CAUSAL, "qkTa", i, 3)
                    conv_qkv_pe(pe, WINDOW, wqkv, i + 1)

                def banks_read():
                    await_(pe, WINDOW, "v", i + 1, 1)
                attention_pe(pe, CAUSAL, i, None, {1: next_qkv, 2: banks_read} if more else {})
                project(pe, CAUSAL, wof, i)
                if more:
                    transpose_qk(pe, WINDOW, i + 1)
                pe.wait_ge(s("c_mr"), i + 1)
                transpose_pair(pe, row0).then_inc(s("c_xT"), 1)

                def logits():
                    pe.wait_ge(s("c_xTc"), 3 * i + (4 if more else 3))
                    for t in range(2):
                        for k in range(KC):
                            ins = nc.tensor.matmul(M1[:, t * E1:(t + 1) * E1], xnT[:, k, t * P:(t + 1) * P],
                                                   wr1[:, k, :], start=(k == 0), stop=(k == KC - 1))
                    ins.then_inc(s("c_logits"), 1)
                if more:
                    attention_pe(pe, WINDOW, i + 1, i + 1, {1: logits})
                    project(pe, WINDOW, wproj, i + 1)
                else:
                    logits()
            turns(pe, B, c_body)
            pe.wait_ge(s("c_done"), B)
            tri, ones = cstb("tri"), cstb("ones")
            for n in range(NT):
                nc.tensor.matmul(T0[:, n * E1:(n + 1) * E1], tri, mask12_all[:, n, 0, :], start=True, stop=False)
                nc.tensor.matmul(T0[:, n * E1:(n + 1) * E1], ones, before_all[:, n, :], start=False, stop=True)
            nc.tensor.matmul(T1[:, 0:E1], ones, before_all[:, NT, :], start=True, stop=True).then_inc(s("e_pos"), 1)
            pe.wait_ge(s("e_tiles"), 1)
            pe.wait_ge(s("ffn1_loaded"), 16 * 3)
            def f_rows(n):
                for r in range(2):
                    pe.wait_ge(s(f"f_loaded{r}"), 16 * n + 16)
                    for k in range(KC):
                        ins = nc.tensor.transpose(M0[0:KP, r * 256 + k * P:r * 256 + (k + 1) * P],
                                                  xs[:, r, 0:C].rearrange("p (f k) -> p k f", k=KC)[:, k, :], ident)
                ins.then_inc(s("f_xT"), 1)

            def experts(n):
                return [pe.value_load(tile_ei[0:1, bass.ds(2 * n + r, 1)], min_val=0, max_val=E1 - 1)
                        for r in range(2)]

            def f_gate_up(n, expert):
                pe.wait_ge(s("f_xTc"), n + 1)
                for r in range(2):
                    for part, bank in enumerate(((S0, S1), (O0, O1))[r]):
                        for k in range(KC):
                            ins = nc.tensor.matmul(bank[:, 0:FF], xsT[:, r, k, :],
                                                   gu1_all[:, bass.ds(expert[r], 1), k, part * FF:(part + 1) * FF]
                                                   .rearrange("p a f -> p (a f)"),
                                                   start=(k == 0), stop=(k == KC - 1))
                        ins.then_inc(s(f"f_gu{r}"), 1)
            f_rows(0)
            f_gate_up(0, experts(0))

            def f_body(n, more):
                expert = experts(n)
                if more:
                    following = experts(n + 1)
                for r in range(2):
                    pe.wait_ge(s(f"f_h{r}"), n + 1)
                    for c in range(DC1):
                        ins = nc.tensor.transpose(PT[r][:, c * P:(c + 1) * P],
                                                  h_sb[:, r, 0:FF].rearrange("p (f c) -> p c f", c=DC1)[:, c, :], ident)
                    ins.then_inc(s(f"f_hT{r}"), 1)
                    if r == 0 and more:
                        f_rows(n + 1)
                pe.wait_ge(s("f_yc"), n + 1)
                for r in range(2):
                    pe.wait_ge(s(f"f_hTc{r}"), n + 1)
                    for c in range(DC1):
                        ins = nc.tensor.matmul(M1[:, r * C:(r + 1) * C], hTs[:, r, c * P:(c + 1) * P],
                                               dn1_all[:, bass.ds(expert[r], 1), c, :].rearrange("p a f -> p (a f)"),
                                               start=(c == 0), stop=(c == DC1 - 1))
                ins.then_inc(s("f_y"), 1)
                if more:
                    f_gate_up(n + 1, following)
            turns(pe, NSORT // 2, f_body)


SHAPES = {"x": (TOK, C), "cf": (P, NCF), "cb": (P, NCB), "L0_conv_w_qkv": (C, 3 * C), "L0_conv_w_proj": (C, C),
          "brow0": (P, 4 * C), "L0_ffn_Wg": (C, E0), "ebias": (P, E0), "L0_ffn_Wsg": (C, IS0), "L0_ffn_Wsu": (C, IS0),
          "L0_ffn_Wsd": (IS0, C), "L0_ffn_W_gate_up": (E0, C, 2 * I0), "L0_ffn_W_down": (E0, I0, C),
          "L1_conv_w": (C, 3 * C), "L1_conv_Wo": (C, C), "brow1": (P, 4 * C), "L1_ffn_w_qkv": (C, 18 * HD),
          "L1_ffn_w_out": (C, C), "norm_w": (P, 2 * C), "L1_ffn_w_router": (C, E1),
          "L1_ffn_w_gate_up": (E1, C, 2 * FF), "L1_ffn_w_down": (E1, FF, C)}


def kernel(**inputs):
    import concourse.bacc as _bacc
    from concourse import mybir as _mybir
    from concourse.bass_utils import run_bass_kernel_spmd as _run

    a = {k: np.asarray(v) for k, v in inputs.items()}
    cf, cb = constants()

    def rows(*vs):
        return np.ascontiguousarray(np.broadcast_to(np.concatenate(vs)[None], (P, sum(len(v) for v in vs))))

    even_odd = np.concatenate([np.arange(0, HD, 2), np.arange(1, HD, 2)])
    order = [h * HD + even_odd for h in range(NH + NKV)] + [np.arange((NH + NKV) * HD, (NH + 2 * NKV) * HD)]
    data = {
        "x": a["x"].reshape(TOK, C), "cf": cf, "cb": cb,
        "L0_conv_w_qkv": a["L0_conv_w_qkv"].T, "L0_conv_w_proj": a["L0_conv_w_proj"].T,
        "brow0": rows(a["L0_conv_b_qkv"], a["L0_conv_b_proj"]), "L0_ffn_Wg": a["L0_ffn_Wg"].T,
        "ebias": rows(a["L0_ffn_e_bias"]), "L0_ffn_Wsg": a["L0_ffn_Wsg"], "L0_ffn_Wsu": a["L0_ffn_Wsu"],
        "L0_ffn_Wsd": a["L0_ffn_Wsd"], "L0_ffn_W_gate_up": a["L0_ffn_W_gate_up"], "L0_ffn_W_down": a["L0_ffn_W_down"],
        "L1_conv_w": np.concatenate([a["L1_conv_Wq"], a["L1_conv_Wk"], a["L1_conv_Wv"]], 1),
        "L1_conv_Wo": a["L1_conv_Wo"],
        "brow1": rows(np.concatenate([a["L1_conv_bq"], a["L1_conv_bk"], a["L1_conv_bv"]]), a["L1_conv_bo"]),
        "L1_ffn_w_qkv": a["L1_ffn_w_qkv"][:, np.concatenate(order)], "L1_ffn_w_out": a["L1_ffn_w_out"],
        "norm_w": rows(a["L1_ffn_norm1_w"], a["L1_ffn_norm2_w"]), "L1_ffn_w_router": a["L1_ffn_w_router"],
        "L1_ffn_w_gate_up": a["L1_ffn_w_gate_up"], "L1_ffn_w_down": a["L1_ffn_w_down"],
    }
    nc = _bacc.Bacc("TRN2", target_bir_lowering=False, num_devices=1)
    arrays, d = {}, {}
    for name, shape in SHAPES.items():
        v = np.ascontiguousarray(data[name])
        assert v.shape == shape, (name, v.shape)
        arrays[f"in_{name}"] = v
        d[name] = nc.dram_tensor(f"in_{name}", v.shape, _mybir.dt.from_np(v.dtype), kind="ExternalInput").ap()
    out = nc.dram_tensor("out_x", (TOK, C), F32, kind="ExternalOutput").ap()
    build(nc, d, out)
    r = _run(nc, [arrays], core_ids=[0])
    return r.results[0]["out_x"].reshape(B, IMG, IMG, C)
```
